# Optimizing a Trainium2 kernel written in Bass

```python
import numpy as np
import jax
import jax.numpy as jnp

def _softmax(x, axis=-1):
    return jax.nn.softmax(x, axis=axis)

def _gelu(x):
    return jax.nn.gelu(x, approximate=True)

def _silu(x):
    return jax.nn.silu(x)

def _sigmoid(x):
    return jax.nn.sigmoid(x)

def _layernorm(x, axis=-1, eps=1e-05):
    m = jnp.mean(x, axis=axis, keepdims=True)
    v = jnp.var(x, axis=axis, keepdims=True)
    return (x - m) / jnp.sqrt(v + eps)

def _scatter_add(tgt, idx, src, axis=0):
    return tgt.at[idx].add(src)

def _segment_sum(src, seg, n):
    return jax.ops.segment_sum(src, seg, n)
kernel_name = 'mk_adaln_d1_jaxref_r8_b0d173'

def setup_inputs(seed: int=0):
    np.random.seed(seed)
    _w = jnp.asarray

    def _L0_attn_setup():
        import jax, jax.numpy as jnp
        import numpy as np
        MAX_W, MIN_W = (120, 24)
        key = jax.random.key(seed)
        ks = jax.random.split(key, 11)
        B, S, D, H = (2, 256, 128, 16)
        hd = D // H
        s = 1.0 / float(np.sqrt(D))
        return {'x': jax.random.normal(ks[0], (B, S, D), jnp.float32), 'alpha': jnp.float32(0.1), 'Wq': jax.random.normal(ks[1], (D, D), jnp.float32) * s, 'bq': jnp.zeros((D,), jnp.float32), 'Wk': jax.random.normal(ks[2], (D, D), jnp.float32) * s, 'bk': jnp.zeros((D,), jnp.float32), 'Wv': jax.random.normal(ks[3], (D, D), jnp.float32) * s, 'bv': jnp.zeros((D,), jnp.float32), 'W_o': jax.random.normal(ks[4], (H, hd, hd), jnp.float32), 'Wfc': jax.random.normal(ks[5], (D, D), jnp.float32) * s, 'bfc': jnp.zeros((D,), jnp.float32)}
    _L0_attn_in = _L0_attn_setup()

    def _L0_ffn_setup():
        import jax, jax.numpy as jnp
        import numpy as np
        EMBED = 128
        D_FF = 4 * EMBED
        N_EXPERTS = 8
        TOP_K = 2
        B, S = (2, 128)
        key = jax.random.key(seed)
        ks = jax.random.split(key, 10)
        sc_d = 1.0 / np.sqrt(EMBED)
        sc_h = 1.0 / np.sqrt(D_FF)
        return {'inputs': jax.random.normal(ks[0], (B, S, EMBED), jnp.float32), 'rw1': jax.random.normal(ks[1], (EMBED, D_FF), jnp.float32) * sc_d, 'rb1': jnp.zeros((D_FF,), jnp.float32), 'rw2': jax.random.normal(ks[2], (D_FF, N_EXPERTS), jnp.float32) * sc_h, 'rb2': jnp.zeros((N_EXPERTS,), jnp.float32), 'W1': jax.random.normal(ks[3], (N_EXPERTS, EMBED, D_FF), jnp.float32) * sc_d, 'b1': jnp.zeros((N_EXPERTS, D_FF), jnp.float32), 'W2': jax.random.normal(ks[4], (N_EXPERTS, D_FF, EMBED), jnp.float32) * sc_h, 'b2': jnp.zeros((N_EXPERTS, EMBED), jnp.float32)}
    _L0_ffn_in = _L0_ffn_setup()
    _L0_c = _w((lambda *s: np.random.randn(*s).astype(np.float32) * 0.05)(4, 128))
    _L0_wmod = _w((lambda *s: np.random.randn(*s).astype(np.float32) * 0.05)(128, 6 * 128) * 128 ** (-0.5))
    _d = {'L0_attn_x': _L0_attn_in['x'], 'L0_attn_alpha': _L0_attn_in['alpha'], 'L0_attn_Wq': _L0_attn_in['Wq'], 'L0_attn_bq': _L0_attn_in['bq'], 'L0_attn_Wk': _L0_attn_in['Wk'], 'L0_attn_bk': _L0_attn_in['bk'], 'L0_attn_Wv': _L0_attn_in['Wv'], 'L0_attn_bv': _L0_attn_in['bv'], 'L0_attn_W_o': _L0_attn_in['W_o'], 'L0_attn_Wfc': _L0_attn_in['Wfc'], 'L0_attn_bfc': _L0_attn_in['bfc'], 'L0_ffn_rw1': _L0_ffn_in['rw1'], 'L0_ffn_rb1': _L0_ffn_in['rb1'], 'L0_ffn_rw2': _L0_ffn_in['rw2'], 'L0_ffn_rb2': _L0_ffn_in['rb2'], 'L0_ffn_W1': _L0_ffn_in['W1'], 'L0_ffn_b1': _L0_ffn_in['b1'], 'L0_ffn_W2': _L0_ffn_in['W2'], 'L0_ffn_b2': _L0_ffn_in['b2'], 'L0_c': _L0_c, 'L0_wmod': _L0_wmod}
    _x0 = _d['L0_attn_x']
    _d['L0_attn_x'] = jax.random.normal(jax.random.fold_in(jax.random.key(seed), 1), (4, 1024, 128), dtype=_x0.dtype)
    del _x0
    return _d

def reference(L0_attn_x, L0_attn_alpha, L0_attn_Wq, L0_attn_bq, L0_attn_Wk, L0_attn_bk, L0_attn_Wv, L0_attn_bv, L0_attn_W_o, L0_attn_Wfc, L0_attn_bfc, L0_ffn_rw1, L0_ffn_rb1, L0_ffn_rw2, L0_ffn_rb2, L0_ffn_W1, L0_ffn_b1, L0_ffn_W2, L0_ffn_b2, L0_c, L0_wmod):

    def _L0_attn_ref(x, alpha, Wq, bq, Wk, bk, Wv, bv, W_o, Wfc, bfc):
        import jax, jax.numpy as jnp
        import numpy as np
        MAX_W, MIN_W = (120, 24)
        B, S, D = x.shape
        H, hd, _ = W_o.shape
        fluct = jnp.abs(x[:, -1] - x[:, -2])
        a = jax.nn.sigmoid(alpha)
        ewma_prev = fluct[0, 0]
        signal = a * fluct.mean() + (1.0 - a) * ewma_prev
        scale = jax.nn.sigmoid(signal)
        w = jnp.floor(MIN_W + (MAX_W - MIN_W) * scale).astype(jnp.int32)
        half = w // 2
        q = (x @ Wq + bq).reshape(B, S, H, hd).transpose(0, 2, 1, 3)
        k = (x @ Wk + bk).reshape(B, S, H, hd).transpose(0, 2, 1, 3)
        v = (x @ Wv + bv).reshape(B, S, H, hd).transpose(0, 2, 1, 3)
        inv_sqrt = 1.0 / float(np.sqrt(hd))
        scores = jnp.einsum('bhqd,bhkd->bhqk', q, k) * inv_sqrt
        idx = jnp.arange(S)
        band = jnp.abs(idx[:, None] - idx[None, :]) <= half
        scores = jnp.where(band[None, None], scores, -1e+30)
        attn = jax.nn.softmax(scores, axis=-1)
        out = jnp.einsum('bhqk,bhkd->bhqd', attn, v)
        out = jnp.einsum('bhqd,hdk->bhqk', out, W_o)
        out = out.transpose(0, 2, 1, 3).reshape(B, S, D)
        return out @ Wfc + bfc

    def _L0_ffn_ref(inputs, rw1, rb1, rw2, rb2, W1, b1, W2, b2):
        import jax, jax.numpy as jnp
        import numpy as np
        EMBED = 128
        D_FF = 4 * EMBED
        N_EXPERTS = 8
        TOP_K = 2
        B, S = (2, 128)
        Bb, Ss, D = inputs.shape
        T = Bb * Ss
        xf = inputs.reshape(T, D)
        score = jax.nn.relu(xf @ rw1 + rb1) @ rw2 + rb2
        _, topi = jax.lax.top_k(score, TOP_K)
        mask = jnp.zeros(score.shape, bool).at[jnp.arange(T)[:, None], topi].set(True)
        gate = jax.nn.softmax(jnp.where(mask, score, -jnp.inf), axis=-1)
        out = jnp.zeros_like(xf)
        for e in range(N_EXPERTS):
            h = jax.nn.relu(xf @ W1[e] + b1[e])
            y = h @ W2[e] + b2[e]
            out = out + gate[:, e:e + 1] * y
        return out.reshape(Bb, Ss, D)
    x = L0_attn_x
    mod = (_silu(L0_c) @ L0_wmod).reshape(L0_c.shape[0], 6, 1, -1)
    sa, ca, ga, sb, cb, gb = (mod[:, 0], mod[:, 1], mod[:, 2], mod[:, 3], mod[:, 4], mod[:, 5])
    ga = (2 * (ga >= 0) - 1) * jnp.maximum(jnp.abs(ga), 0.25)
    gb = (2 * (gb >= 0) - 1) * jnp.maximum(jnp.abs(gb), 0.25)
    h = _layernorm(x, axis=-1) * (1 + ca) + sa
    x = x + ga * _L0_attn_ref(h, L0_attn_alpha, L0_attn_Wq, L0_attn_bq, L0_attn_Wk, L0_attn_bk, L0_attn_Wv, L0_attn_bv, L0_attn_W_o, L0_attn_Wfc, L0_attn_bfc)
    h = _layernorm(x, axis=-1) * (1 + cb) + sb
    x = x + gb * _L0_ffn_ref(h, L0_ffn_rw1, L0_ffn_rb1, L0_ffn_rw2, L0_ffn_rb2, L0_ffn_W1, L0_ffn_b1, L0_ffn_W2, L0_ffn_b2)
    return x

_drawn_inputs = setup_inputs


def setup_inputs(seed=0):
    import zlib

    import numpy as np

    out = dict(_drawn_inputs(seed))
    spreads = {'L0_attn_bq': (0.0, 0.481),
     'L0_attn_bk': (0.0, 0.8),
     'L0_attn_bv': (0.0, 0.1),
     'L0_attn_bfc': (0.0, 0.269),
     'L0_ffn_rb1': (0.0, 0.1),
     'L0_ffn_rb2': (0.0, 0.1),
     'L0_ffn_b1': (0.0, 0.63),
     'L0_ffn_b2': (0.0, 0.476)}
    factors = {}
    for name, (base, spread) in spreads.items():
        noise = np.random.default_rng([zlib.crc32(name.encode()), seed]).standard_normal(out[name].shape)
        drawn = base * np.exp(spread * noise) if base else spread * noise
        out[name] = jnp.asarray(drawn.astype(out[name].dtype))
    for name, factor in factors.items():
        out[name] = (out[name] * factor).astype(out[name].dtype)
    return out
```

```python
import numpy as np
import concourse.bass as bass
from concourse import mybir
from contextlib import ExitStack

F32 = mybir.dt.float32
F32R = mybir.dt.float32r
BF16 = mybir.dt.bfloat16
I32 = mybir.dt.int32
U32 = mybir.dt.uint32
ALU = mybir.AluOpType
ACT = mybir.ActivationFunctionType
AX = mybir.AxisListType

P = 128
B, S, D = 4, 1024, 128
H, HD = 16, 8
T = B * S
NT = T // P
TPB = S // P
MIN_W, MAX_W = 24, 120
HALO = 64
HG = 4
QB = 32
WIN = QB + 2 * HALO
KW = P + 2 * HALO
KBLK = KW // QB
GRP = 512
NG = T // GRP
BIG = 1e30
EPS = 1e-5
NE, TOPK, FF = 8, 2, 512
FC = FF // P
FT = 256
NF = T * TOPK // FT + NE - 1
SC = NF * FT // P
ISQ = 1.0 / float(np.sqrt(HD))


class Count:

    def __init__(self, sem, n):
        self.sem, self.n = sem, n

    def open(self, eng):
        eng.sem_inc(self.sem, 2 * self.n)

    def wait(self, eng, turn, u, k=None, back=0):
        k = self.n if k is None else k
        eng.wait_ge(self.sem, turn * (2 * self.n) + (2 * self.n + self.n * (u - back) + k))


class Flights:

    def __init__(self, sem, n):
        self.sem, self.n = sem, n

    def open(self, eng):
        eng.sem_inc(self.sem, 16)

    def wait(self, eng, turn, k=0):
        eng.wait_ge(self.sem, turn * (16 * self.n) + (16 + 16 * k))


def strided(ap, offset, dims):
    return bass.AP(tensor=ap.tensor, offset=ap.offset + offset, ap=[list(ap.ap[0])] + dims)


def apart(eng):
    eng.nop(nofuse=True)


def bcast_row(rows, b, n):
    return rows[:, bass.ds(b, 1), :].broadcast_to([P, n, D])


def build(nc, x, alpha, Wq, bq, Wk, bk, Wv, bv, W_o, Wfc, bfc, rw1, rb1, rw2, rb2, W1, b1, W2, b2, c, wmod, out, stop=9):
    top = ExitStack()

    def sem(name):
        return top.enter_context(nc.semaphore(name))

    def sb(name, shape, dt=F32, ctx=top):
        return ctx.enter_context(nc.sbuf_tensor(name, shape, dt))

    def pb(ctx, name, shape, dt=F32):
        return ctx.enter_context(nc.psum_tensor(name, shape, dt))

    xf = x.rearrange("b s d -> (b s) d")
    of = out.rearrange("b s d -> (b s) d")

    with top:
        x_all = sb("x_all", [P, NT + 1, D])
        ident = sb("ident", [P, P])
        ga_bc = sb("ga_bc", [P, B + 1, D])
        gacv_bc = sb("gacv_bc", [P, B + 1, D])
        sb_bc = sb("sb_bc", [P, B, D])
        cb_bc = sb("cb_bc", [P, B, D])
        gb_bc = sb("gb_bc", [P, B, D])
        q_scr = nc.dram_tensor("q_scr", (4, QB, HG, T), F32, kind="Internal").ap()
        k_scr = nc.dram_tensor("k_scr", (4, QB, HG, T), F32, kind="Internal").ap()
        v_scr = nc.dram_tensor("v_scr", (T + 2 * HALO, D), F32, kind="Internal").ap()

        attn = ExitStack()
        kst = sb("kst", [P, HG, T + 2 * HALO], F32R, attn)
        wqs = sb("wqs", [P, D], F32, attn)
        wk_sb = sb("wk_sb", [P, D], F32, attn)
        wv_sb = sb("wv_sb", [P, D], F32, attn)
        wc = sb("wc", [P, D], F32, attn)
        bqs = sb("bqs", [P, 1], F32, attn)
        bk_sb = sb("bk_sb", [P, 1], F32, attn)
        sa_t = sb("sa_t", [P, B], F32, attn)
        ca_t = sb("ca_t", [P, B], F32, attn)
        rstd = sb("rstd", [P, NT], F32, attn)
        nmr = sb("nmr", [P, NT], F32, attn)
        identb = sb("identb", [P, P], BF16, attn)
        eqh = sb("eqh", [P, 4], F32, attn)
        eqg = sb("eqg", [P, 4], F32, attn)
        eqd = sb("eqd", [P, 4], F32, attn)
        eqq = sb("eqq", [P, 4], F32, attn)
        st_den = sb("st_den", [P, D], F32, attn)
        masks = sb("masks", [P, TPB, 4 * WIN], BF16, attn)

        with ExitStack() as one:
            s1 = lambda n, sh, dt=F32: sb(n, sh, dt, one)
            wq_sb = s1("wq_sb", [P, D])
            wfc_sb = s1("wfc_sb", [P, D])
            wo_sb = s1("wo_sb", [P, HD])
            bq_sb = s1("bq_sb", [P, 1])
            bv_sb = s1("bv_sb", [P, 1])
            bfc_bc = s1("bfc_bc", [P, D])
            cT = s1("cT", [P, B])
            silu = s1("silu", [P, B])
            tmp4 = s1("tmp4", [P, B])
            wmod_sb = s1("wmod_sb", [P, 6 * D])
            stats = s1("stats", [P, NT, 6])
            mv = s1("mv", [P, NT, 2])
            varr = s1("varr", [P, NT + 2])
            xl = s1("xl", [B, 2, D])
            statl = s1("statl", [B, 2, 6])
            mvl = s1("mvl", [B, 2, 2])
            nml = s1("nml", [B, 2])
            sac = s1("sac", [B, 2 * D])
            fl = s1("fl", [B, 2, D])
            flsum = s1("flsum", [B, 1])
            rcp = s1("rcp", [P, NT + 2])
            sc = s1("sc", [1, 16])
            sci = s1("sci", [1, 4], I32)
            ones_r = s1("ones_r", [B, P])
            half = s1("half", [P, 1])
            pint = s1("pint", [P, 1], I32)
            pbits = s1("pbits", [P, 6], I32)
            pf = s1("pf", [P, 6])
            ci = s1("ci", [P, WIN], I32)
            cf = s1("cf", [P, WIN])
            dist = s1("dist", [P, WIN])
            adist = s1("adist", [P, WIN])
            mint = s1("mint", [P, WIN], BF16)
            eq16 = s1("eq16", [P, H])
            bdo = s1("bdo", [P, D])
            bdoT = s1("bdoT", [P, D])
            sgn = s1("sgn", [P, B, D])
            zero_kv = s1("zero_kv", [P, HG * HALO])
            ps_row = [pb(one, f"ps_row{b}", [P, 512]) for b in range(B)]
            ps_col = pb(one, "ps_col", [P, 512])
            ps_a = pb(one, "ps_a", [P, 512])
            ps_b = pb(one, "ps_b", [P, 512])
            ps_h = pb(one, "ps_h", [P, 512])

            ld_al = sem("ld_al")
            ld_x, ld_w, ld_c, ld_f = sem("ld_x"), sem("ld_w"), sem("ld_c"), sem("ld_f")
            s_pad = sem("s_pad")
            p_cst = sem("p_cst")
            v1, a1, t1 = sem("v1"), sem("a1"), sem("t1")
            kv = [0]
            nv = {}
            block = one.enter_context(nc.Block())

            @block.vector
            def _(e):
                def step(name, ins):
                    kv[0] += 1
                    nv[name] = kv[0]
                    ins.then_inc(v1, 1)

                def own():
                    e.wait_ge(v1, kv[0])

                step("zero", e.memset(zero_kv[:, :], 0.0))
                e.wait_ge(a1, 1)
                e.wait_ge(ld_c, 32)
                step("silu1", e.tensor_scalar(tmp4[:, :], silu[:, :], 1.0, None, ALU.add))
                own()
                step("silu2", e.reciprocal(tmp4[:, :], tmp4[:, :]))
                own()
                e.wait_ge(p_cst, 4)
                step("silu3", e.tensor_tensor(silu[:, :], cT[:, :], tmp4[:, :], ALU.mult))
                for k, (sh, msk) in enumerate(((5, 3), (2, 7), (0, 3), (3, 15), (0, 31), (3, 3))):
                    step(f"pb{k}", e.tensor_scalar(pbits[:, k:k + 1], pint[:, :], sh, msk, ALU.logical_shift_right, ALU.bitwise_and))
                own()
                step("pf", e.tensor_copy(pf[:, :], pbits[:, :]))
                step("cf", e.tensor_copy(cf[:, :], ci[:, :]))
                own()
                step("eqh", e.tensor_scalar(eqh[:, :], cf[:, 0:4], pf[:, 0:1], None, ALU.is_equal))
                step("eqg", e.tensor_scalar(eqg[:, :], cf[:, 0:4], pf[:, 1:2], None, ALU.is_equal))
                step("eqq", e.tensor_scalar(eqq[:, :], cf[:, 0:4], pf[:, 2:3], None, ALU.is_equal))
                step("eqd", e.tensor_scalar(eqd[:, :], cf[:, 0:4], pf[:, 5:6], None, ALU.is_equal))
                step("eq16", e.tensor_scalar(eq16[:, :], cf[:, 0:H], pf[:, 3:4], None, ALU.is_equal))
                own()
                step("st", e.tensor_tensor(st_den[:, :].rearrange("p (g h d) -> p g h d", g=4, h=4),
                                           strided(eqh[:, :], 0, [[0, 4], [1, 4], [0, 8]]),
                                           strided(eqg[:, :], 0, [[1, 4], [0, 4], [0, 8]]), ALU.mult))
                e.wait_ge(ld_w, 16 * 9)
                step("bdo", e.tensor_tensor(bdo[:, :].rearrange("p (h k) -> p h k", h=H),
                                            strided(wo_sb[:, :], 0, [[0, H], [1, HD]]),
                                            strided(eq16[:, :], 0, [[1, H], [0, HD]]), ALU.mult))
                step("identb", e.tensor_copy(identb[:, :], ident[:, :]))
                step("ones", e.memset(ones_r[:, :], 1.0))
                e.wait_ge(t1, 1)
                step("bdoT", e.tensor_copy(bdoT[:, :], ps_a[:, 0:D]))
                e.wait_ge(t1, 2)
                step("modT1", e.tensor_copy(sa_t[:, :], ps_col[:, 0:B]))
                step("modT2", e.tensor_scalar(ca_t[:, :], ps_col[:, B:2 * B], 1.0, None, ALU.add))
                step("wqs", e.tensor_scalar(wqs[:, :], wq_sb[:, :], -ISQ, None, ALU.mult))
                step("bqs", e.tensor_scalar(bqs[:, :], bq_sb[:, :], -ISQ, None, ALU.mult))
                e.wait_ge(ld_x, 16 * B)
                e.wait_ge(ld_f, 32)
                for n in range(NT):
                    step("_s", e.bn_stats(stats[:, n, :], x_all[:, n + 1, :]))
                for k in range(2):
                    step("_s", e.bn_stats(statl[:, k, :], xl[:, k, :]))
                own()
                for k in range(2):
                    step("_a", e.bn_aggr(mvl[:, k, :], statl[:, k, :]))
                for n in range(NT):
                    step("_a", e.bn_aggr(mv[:, n, :], stats[:, n, :]))
                own()
                step("_v", e.memset(varr[:, NT:], 1.0))
                own()
                step("_v", e.tensor_scalar(varr[0:B, NT:], mvl[:, :, 1], EPS, None, ALU.add))
                step("var", e.tensor_scalar(varr[:, 0:NT], mv[:, :, 1], EPS, None, ALU.add))
                e.wait_ge(a1, 3)
                step("_r", e.reciprocal(rcp[:, :], varr[:, :]))
                own()
                step("_r", e.tensor_copy(rstd[:, :], rcp[:, 0:NT]))
                step("_r", e.scalar_tensor_tensor(out=nmr[:, :], in0=mv[:, :, 0], scalar=-1.0, in1=rcp[:, 0:NT], op0=ALU.mult, op1=ALU.mult))
                step("_r", e.scalar_tensor_tensor(out=nml[:, :], in0=mvl[:, :, 0], scalar=-1.0, in1=rcp[0:B, NT:], op0=ALU.mult, op1=ALU.mult))
                step("_r", e.tensor_copy(sac[:, 0:D], ps_h[0:B, 0:D]))
                step("_r", e.tensor_scalar(sac[:, D:], ps_h[0:B, D:2 * D], 1.0, None, ALU.add))
                own()
                for k in range(2):
                    step("_f", e.tensor_scalar(xl[:, k, :], xl[:, k, :], rcp[0:B, NT + k:NT + k + 1], nml[:, k:k + 1], ALU.mult, ALU.add))
                    own()
                    step("_f", e.tensor_tensor(xl[:, k, :], xl[:, k, :], sac[:, D:], ALU.mult))
                    own()
                    step("_f", e.tensor_tensor(xl[:, k, :], xl[:, k, :], sac[:, 0:D], ALU.add))
                    own()
                step("fd", e.tensor_tensor(fl[:, 0, :], xl[:, 0, :], xl[:, 1, :], ALU.subtract))
                own()
                step("fa", e.scalar_tensor_tensor(out=fl[:, 1, :], in0=fl[:, 0, :], scalar=-1.0, in1=fl[:, 0, :], op0=ALU.mult, op1=ALU.max))
                own()
                step("fs", e.tensor_reduce(flsum[:, :], fl[:, 1, :], AX.X, ALU.add))
                e.wait_ge(t1, 3)
                step("fs2", e.tensor_copy(sc[:, 1:2], ps_b[0:1, 256:257]))
                e.wait_ge(a1, 2)
                step("al1", e.tensor_scalar(sc[:, 3:4], sc[:, 2:3], 1.0, None, ALU.add))
                own()
                step("al2", e.reciprocal(sc[:, 4:5], sc[:, 3:4]))
                own()
                step("al3", e.tensor_scalar(sc[:, 5:6], sc[:, 4:5], -1.0, 1.0, ALU.mult, ALU.add))
                own()
                step("al4", e.tensor_tensor(sc[:, 6:7], sc[:, 5:6], fl[0:1, 1, 0:1], ALU.mult))
                step("al5", e.tensor_scalar(sc[:, 7:8], sc[:, 1:2], 1.0 / (B * D), None, ALU.mult))
                own()
                step("fm", e.tensor_tensor(sc[:, 7:8], sc[:, 7:8], sc[:, 4:5], ALU.mult))
                own()
                step("sg", e.tensor_tensor(sc[:, 8:9], sc[:, 7:8], sc[:, 6:7], ALU.add))
                e.wait_ge(a1, 4)
                step("sg1", e.tensor_scalar(sc[:, 10:11], sc[:, 9:10], 1.0, None, ALU.add))
                own()
                step("sg2", e.reciprocal(sc[:, 11:12], sc[:, 10:11]))
                own()

                def floor(name, val, dst, k):
                    step(name + "1", e.tensor_copy(sci[:, k:k + 1], val))
                    own()
                    step(name + "2", e.tensor_copy(dst, sci[:, k:k + 1]))
                    own()
                    step(name + "3", e.tensor_tensor(sc[:, 15:16], dst, val, ALU.is_gt))
                    own()
                    step(name + "4", e.tensor_tensor(dst, dst, sc[:, 15:16], ALU.subtract))
                    own()

                step("w0", e.tensor_scalar(sc[:, 12:13], sc[:, 11:12], float(MAX_W - MIN_W), float(MIN_W), ALU.mult, ALU.add))
                own()
                floor("w", sc[:, 12:13], sc[:, 13:14], 0)
                step("h1", e.tensor_scalar(sc[:, 14:15], sc[:, 13:14], 0.5, None, ALU.mult))
                own()
                step("h2", e.tensor_copy(sci[:, 1:2], sc[:, 14:15]))
                own()
                step("h3", e.tensor_copy(sc[:, 12:13], sci[:, 1:2]))
                own()
                step("h4", e.tensor_tensor(sc[:, 15:16], sc[:, 12:13], sc[:, 14:15], ALU.is_gt))
                own()
                step("h5", e.tensor_tensor(sc[:, 12:13], sc[:, 12:13], sc[:, 15:16], ALU.subtract))
                e.wait_ge(t1, 4)
                step("half", e.tensor_copy(half[:, :], ps_h[:, 256:257]))
                e.wait_ge(t1, 5)
                step("wc", e.tensor_copy(wc[:, :], ps_b[:, 0:D]))
                own()
                step("dist", e.tensor_scalar(dist[:, :], cf[:, :], pf[:, 4:5], float(HALO), ALU.subtract, ALU.subtract))
                own()
                step("adist", e.scalar_tensor_tensor(out=adist[:, :], in0=dist[:, :], scalar=-1.0, in1=dist[:, :], op0=ALU.mult, op1=ALU.max))
                own()
                step("mint", e.tensor_scalar(mint[:, :], adist[:, :], half[:, 0:1], BIG, ALU.is_gt, ALU.mult))
                own()
                step("_m", e.tensor_copy(masks[:, :, :].rearrange("p t (q w) -> p (t q) w", q=4),
                                         strided(mint[:, :], 0, [[0, TPB * 4], [1, WIN]])))
                own()
                for q in range(HALO // QB):
                    step("_e", e.memset(masks[:, 0, q * WIN:q * WIN + HALO - q * QB], BIG))
                    qq = 3 - q
                    step("_e", e.memset(masks[:, TPB - 1, (qq + 1) * WIN - HALO + q * QB:(qq + 1) * WIN], BIG))
                e.wait_ge(t1, 6)
                for b in range(B):
                    r = ps_row[b]
                    step("_g", e.tensor_scalar(sgn[:, b, :], r[:, 0:D], 0.0, 0.5, ALU.is_ge, ALU.subtract))
                    step("_b", e.tensor_copy(sb_bc[:, b, :], r[:, D:2 * D]))
                    step("_b", e.tensor_scalar(cb_bc[:, b, :], r[:, 2 * D:3 * D], 1.0, None, ALU.add))
                    own()
                    step("_b", e.tensor_tensor(ga_bc[:, b + 1, :], r[:, 0:D], sgn[:, b, :], ALU.mult))
                    own()
                    step("_b", e.tensor_scalar(ga_bc[:, b + 1, :], ga_bc[:, b + 1, :], 0.125, 4.0, ALU.max, ALU.mult))
                    own()
                    step("_b", e.tensor_tensor(ga_bc[:, b + 1, :], ga_bc[:, b + 1, :], sgn[:, b, :], ALU.mult))
                    own()
                    step("_g", e.tensor_scalar(sgn[:, b, :], r[:, 3 * D:4 * D], 0.0, 0.5, ALU.is_ge, ALU.subtract))
                    own()
                    step("_b", e.tensor_tensor(gb_bc[:, b, :], r[:, 3 * D:4 * D], sgn[:, b, :], ALU.mult))
                    own()
                    step("_b", e.tensor_scalar(gb_bc[:, b, :], gb_bc[:, b, :], 0.125, 4.0, ALU.max, ALU.mult))
                    own()
                    step("_b", e.tensor_tensor(gb_bc[:, b, :], gb_bc[:, b, :], sgn[:, b, :], ALU.mult))
                    own()
                step("_c", e.tensor_copy(ga_bc[:, 0, :], ga_bc[:, 1, :]))
                step("_c", e.tensor_tensor(bfc_bc[:, :], bfc_bc[:, :], ps_a[:, 0:D], ALU.add))
                own()
                step("_c", e.tensor_tensor(gacv_bc[:, :, :], ga_bc[:, :, :], strided(bfc_bc[:, :], 0, [[0, B + 1], [1, D]]), ALU.mult))

            @block.sync
            def _(e):
                with nc.allow_non_contiguous_dma(reason="four values a partition"):
                    e.dma_start(cT[:, :], c.rearrange("b d -> d b")).then_inc(ld_c, 16)
                e.dma_start(wmod_sb[:, :], wmod).then_inc(ld_c, 16)
                e.dma_start(xl[:, 0, :], x[:, S - 1, :]).then_inc(ld_f, 16)
                e.dma_start(xl[:, 1, :], x[:, S - 2, :]).then_inc(ld_f, 16)
                e.dma_start(sc[0:1, 0:1], alpha).then_inc(ld_al, 16)
                for b in range(B):
                    e.dma_start(x_all[:, 1 + b * TPB:1 + (b + 1) * TPB, :],
                                xf[b * S:(b + 1) * S, :].rearrange("(n p) d -> p n d", p=P)).then_inc(ld_x, 16)
                for dst, src in ((wq_sb, Wq), (wk_sb, Wk), (wv_sb, Wv), (wfc_sb, Wfc)):
                    e.dma_start(dst[:, :], src).then_inc(ld_w, 16)
                e.dma_start(wo_sb[:, :], W_o.rearrange("h d k -> (h d) k")).then_inc(ld_w, 16)
                for dst, src in ((bq_sb, bq), (bk_sb, bk), (bv_sb, bv)):
                    e.dma_start(dst[:, :], src.rearrange("(d a) -> d a", a=1)).then_inc(ld_w, 16)
                e.dma_start(bfc_bc[:, :], bfc.rearrange("(a d) -> a d", a=1).broadcast_to([P, D])).then_inc(ld_w, 16)
                e.wait_ge(v1, nv["zero"])
                e.dma_start(kst[:, :, 0:HALO].bitcast(F32), zero_kv[:, :].rearrange("p (g t) -> p g t", g=HG)).then_inc(s_pad, 16)
                e.dma_start(kst[:, :, HALO + T:].bitcast(F32), zero_kv[:, :].rearrange("p (g t) -> p g t", g=HG)).then_inc(s_pad, 16)
                e.dma_start(v_scr[0:HALO, :], zero_kv[0:HALO, 0:D]).then_inc(s_pad, 16)
                e.dma_start(v_scr[HALO + T:, :], zero_kv[0:HALO, 0:D]).then_inc(s_pad, 16)
                e.wait_ge(s_pad, 64)

            @block.gpsimd
            def _(e):
                e.memset(x_all[:, 0, :], 0.0)
                e.memset(ident[:, :], 0.0).then_inc(p_cst, 1)
                e.iota(pint[:, :], [[0, 1]], 0, 1).then_inc(p_cst, 1)
                e.iota(ci[:, :], [[1, WIN]], 0, 0).then_inc(p_cst, 1)
                e.wait_ge(p_cst, 1)
                e.affine_select(out=ident[:, :], in_=ident[:, :], compare_op=ALU.not_equal, fill=1.0,
                                base=0, pattern=[[-1, P]], channel_multiplier=1).then_inc(p_cst, 1)

            @block.scalar
            def _(e):
                e.wait_ge(ld_c, 32)
                e.activation(silu[:, :], cT[:, :], ACT.Exp, scale=-1.0).then_inc(a1, 1)
                e.wait_ge(ld_al, 16)
                e.activation(sc[:, 2:3], sc[:, 0:1], ACT.Exp, scale=-1.0).then_inc(a1, 1)
                e.wait_ge(v1, nv["var"])
                e.activation(varr[:, :], varr[:, :], ACT.Sqrt).then_inc(a1, 1)
                e.wait_ge(v1, nv["sg"])
                e.activation(sc[:, 9:10], sc[:, 8:9], ACT.Exp, scale=-1.0).then_inc(a1, 1)

            @block.tensor
            def _(e):
                e.wait_ge(v1, nv["bdo"])
                e.wait_ge(p_cst, 4)
                e.transpose(ps_a[:, 0:D], bdo[:, :], ident[:, :]).then_inc(t1, 1)
                e.wait_ge(v1, nv["silu3"])
                for j in range(2):
                    e.matmul(ps_col[:, j * B:(j + 1) * B], wmod_sb[:, j * D:(j + 1) * D], silu[:, :], start=True, stop=True)
                e.matmul(ps_h[0:B, 0:2 * D], silu[:, :], wmod_sb[:, 0:2 * D], start=True, stop=True).then_inc(t1, 1)
                e.wait_ge(v1, nv["fs"])
                e.matmul(ps_b[0:1, 256:257], flsum[:, :], ones_r[0:B, 0:1], start=True, stop=True).then_inc(t1, 1)
                e.wait_ge(v1, nv["h5"])
                e.matmul(ps_h[:, 256:257], ones_r[0:1, :], sc[0:1, 12:13], start=True, stop=True).then_inc(t1, 1)
                e.wait_ge(v1, nv["bdoT"])
                e.matmul(ps_b[:, 0:D], bdoT[:, :], wfc_sb[:, :], start=True, stop=True).then_inc(t1, 1)
                for b in range(B):
                    e.matmul(ps_row[b][:, :], strided(silu[:, b:b + 1], 0, [[0, P]]), wmod_sb[:, 2 * D:6 * D], start=True, stop=True)
                e.wait_ge(v1, nv["wc"])
                e.matmul(ps_a[:, 0:D], strided(bv_sb[:, 0:1], 0, [[0, P]]), wc[:, :], start=True, stop=True).then_inc(t1, 1)

        with ExitStack() as two:
            hn = [sb(f"hn{u}", [P, 4, D], F32, two) for u in range(2)]
            hT = [sb(f"hT{u}", [P, GRP], F32, two) for u in range(2)]
            khi = [sb(f"khi{u}", [P, GRP], F32R, two) for u in range(2)]
            klo = [sb(f"klo{u}", [P, GRP], F32R, two) for u in range(2)]
            qhi = [sb(f"qhi{u}", [P, GRP], F32R, two) for u in range(2)]
            qlo = [sb(f"qlo{u}", [P, GRP], F32R, two) for u in range(2)]
            vn = [sb(f"vn{u}", [P, 4, D], F32, two) for u in range(2)]
            pT = [pb(two, f"pT{u}", [P, GRP]) for u in range(2)]
            pK = [pb(two, f"pK{u}", [P, GRP]) for u in range(2)]
            pQ = [pb(two, f"pQ{u}", [P, GRP]) for u in range(2)]
            pV = [pb(two, f"pV{u}", [P, GRP]) for u in range(2)]
            v_hn = Count(sem("v_hn"), 4)
            t_tr = Count(sem("t_tr"), 1)
            a_hT = Count(sem("a_hT"), 1)
            t_kqv = Count(sem("t_kqv"), 3)
            a_kqv = Count(sem("a_kqv"), 3)
            v_lo = Count(sem("v_lo"), 2)
            d_st = [Flights(sem(f"d_st{u}"), 4 + 1) for u in range(2)]
            d_k = [Flights(sem(f"d_k{u}"), 4) for u in range(2)]
            d_kst = sem("d_kst")
            block = two.enter_context(nc.Block())

            @block.vector
            def _(e):
                v_hn.open(e)
                v_lo.open(e)
                with e.Fori(0, NG // 2) as i:
                    for u in range(2):
                        t_tr.wait(e, i, u, back=2)
                        for n in range(4):
                            g = i * 8 + (4 * u + n)
                            e.tensor_scalar(hn[u][:, n, :], x_all[:, bass.ds(g + 1, 1), :].rearrange("p a d -> p (a d)"),
                                            rstd[:, bass.ds(g, 1)], nmr[:, bass.ds(g, 1)], ALU.mult, ALU.add).then_inc(v_hn.sem, 1)
                        d_st[u].wait(e, i)
                        d_k[u].wait(e, i)
                        a_kqv.wait(e, i, u, 1)
                        e.scalar_tensor_tensor(out=klo[u][:, :], in0=pK[u][:, :], scalar=bk_sb[:, 0:1],
                                               in1=khi[u][:, :].bitcast(F32), op0=ALU.add, op1=ALU.subtract).then_inc(v_lo.sem, 1)
                        a_kqv.wait(e, i, u, 2)
                        e.scalar_tensor_tensor(out=qlo[u][:, :], in0=pQ[u][:, :], scalar=bqs[:, 0:1],
                                               in1=qhi[u][:, :].bitcast(F32), op0=ALU.add, op1=ALU.subtract).then_inc(v_lo.sem, 1)

            @block.scalar
            def _(e):
                a_hT.open(e)
                a_kqv.open(e)
                with e.Fori(0, NG // 2) as i:
                    for u in range(2):
                        t_tr.wait(e, i, u)
                        t_kqv.wait(e, i, u, back=2)
                        apart(e)
                        e.activation(hT[u][:, :], pT[u][:, :], ACT.Identity, bias=sa_t[:, bass.ds(i, 1)],
                                     scale=ca_t[:, bass.ds(i, 1)]).then_inc(a_hT.sem, 1)
                        d_st[u].wait(e, i)
                        d_k[u].wait(e, i)
                        v_lo.wait(e, i, u, back=2)
                        t_kqv.wait(e, i, u, 1)
                        e.activation(khi[u][:, :], pK[u][:, :], ACT.Identity, bias=bk_sb[:, 0:1]).then_inc(a_kqv.sem, 1)
                        t_kqv.wait(e, i, u, 2)
                        e.activation(qhi[u][:, :], pQ[u][:, :], ACT.Identity, bias=bqs[:, 0:1]).then_inc(a_kqv.sem, 1)
                        t_kqv.wait(e, i, u, 3)
                        e.activation(vn[u][:, :, :], pV[u][:, :].rearrange("p (n d) -> p n d", n=4), ACT.Copy).then_inc(a_kqv.sem, 1)

            @block.tensor
            def _(e):
                t_tr.open(e)
                t_kqv.open(e)
                with e.Fori(0, NG // 2) as i:
                    for u in range(2):
                        a_hT.wait(e, i, u, back=2)
                        for n in range(4):
                            v_hn.wait(e, i, u, n + 1)
                            mm = e.transpose(pT[u][:, n * P:(n + 1) * P], hn[u][:, n, :], ident[:, :])
                        mm.then_inc(t_tr.sem, 1)
                        a_hT.wait(e, i, u)
                        v_lo.wait(e, i, u, back=2)
                        a_kqv.wait(e, i, u, back=2)
                        e.matmul(pK[u][:, :], wk_sb[:, :], hT[u][:, :], start=True, stop=True).then_inc(t_kqv.sem, 1)
                        e.matmul(pQ[u][:, :], wqs[:, :], hT[u][:, :], start=True, stop=True).then_inc(t_kqv.sem, 1)
                        for n in range(4):
                            mm = e.matmul(pV[u][:, n * P:(n + 1) * P], hT[u][:, n * P:(n + 1) * P], wv_sb[:, :], start=True, stop=True)
                        mm.then_inc(t_kqv.sem, 1)

            @block.sync
            def _(e):
                for f in (*d_st, *d_k):
                    f.open(e)
                with e.Fori(0, NG // 2) as i:
                    for u in range(2):
                        tok = i * (2 * GRP) + u * GRP
                        v_lo.wait(e, i, u, 1)
                        for k, part in enumerate((khi, klo, khi, klo)):
                            e.dma_start(k_scr[k, :, :, bass.ds(tok, GRP)].rearrange("r g t -> g r t"), part[u][:, :].bitcast(F32)).then_inc(d_k[u].sem, 16)
                        v_lo.wait(e, i, u, 2)
                        for k, part in enumerate((qhi, qhi, qlo, qlo)):
                            e.dma_start(q_scr[k, :, :, bass.ds(tok, GRP)].rearrange("r g t -> g r t"), part[u][:, :].bitcast(F32)).then_inc(d_st[u].sem, 16)
                        a_kqv.wait(e, i, u, 3)
                        e.dma_start(v_scr[bass.ds(tok + HALO, GRP), :].rearrange("(n p) d -> p n d", p=P), vn[u][:, :, :]).then_inc(d_st[u].sem, 16)
                        d_k[u].wait(e, i + 1)
                        e.dma_start(kst[:, :, bass.ds(tok + HALO, GRP)].bitcast(F32),
                                    k_scr[:, :, :, bass.ds(tok, GRP)].rearrange("k r g t -> (k r) g t")).then_inc(d_kst, 16)
                for u in range(2):
                    d_st[u].wait(e, NG // 2)
                e.wait_ge(d_kst, 16 * NG)

        with ExitStack() as three:
            qbd = [sb(f"qbd{u}", [P, HG, 4, 4 * QB], F32R, three) for u in range(2)]
            qst = [sb(f"qst{u}", [P, HG, P], F32, three) for u in range(2)]
            vrep = [sb(f"vrep{u}", [P, KBLK, D], F32, three) for u in range(2)]
            vbd = [sb(f"vbd{u}", [P, KBLK, D], F32, three) for u in range(2)]
            pr = sb("pr", [P, HG, 4 * WIN], F32, three)
            prT = [sb(f"prT{u}", [P, HG, 4 * WIN], F32, three) for u in range(2)]
            nmax = sb("nmax", [P, 4 * HG], F32, three)
            rs = [sb(f"rs{u}", [P, 32], F32, three) for u in range(2)]
            rsT = sb("rsT", [P, 32], F32, three)
            rden = sb("rden", [P, 32], F32, three)
            mvd = sb("mvd", [P, 4, 32], F32, three)
            rbc = sb("rbc", [P, P], F32, three)
            oT = sb("oT", [P, P], F32, three)
            xg = sb("xg", [P, D], F32, three)
            xa = sb("xa", [P, D], F32, three)
            pS = [pb(three, f"pS{k}", [P, 1024]) for k in range(2)]
            pO = [pb(three, f"pO{u}", [P, 512]) for u in range(2)]
            pR = pb(three, "pR", [P, 512])
            pF = pb(three, "pF", [P, 512])
            t_s = Count(sem("t_s"), 4)
            v_mx = Count(sem("v_mx"), 4)
            a_e = Count(sem("a_e"), 16)
            v_tr = Count(sem("v_tr"), 4)
            v_den = Count(sem("v_den"), 3)
            p_vb = Count(sem("p_vb"), 1)
            p_qb = Count(sem("p_qb"), 1)
            t_o = Count(sem("t_o"), 1)
            t_r = Count(sem("t_r"), 1)
            a_r = Count(sem("a_r"), 1)
            v_o = Count(sem("v_o"), 1)
            t_f = Count(sem("t_f"), 1)
            v_x = Count(sem("v_x"), 1)
            p_x = Count(sem("p_x"), 2)
            s_z = sem("s_z")
            s_zp = sem("s_zp")
            d_q = [sem(f"d_q{u}") for u in range(2)]
            d_v = [sem(f"d_v{u}") for u in range(2)]
            block = three.enter_context(nc.Block())
            NI = NT // 2

            @block.sync
            def _(e):
                with e.Fori(0, NI) as i:
                    for u in range(2):
                        tok = i * (2 * P) + u * P
                        p_qb.wait(e, i, u, back=2)
                        e.dma_start(qst[u][:, :, :], q_scr[:, :, :, bass.ds(tok, P)].rearrange("k r g t -> (k r) g t")).then_inc(d_q[u], 16)
                        p_vb.wait(e, i, u, back=2)
                        for r in range(4):
                            src = v_scr[bass.ds(tok, KW), :].rearrange("(n k) d -> k n d", k=QB)
                            e.dma_start(vrep[u][32 * r:32 * r + 32, :, :], src).then_inc(d_v[u], 16)
                p_qb.wait(e, NI, 0, back=2)
                e.dma_start(qst[0][:, :, :], q_scr[:, :, :, 0:P].rearrange("k r g t -> (k r) g t")).then_inc(d_q[0], 16)

            @block.gpsimd
            def _(e):
                p_vb.open(e)
                p_x.open(e)
                p_qb.open(e)
                e.memset(vbd[1][:, :, :], 0.0).then_inc(s_zp, 1)

                def queries(i, u):
                    e.wait_ge(d_q[u], i * 16 + 16)
                    t_s.wait(e, i, u, back=2)
                    p_qb.wait(e, i, u, back=1)
                    e.tensor_tensor(qbd[u][:, :, :, :].rearrange("p g q (h t) -> p (g q) h t", h=4),
                                    strided(qst[u][:, :, :], 0, [[QB, 4 * HG], [0, 4], [1, QB]]),
                                    strided(eqd[:, :], 0, [[0, 4 * HG], [1, 4], [0, QB]]), ALU.mult).then_inc(p_qb.sem, 1)

                def residual(i, u):
                    g = i * 2 + u
                    sl = x_all[:, bass.ds(g, 1), :].rearrange("p a d -> p (a d)")
                    b = (g + (TPB - 1)) // TPB
                    p_x.wait(e, i, u, back=1)
                    apart(e)
                    e.tensor_tensor(xg[:, :], sl, gacv_bc[:, bass.ds(b, 1), :].rearrange("p a d -> p (a d)"), ALU.add).then_inc(p_x.sem, 1)
                    p_x.wait(e, i, u, 1)
                    v_x.wait(e, i, u)
                    apart(e)
                    e.tensor_tensor(sl, xg[:, :], xa[:, :], ALU.add).then_inc(p_x.sem, 1)

                queries(0, 0)
                with e.Fori(0, NI) as i:
                    for u in range(2):
                        e.wait_ge(d_v[u], i * 64 + 64)
                        t_o.wait(e, i, u, back=1)
                        e.tensor_tensor(vbd[u][:, :, :].rearrange("p n (g h d) -> p (n g) h d", g=HG, h=4),
                                        vrep[u][:, :, :].rearrange("p n (g h d) -> p (n g) h d", g=HG, h=4),
                                        strided(eqh[:, :], 0, [[0, KBLK * HG], [1, 4], [0, HD]]), ALU.mult).then_inc(p_vb.sem, 1)
                        queries(i + u, 1 - u)
                        residual(i, u)
                residual(NI, 0)
                p_x.wait(e, NI, 0)

            @block.scalar
            def _(e):
                a_e.open(e)
                a_r.open(e)
                with e.Fori(0, NI) as i:
                    for u in range(2):
                        for hg in range(HG):
                            v_mx.wait(e, i, u, hg + 1)
                            v_tr.wait(e, i, u, hg + 1, back=1)
                            if hg == 0:
                                v_den.wait(e, i, u, back=1)
                            for q in range(4):
                                k = 4 * hg + q
                                e.activation(pr[:, hg, q * WIN:(q + 1) * WIN], pS[hg % 2][:, q * (KW + QB):q * (KW + QB) + WIN], ACT.Exp,
                                             bias=nmax[:, k:k + 1], scale=-1.0, accum_out=rs[u][:, k:k + 1]).then_inc(a_e.sem, 1)
                            if hg == 1:
                                t_r.wait(e, i, u)
                                v_o.wait(e, i, u, back=1)
                                e.activation(rbc[:, :], pR[:, 0:P], ACT.Copy).then_inc(a_r.sem, 1)
                t_r.wait(e, NI, 0)
                v_o.wait(e, NI, 0, back=1)
                e.activation(rbc[:, :], pR[:, 0:P], ACT.Copy).then_inc(a_r.sem, 1)

            @block.tensor
            def _(e):
                t_s.open(e)
                t_o.open(e)
                t_r.open(e)
                t_f.open(e)
                e.wait_ge(s_z, 1)
                e.wait_ge(s_zp, 1)

                def scores(i, u, hg):
                    if hg >= 2:
                        a_e.wait(e, i, u, 4 * (hg - 1))
                    else:
                        a_e.wait(e, i, u, 4 * (hg + 3), back=1)
                    tok = i * (2 * P) + u * P
                    for q in range(4):
                        e.matmul(pS[hg % 2][:, q * KW:(q + 1) * KW], qbd[u][:, hg, q, :],
                                 kst[:, hg, bass.ds(tok, KW)], start=q % 2 == 0, stop=False, skip_group_check=True)
                        if q % 2:
                            m = (i * 2 + u) % TPB
                            mm = e.matmul(strided(pS[hg % 2][:, 0:1], (q - 1) * (KW + QB), [[KW + QB, 2], [1, WIN]]), identb[:, :],
                                          masks[:, bass.ds(m, 1), (q - 1) * WIN:(q + 1) * WIN].rearrange("p a w -> p (a w)"),
                                          start=False, stop=True, skip_group_check=True)
                    mm.then_inc(t_s.sem, 1)

                def weighted(i, u):
                    w = 1 - u
                    v_tr.wait(e, i, u, back=1)
                    p_vb.wait(e, i, u, back=1)
                    v_o.wait(e, i, u, back=2)
                    for j in range(KBLK):
                        lo, hi = max(0, j - 4), min(3, j)
                        for hg in range(HG):
                            mm = e.matmul(pO[w][32 * hg:32 * hg + 32, lo * QB:(hi + 1) * QB], vbd[w][:, j, 32 * hg:32 * hg + 32],
                                          strided(prT[w][:, hg, 0:1], j * QB + lo * (WIN - QB), [[WIN - QB, hi - lo + 1], [1, QB]]),
                                          start=j == 0, stop=j == KBLK - 1, skip_group_check=True)
                    mm.then_inc(t_o.sem, 1)

                def spread(i, u):
                    v_den.wait(e, i, u)
                    a_r.wait(e, i, u, back=1)
                    e.matmul(pR[:, 0:P], st_den[:, :], mvd[:, :, :].rearrange("p q t -> p (q t)"), start=True, stop=True).then_inc(t_r.sem, 1)

                def project(i, u):
                    v_o.wait(e, i, u)
                    v_x.wait(e, i, u, back=1)
                    e.matmul(pF[:, 0:D], oT[:, :], wc[:, :], start=True, stop=True).then_inc(t_f.sem, 1)

                with e.Fori(0, NI) as i:
                    for u in range(2):
                        p_qb.wait(e, i, u)
                        scores(i, u, 0)
                        scores(i, u, 1)
                        weighted(i, u)
                        scores(i, u, 2)
                        spread(i, u)
                        scores(i, u, 3)
                        project(i, u)
                weighted(NI, 0)
                spread(NI, 0)
                project(NI, 0)

            @block.vector
            def _(e):
                for cnt in (v_mx, v_tr, v_den, v_o, v_x):
                    cnt.open(e)
                for w in range(2):
                    e.memset(rs[w][:, :], 1.0)
                e.memset(prT[1][:, :, :], 0.0).then_inc(s_z, 1)
                e.wait_ge(s_z, 1)

                def maxima(i, u, hg):
                    t_s.wait(e, i, u, hg + 1)
                    a_e.wait(e, i, u, 4 * hg + 4, back=1)
                    e.tensor_reduce(nmax[:, 4 * hg:4 * hg + 4], strided(pS[hg % 2][:, 0:1], 0, [[KW + QB, 4], [1, WIN]]),
                                    AX.X, ALU.min).then_inc(v_mx.sem, 1)

                def turn(i, u, hg):
                    a_e.wait(e, i, u, 4 * hg + 4)
                    if hg == 0:
                        t_o.wait(e, i, u, back=1)
                    e.transpose(prT[u][:, hg, :], pr[:, hg, :]).then_inc(v_tr.sem, 1)

                def denominators(i, u):
                    w = 1 - u
                    a_e.wait(e, i, u, back=1)
                    v_den.wait(e, i, u, 2, back=1)
                    e.transpose(rsT[:, :], rs[w][:, :]).then_inc(v_den.sem, 1)
                    v_den.wait(e, i, u, 1)
                    e.reciprocal(rden[:, :], rsT[:, :]).then_inc(v_den.sem, 1)
                    v_den.wait(e, i, u, 2)
                    t_r.wait(e, i, u, back=1)
                    e.tensor_tensor(mvd[:, :, :], strided(rden[:, :], 0, [[0, 4], [1, 32]]),
                                    strided(eqq[:, :], 0, [[1, 4], [0, 32]]), ALU.mult).then_inc(v_den.sem, 1)

                def normalise(i, u):
                    a_r.wait(e, i, u)
                    t_o.wait(e, i, u)
                    t_f.wait(e, i, u, back=1)
                    e.tensor_tensor(oT[:, :], pO[1 - u][:, 0:P], rbc[:, :], ALU.mult).then_inc(v_o.sem, 1)

                def scaled(i, u):
                    g = i * 2 + u
                    b = (g + (TPB - 1)) // TPB
                    t_f.wait(e, i, u)
                    p_x.wait(e, i, u, back=1)
                    e.tensor_tensor(xa[:, :], pF[:, 0:D], ga_bc[:, bass.ds(b, 1), :].rearrange("p a d -> p (a d)"), ALU.mult).then_inc(v_x.sem, 1)

                with e.Fori(0, NI) as i:
                    for u in range(2):
                        maxima(i, u, 0)
                        denominators(i, u)
                        maxima(i, u, 1)
                        turn(i, u, 0)
                        maxima(i, u, 2)
                        normalise(i, u)
                        turn(i, u, 1)
                        maxima(i, u, 3)
                        scaled(i, u)
                        turn(i, u, 2)
                        turn(i, u, 3)
                denominators(NI, 0)
                normalise(NI, 0)
                scaled(NI, 0)

        attn.close()

        gates = sb("gates", [P, 2, NT])
        gidx = sb("gidx", [P, 2 * (NF + 2)], I32)
        sidx = sb("sidx", [P, 2 * (NF + 2)], I32)
        eid = sb("eid", [1, NF + 2], I32)
        h_scr = nc.dram_tensor("h_scr", (T, D), F32, kind="Internal").ap()
        w1_all = sb("w1_all", [P, NE * FF])
        w2_all = sb("w2_all", [P, NE * FC * D])
        b1_all = sb("b1_all", [P, NE * FC])
        b2_all = sb("b2_all", [P, NE, D])
        d_wt = sem("d_wt")
        N_WT = 6
        y_scr = nc.dram_tensor("y_scr", (2 * T + NF * FT + 2, D), F32, kind="Internal").ap()

        route = ExitStack()
        score = sb("score", [P, NT, NE], F32, route)
        with ExitStack() as four:
            s4 = lambda n, sh, dt=F32: sb(n, sh, dt, four)
            rw1_sb = s4("rw1_sb", [P, FF])
            rb1_sb = s4("rb1_sb", [P, FC])
            rw2_sb = s4("rw2_sb", [P, FC, NE])
            rb2_bc = s4("rb2_bc", [P, NE])
            stat2 = s4("stat2", [P, NT, 6])
            mv2 = s4("mv2", [P, NT, 2])
            var2 = s4("var2", [P, NT])
            rstd2 = s4("rstd2", [P, NT])
            nmr2 = s4("nmr2", [P, NT])
            hn2 = [s4(f"hn2{u}", [P, 4, D]) for u in range(2)]
            hm2 = [s4(f"hm2{u}", [P, 4, D]) for u in range(2)]
            h2 = [s4(f"h2{u}", [P, 4, D]) for u in range(2)]
            h2T = [s4(f"h2T{u}", [P, GRP]) for u in range(2)]
            act = [s4(f"act{u}", [P, FC, GRP]) for u in range(2)]
            pT2 = [pb(four, f"pT2{u}", [P, GRP]) for u in range(2)]
            pA2 = [pb(four, f"pA2{k}", [P, GRP]) for k in range(FC)]
            pSc = [pb(four, f"pSc{u}", [P, GRP]) for u in range(2)]
            d_rw = sem("d_rw")
            v_st = sem("v_st")
            a_rt = sem("a_rt")
            v_h2 = Count(sem("v_h2"), 4)
            p_h2 = Count(sem("p_h2"), 2)
            t_t2 = Count(sem("t_t2"), 1)
            a_t2 = Count(sem("a_t2"), 1)
            t_a2 = Count(sem("t_a2"), FC)
            a_a2 = Count(sem("a_a2"), FC)
            t_sc = Count(sem("t_sc"), 1)
            v_sc = Count(sem("v_sc"), 1)
            d_h = [Flights(sem(f"d_h{u}"), 1) for u in range(2)]
            block = four.enter_context(nc.Block())

            @block.sync
            def _(e):
                for f in d_h:
                    f.open(e)
                e.dma_start(rw1_sb[:, :], rw1).then_inc(d_rw, 16)
                e.dma_start(rw2_sb[:, :, :], rw2.rearrange("(c p) n -> p c n", p=P)).then_inc(d_rw, 16)
                with nc.allow_non_contiguous_dma(reason="four values a partition"):
                    e.dma_start(rb1_sb[:, :], rb1.rearrange("(c p) -> p c", p=P)).then_inc(d_rw, 16)
                e.dma_start(rb2_bc[:, :], rb2.rearrange("(a n) -> a n", a=1).broadcast_to([P, NE])).then_inc(d_rw, 16)
                for k in range(2):
                    half_e = slice(k * NE // 2, (k + 1) * NE // 2)
                    e.dma_start(w1_all[:, k * NE * FF // 2:(k + 1) * NE * FF // 2].rearrange("p (e f) -> p e f", f=FF),
                                W1[half_e, :, :].rearrange("e d f -> d e f")).then_inc(d_wt, 16)
                    e.dma_start(w2_all[:, k * NE * FF // 2:(k + 1) * NE * FF // 2].rearrange("p (c d) -> p c d", d=D),
                                W2[half_e, :, :].rearrange("e (c p) d -> p (e c) d", p=P)).then_inc(d_wt, 16)
                with nc.allow_non_contiguous_dma(reason="32 values a partition, once"):
                    e.dma_start(b1_all[:, :], b1.rearrange("e (c p) -> p (e c)", p=P)).then_inc(d_wt, 16)
                e.dma_start(b2_all[:, :, :], b2.rearrange("(a e) d -> a e d", a=1).broadcast_to([P, NE, D])).then_inc(d_wt, 16)
                with e.Fori(0, NG // 2) as i:
                    for u in range(2):
                        p_h2.wait(e, i, u)
                        e.dma_start(h_scr[bass.ds(i * (2 * GRP) + u * GRP, GRP), :].rearrange("(n p) d -> p n d", p=P),
                                    h2[u][:, :, :]).then_inc(d_h[u].sem, 16)
                for u in range(2):
                    d_h[u].wait(e, NG // 2)

            @block.vector
            def _(e):
                v_h2.open(e)
                v_sc.open(e)
                with e.Fori(0, NT // 4) as i:
                    for n in range(4):
                        g = i * 4 + n
                        e.bn_stats(stat2[:, bass.ds(g, 1), :].rearrange("p a s -> p (a s)"),
                                   x_all[:, bass.ds(g + 1, 1), :].rearrange("p a d -> p (a d)")).then_inc(v_st, 1)
                e.wait_ge(v_st, NT)
                for n in range(NT):
                    e.bn_aggr(mv2[:, n, :], stat2[:, n, :]).then_inc(v_st, 1)
                e.wait_ge(v_st, 2 * NT)
                e.tensor_scalar(var2[:, :], mv2[:, :, 1], EPS, None, ALU.add).then_inc(v_st, 1)
                e.wait_ge(a_rt, 1)
                e.reciprocal(rstd2[:, :], var2[:, :]).then_inc(v_st, 1)
                e.wait_ge(v_st, 2 * NT + 2)
                e.scalar_tensor_tensor(out=nmr2[:, :], in0=mv2[:, :, 0], scalar=-1.0, in1=rstd2[:, :], op0=ALU.mult, op1=ALU.mult).then_inc(v_st, 1)
                e.wait_ge(v_st, 2 * NT + 3)

                def add_bias(i, u):
                    t_sc.wait(e, i, u)
                    e.tensor_tensor(score[:, bass.ds(i * 8 + 4 * u, 4), :], pSc[u][:, 0:4 * NE].rearrange("p (n k) -> p n k", n=4),
                                    strided(rb2_bc[:, :], 0, [[0, 4], [1, NE]]), ALU.add).then_inc(v_sc.sem, 1)

                e.wait_ge(d_rw, 64)
                with e.Fori(0, NG // 2) as i:
                    for u in range(2):
                        p_h2.wait(e, i, u, 1, back=2)
                        for n in range(4):
                            g = i * 8 + (4 * u + n)
                            e.tensor_scalar(hn2[u][:, n, :], x_all[:, bass.ds(g + 1, 1), :].rearrange("p a d -> p (a d)"),
                                            rstd2[:, bass.ds(g, 1)], nmr2[:, bass.ds(g, 1)], ALU.mult, ALU.add).then_inc(v_h2.sem, 1)
                        if u == 1:
                            add_bias(i, 0)
                            add_bias(i, 1)

            @block.gpsimd
            def _(e):
                p_h2.open(e)
                e.wait_ge(d_rw, 64)
                with e.Fori(0, NG // 2) as i:
                    for u in range(2):
                        v_h2.wait(e, i, u)
                        t_t2.wait(e, i, u, back=2)
                        d_h[u].wait(e, i)
                        apart(e)
                        e.tensor_tensor(hm2[u][:, :, :], hn2[u][:, :, :], bcast_row(cb_bc, i, 4), ALU.mult).then_inc(p_h2.sem, 1)
                        p_h2.wait(e, i, u, 1)
                        apart(e)
                        e.tensor_tensor(h2[u][:, :, :], hm2[u][:, :, :], bcast_row(sb_bc, i, 4), ALU.add).then_inc(p_h2.sem, 1)

            @block.scalar
            def _(e):
                a_t2.open(e)
                a_a2.open(e)
                e.wait_ge(v_st, 2 * NT + 1)
                e.activation(var2[:, :], var2[:, :], ACT.Sqrt).then_inc(a_rt, 1)
                e.wait_ge(d_rw, 64)
                with e.Fori(0, NG // 2) as i:
                    for u in range(2):
                        t_t2.wait(e, i, u)
                        t_a2.wait(e, i, u, back=2)
                        e.activation(h2T[u][:, :], pT2[u][:, :], ACT.Copy).then_inc(a_t2.sem, 1)
                        for k in range(FC):
                            t_a2.wait(e, i, u, k + 1)
                            t_sc.wait(e, i, u, back=2)
                            e.activation(act[u][:, k, :], pA2[k][:, :], ACT.Relu, bias=rb1_sb[:, k:k + 1]).then_inc(a_a2.sem, 1)

            @block.tensor
            def _(e):
                t_t2.open(e)
                t_a2.open(e)
                t_sc.open(e)
                e.wait_ge(d_rw, 64)
                with e.Fori(0, NG // 2) as i:
                    for u in range(2):
                        p_h2.wait(e, i, u)
                        a_t2.wait(e, i, u, back=2)
                        for n in range(4):
                            mm = e.transpose(pT2[u][:, n * P:(n + 1) * P], h2[u][:, n, :], ident[:, :])
                        mm.then_inc(t_t2.sem, 1)
                        a_t2.wait(e, i, u)
                        for k in range(FC):
                            a_a2.wait(e, i, u, k + 1, back=1)
                            e.matmul(pA2[k][:, :], rw1_sb[:, k * P:(k + 1) * P], h2T[u][:, :], start=True, stop=True).then_inc(t_a2.sem, 1)
                        v_sc.wait(e, i, u, back=2)
                        a_a2.wait(e, i, u)
                        for n in range(4):
                            for k in range(FC):
                                mm = e.matmul(pSc[u][:, n * NE:(n + 1) * NE], act[u][:, k, n * P:(n + 1) * P], rw2_sb[:, k, :],
                                              start=k == 0, stop=k == FC - 1)
                        mm.then_inc(t_sc.sem, 1)

        with ExitStack() as five:
            s5 = lambda n, sh, dt=F32: sb(n, sh, dt, five)
            rev = s5("rev", [P, NE])
            m12 = s5("m12", [P, 2, NT])
            eqm = s5("eqm", [P, NT, NE])
            rank = s5("rank", [P, NT])
            oh = [s5(f"oh{k}", [P, NT, NE]) for k in range(2)]
            sc2 = s5("sc2", [P, NT, NE])
            ohb = s5("ohb", [P, NT * NE], BF16)
            upper = s5("upper", [P, P], BF16)
            onesb = s5("onesb", [P, P], BF16)
            tot = s5("tot", [P, NT + 16, NE])
            cum = [s5(f"cum{k}", [P, NT + 16, NE]) for k in range(2)]
            off = s5("off", [P, NT, NE])
            cnt_i = s5("cnt_i", [P, NE], I32)
            til = s5("til", [P, NE])
            tcu = [s5(f"tcu{k}", [P, 8 + NE]) for k in range(2)]
            base = s5("base", [P, NE])
            posg = s5("posg", [P, NT, NE])
            posm = s5("posm", [P, NT, NE])
            pos = s5("pos", [P, 2, NT])
            pos_i = s5("pos_i", [P, 2 * NT], I32)
            lo_i = s5("lo_i", [P, 2 * NT], I32)
            hi_i = s5("hi_i", [P, 2 * NT], I32)
            lo_b = s5("lo_b", [P, 2 * NT], BF16)
            hi_b = s5("hi_b", [P, 2 * NT], BF16)
            io_lo = s5("io_lo", [P, P, 2 * NT], BF16)
            io_hi = s5("io_hi", [P, SC, 2 * NT], BF16)
            io_c = s5("io_c", [P, 2 * NT], BF16)
            io_p = s5("io_p", [P, 1])
            io_s = s5("io_s", [P, SC])
            one_lo = s5("one_lo", [P, P, 2 * NT], BF16)
            one_hi = s5("one_hi", [P, SC, 2 * NT], BF16)
            mapv = s5("mapv", [P, 2, SC, 2 * NT], BF16)
            io_j = s5("io_j", [1, NF + 2])
            ge = s5("ge", [1, NF + 2, NE])
            eidf = s5("eidf", [1, NF + 2])
            cc = s5("cc", [P, SC])
            pp = s5("pp", [P, SC])
            fa = s5("fa", [P, SC])
            fb = s5("fb", [P, SC])
            fc = s5("fc", [P, SC])
            fd = s5("fd", [P, SC])
            pPre = pb(five, "pPre", [P, 512])
            pTot = pb(five, "pTot", [P, 512])
            pMap = pb(five, "pMap", [P, 512])
            v5, p5, a5, t5 = sem("v5"), sem("p5"), sem("a5"), sem("t5")
            n5 = {}
            k5 = [0]
            block = five.enter_context(nc.Block())

            @block.gpsimd
            def _(e):
                small = dict(allow_small_or_imprecise_dtypes=True)
                e.iota(rev[:, :], [[-1, NE]], NE, 0, **small).then_inc(p5, 1)
                e.memset(onesb[:, :], 1.0).then_inc(p5, 1)
                e.wait_ge(p5, 2)
                e.affine_select(out=upper[:, :], in_=onesb[:, :], compare_op=ALU.is_gt, fill=0.0, base=0,
                                pattern=[[1, P]], channel_multiplier=-1).then_inc(p5, 1)
                e.iota(io_j[:, :], [[1, NF + 2]], 0, 0, **small).then_inc(p5, 1)
                e.iota(io_lo[:, :, :], [[1, P], [0, 2 * NT]], 0, 0, **small).then_inc(p5, 1)
                e.iota(io_hi[:, :, :], [[1, SC], [0, 2 * NT]], 0, 0, **small).then_inc(p5, 1)
                e.iota(io_c[:, :], [[1, 2 * NT]], 1, 0, **small).then_inc(p5, 1)
                e.iota(io_p[:, :], [[0, 1]], 0, 1, **small).then_inc(p5, 1)
                e.iota(io_s[:, :], [[P, SC]], 0, 1, **small).then_inc(p5, 1)

            @block.vector
            def _(e):
                def step(ins, name=None):
                    k5[0] += 1
                    if name:
                        n5[name] = k5[0]
                    ins.then_inc(v5, 1)

                def own():
                    e.wait_ge(v5, k5[0])

                def per_tile(t):
                    return strided(t, 0, [[1, NT], [0, NE]])

                def per_expert(t, n=NT):
                    return strided(t, 0, [[0, n], [1, NE]])

                e.wait_ge(p5, 2)
                cur = score
                for k in range(2):
                    step(e.tensor_reduce(m12[:, k, :], cur[:, :, :], AX.X, ALU.max), f"m{k}")
                    own()
                    step(e.tensor_tensor(eqm[:, :, :], cur[:, :, :], per_tile(m12[:, k, :]), ALU.is_equal))
                    own()
                    step(e.tensor_tensor(eqm[:, :, :], eqm[:, :, :], per_expert(rev[:, :]), ALU.mult))
                    own()
                    step(e.tensor_reduce(rank[:, :], eqm[:, :, :], AX.X, ALU.max))
                    own()
                    step(e.tensor_tensor(oh[k][:, :, :], per_expert(rev[:, :]), per_tile(rank[:, :]), ALU.is_equal))
                    own()
                    if k == 0:
                        step(e.scalar_tensor_tensor(out=sc2[:, :, :], in0=oh[0][:, :, :], scalar=-3e38, in1=score[:, :, :],
                                                    op0=ALU.mult, op1=ALU.add))
                        own()
                        cur = sc2
                step(e.tensor_tensor(ohb[:, :].rearrange("p (t k) -> p t k", k=NE), oh[0][:, :, :], oh[1][:, :, :], ALU.add), "ohb")
                step(e.tensor_tensor(gates[:, 1, :], m12[:, 1, :], m12[:, 0, :], ALU.subtract), "gd")
                for t in (tot, cum[0], cum[1]):
                    step(e.memset(t[:, 0:16, :], 0.0))
                for t in tcu:
                    step(e.memset(t[:, 0:8], 0.0))
                own()
                e.wait_ge(t5, 1)
                step(e.tensor_copy(tot[:, 16:, :], pTot[:, 0:NT * NE].rearrange("p (t k) -> p t k", k=NE)))
                own()
                src = tot
                for r, s in enumerate((1, 2, 4, 8, 16)):
                    dst = cum[r % 2]
                    step(e.tensor_tensor(dst[:, 16:, :], src[:, 16:, :], src[:, 16 - s:16 + NT - s, :], ALU.add))
                    own()
                    src = dst
                step(e.tensor_scalar(til[:, :], src[:, 16 + NT - 1, :], float(FT - 1), None, ALU.add))
                own()
                step(e.tensor_copy(cnt_i[:, :], til[:, :]))
                own()
                step(e.tensor_scalar(cnt_i[:, :], cnt_i[:, :], FT.bit_length() - 1, None, ALU.logical_shift_right))
                own()
                step(e.tensor_copy(tcu[0][:, 8:], cnt_i[:, :]))
                own()
                for r, s in enumerate((1, 2, 4)):
                    step(e.tensor_tensor(tcu[(r + 1) % 2][:, 8:], tcu[r % 2][:, 8:], tcu[r % 2][:, 8 - s:8 + NE - s], ALU.add))
                    own()
                step(e.tensor_copy(til[:, :], cnt_i[:, :]))
                own()
                step(e.tensor_tensor(base[:, :], tcu[1][:, 8:], til[:, :], ALU.subtract))
                own()
                step(e.tensor_scalar(base[:, :], base[:, :], float(FT), None, ALU.mult))
                e.wait_ge(p5, 9)
                step(e.tensor_tensor(ge[:, :, :], strided(io_j[:, :], 0, [[1, NF + 2], [0, NE]]),
                                     strided(tcu[1][0:1, 8:9], 0, [[0, NF + 2], [1, NE]]), ALU.is_ge))
                own()
                step(e.tensor_reduce(eidf[:, :], ge[:, :, :], AX.X, ALU.add))
                own()
                step(e.tensor_scalar(eid[:, :], eidf[:, :], float(NE - 1), None, ALU.min))
                step(e.tensor_tensor(off[:, :, :], src[:, 16:, :], tot[:, 16:, :], ALU.subtract))
                own()
                step(e.tensor_tensor(off[:, :, :], off[:, :, :], per_expert(base[:, :]), ALU.add))
                own()
                step(e.tensor_tensor(posg[:, :, :], pPre[:, 0:NT * NE].rearrange("p (t k) -> p t k", k=NE), off[:, :, :], ALU.add))
                own()
                for k in range(2):
                    step(e.tensor_tensor(posm[:, :, :], posg[:, :, :], oh[k][:, :, :], ALU.mult))
                    own()
                    step(e.tensor_reduce(pos[:, k, :], posm[:, :, :], AX.X, ALU.add))
                    own()
                step(e.tensor_copy(pos_i[:, :], pos[:, :, :].rearrange("p k t -> p (k t)")))
                own()
                step(e.tensor_scalar(lo_i[:, :], pos_i[:, :], P - 1, None, ALU.bitwise_and))
                step(e.tensor_scalar(hi_i[:, :], pos_i[:, :], P.bit_length() - 1, None, ALU.logical_shift_right))
                own()
                step(e.tensor_copy(lo_b[:, :], lo_i[:, :]))
                step(e.tensor_copy(hi_b[:, :], hi_i[:, :]))
                own()
                step(e.tensor_tensor(one_hi[:, :, :], io_hi[:, :, :], strided(hi_b[:, :], 0, [[0, SC], [1, 2 * NT]]), ALU.is_equal))
                step(e.tensor_tensor(one_lo[:, :, :], io_lo[:, :, :], strided(lo_b[:, :], 0, [[0, P], [1, 2 * NT]]), ALU.is_equal))
                own()
                step(e.tensor_tensor(mapv[:, 0, :, :], one_hi[:, :, :], strided(io_c[:, :], 0, [[0, SC], [1, 2 * NT]]), ALU.mult))
                step(e.tensor_scalar(mapv[:, 1, :, :], one_hi[:, :, :], io_p[:, 0:1], None, ALU.mult), "map")
                e.wait_ge(a5, 1)
                step(e.tensor_scalar(m12[:, 0, :], m12[:, 1, :], 1.0, None, ALU.add))
                own()
                step(e.reciprocal(gates[:, 0, :], m12[:, 0, :]))
                own()
                step(e.tensor_tensor(gates[:, 1, :], m12[:, 1, :], gates[:, 0, :], ALU.mult))
                step(e.memset(gidx[:, SC:], 0))
                step(e.memset(sidx[:, SC:], 0))
                e.wait_ge(t5, 2)
                step(e.tensor_copy(cc[:, :], pMap[:, 0:SC]))
                step(e.tensor_copy(pp[:, :], pMap[:, SC:2 * SC]))
                own()
                step(e.tensor_scalar(fa[:, :], cc[:, :], float(NT + 1), -float(NT), ALU.is_ge, ALU.mult))
                own()
                step(e.tensor_tensor(fb[:, :], fa[:, :], cc[:, :], ALU.add))
                own()
                step(e.tensor_scalar(fb[:, :], fb[:, :], float(P), -float(P), ALU.mult, ALU.add))
                own()
                step(e.tensor_tensor(fb[:, :], fb[:, :], pp[:, :], ALU.add))
                own()
                step(e.tensor_scalar(gidx[:, 0:SC], fb[:, :], 0.0, None, ALU.max))
                step(e.tensor_scalar(fc[:, :], cc[:, :], float(P), -float(P), ALU.mult, ALU.add))
                own()
                step(e.tensor_tensor(fc[:, :], fc[:, :], pp[:, :], ALU.add))
                step(e.tensor_scalar(fd[:, :], io_s[:, :], float(2 * T + P), None, ALU.add))
                step(e.tensor_scalar(fa[:, :], cc[:, :], 0.0, None, ALU.is_equal))
                own()
                step(e.tensor_tensor(fd[:, :], fd[:, :], fa[:, :], ALU.mult))
                own()
                step(e.tensor_tensor(sidx[:, 0:SC], fd[:, :], fc[:, :], ALU.add))
                own()

            @block.scalar
            def _(e):
                e.wait_ge(v5, n5["gd"])
                e.activation(m12[:, 1, :], gates[:, 1, :], ACT.Exp).then_inc(a5, 1)

            @block.tensor
            def _(e):
                e.wait_ge(p5, 3)
                e.wait_ge(v5, n5["ohb"])
                e.matmul(pPre[:, 0:NT * NE], upper[:, :], ohb[:, :], start=True, stop=True)
                e.matmul(pTot[:, 0:NT * NE], onesb[:, :], ohb[:, :], start=True, stop=True).then_inc(t5, 1)
                e.wait_ge(v5, n5["map"])
                for k in range(2 * NT):
                    mm = e.matmul(pMap[:, 0:2 * SC], one_lo[:, :, k], mapv[:, :, :, k].rearrange("p a s -> p (a s)"),
                                  start=k == 0, stop=k == 2 * NT - 1)
                mm.then_inc(t5, 1)

        route.close()

        with ExitStack() as six:
            s6 = lambda n, sh, dt=F32: sb(n, sh, dt, six)
            gi = [s6(f"gi{u}", [P, 2], I32) for u in range(2)]
            si = [s6(f"si{u}", [P, 2], I32) for u in range(2)]
            w1t = [s6(f"w1t{u}", [P, FF]) for u in range(2)]
            hg = [s6(f"hg{u}", [P, 2, P]) for u in range(2)]
            hgT = [s6(f"hgT{u}", [P, FT]) for u in range(2)]
            ac = [s6(f"ac{u}", [P, FC, FT]) for u in range(2)]
            ys = [s6(f"ys{u}", [P, 2, D]) for u in range(2)]
            pTg = [pb(six, f"pTg{u}", [P, 512]) for u in range(2)]
            pU = [[pb(six, f"pU{u}{k}", [P, 512]) for k in range(2)] for u in range(2)]
            pY = [pb(six, f"pY{u}", [P, 512]) for u in range(2)]
            d_g = [sem(f"d_g{u}") for u in range(2)]
            d_y = [Flights(sem(f"d_y{u}"), 2) for u in range(2)]
            v_gi = Count(sem("v_gi"), 1)
            v_si = Count(sem("v_si"), 1)
            v_w = Count(sem("v_w"), 1)
            t_tg = Count(sem("t_tg"), 1)
            v_tg = Count(sem("v_tg"), 1)
            t_up = Count(sem("t_up"), 2)
            a_up = Count(sem("a_up"), FC)
            t_dn = Count(sem("t_dn"), 1)
            v_y = Count(sem("v_y"), 1)
            block = six.enter_context(nc.Block())
            NI6 = NF // 2

            def expert(e, i, u):
                return e.value_load(eid[0:1, bass.ds(i * 2 + u, 1)], min_val=0, max_val=NE - 1)

            @block.gpsimd
            def _(e):
                def gather(i, u):
                    v_gi.wait(e, i, u)
                    t_tg.wait(e, i, u, back=2)
                    apart(e)
                    for k in range(2):
                        e.indirect_dma_start(out=hg[u][:, k, :], out_offset=None, in_=h_scr,
                                             in_offset=bass.IndirectOffsetOnAxis(ap=gi[u][:, k:k + 1].bitcast(U32), axis=0)).then_inc(d_g[u], 16)

                def scatter(i, u):
                    v_si.wait(e, i, u)
                    v_y.wait(e, i, u)
                    apart(e)
                    for k in range(2):
                        e.indirect_dma_start(out=y_scr, out_offset=bass.IndirectOffsetOnAxis(ap=si[u][:, k:k + 1].bitcast(U32), axis=0),
                                             in_=ys[u][:, k, :], in_offset=None).then_inc(d_y[u].sem, 16)

                for u in range(2):
                    spare = 2 * T + NF * FT + u
                    e.dma_start(y_scr[spare:spare + 1, :], ident[0:1, :]).then_inc(d_y[u].sem, 16)
                gather(0, 0)
                gather(0, 1)
                with e.Fori(0, NI6) as i:
                    for u in range(2):
                        gather(i + 1, u)
                        scatter(i, u)
                scatter(NI6, 0)
                for u in range(2):
                    e.wait_ge(d_g[u], 32 * (NI6 + 1))
                    d_y[u].wait(e, NI6 + 1 - u)

            @block.scalar
            def _(e):
                a_up.open(e)
                e.wait_ge(d_wt, 16 * N_WT)

                def relu(i, u):
                    x_ = expert(e, i, u)
                    t_dn.wait(e, i, u, back=2)
                    for k in range(FC):
                        if k % 2 == 0:
                            t_up.wait(e, i, u, k // 2 + 1)
                            apart(e)
                        e.activation(ac[u][:, k, :], pU[u][k // 2][:, (k % 2) * FT:(k % 2 + 1) * FT], ACT.Relu,
                                     bias=b1_all[:, bass.ds(x_ * FC + k, 1)]).then_inc(a_up.sem, 1)

                with e.Fori(0, NI6) as i:
                    for u in range(2):
                        relu(i, u)
                relu(NI6, 0)

            @block.vector
            def _(e):
                for cnt in (v_gi, v_si, v_w, v_tg, v_y):
                    cnt.open(e)
                e.wait_ge(d_wt, 16 * N_WT)

                def first_matrix(i, u):
                    x_ = expert(e, i, u)
                    t_up.wait(e, i, u, back=2)
                    apart(e)
                    e.tensor_copy(w1t[u][:, :], w1_all[:, bass.ds(x_ * FF, FF)]).then_inc(v_w.sem, 1)

                def gather_index(i, u):
                    t_tg.wait(e, i, u, back=2)
                    apart(e)
                    e.tensor_copy(gi[u][:, :], gidx[:, bass.ds(i * 4 + 2 * u, 2)]).then_inc(v_gi.sem, 1)

                def gathered(i, u):
                    t_tg.wait(e, i, u)
                    t_up.wait(e, i, u, back=2)
                    e.tensor_copy(hgT[u][:, :], pTg[u][:, 0:FT]).then_inc(v_tg.sem, 1)

                def result(i, u):
                    x_ = expert(e, i, u)
                    d_y[u].wait(e, i)
                    apart(e)
                    e.tensor_copy(si[u][:, :], sidx[:, bass.ds(i * 4 + 2 * u, 2)]).then_inc(v_si.sem, 1)
                    t_dn.wait(e, i, u)
                    e.tensor_tensor(ys[u][:, :, :], pY[u][:, 0:2 * D].rearrange("p (k d) -> p k d", k=2),
                                    b2_all[:, bass.ds(x_, 1), :].broadcast_to([P, 2, D]), ALU.add).then_inc(v_y.sem, 1)

                gather_index(0, 0)
                gather_index(0, 1)
                first_matrix(0, 0)
                gathered(0, 0)
                with e.Fori(0, NI6) as i:
                    for u in range(2):
                        gather_index(i + 1, u)
                        first_matrix(i + u, 1 - u)
                        gathered(i + u, 1 - u)
                        result(i, u)
                result(NI6, 0)

            @block.tensor
            def _(e):
                for cnt in (t_tg, t_up, t_dn):
                    cnt.open(e)
                e.wait_ge(d_wt, 16 * N_WT)

                def up(i, u):
                    e.wait_ge(d_g[u], i * 32 + 32)
                    v_tg.wait(e, i, u, back=2)
                    for k in range(2):
                        mm = e.transpose(pTg[u][:, k * P:(k + 1) * P], hg[u][:, k, :], ident[:, :])
                    mm.then_inc(t_tg.sem, 1)
                    v_w.wait(e, i, u)
                    v_tg.wait(e, i, u)
                    a_up.wait(e, i, u, back=2)
                    for k in range(FC):
                        mm = e.matmul(pU[u][k // 2][:, (k % 2) * FT:(k % 2 + 1) * FT], w1t[u][:, k * P:(k + 1) * P], hgT[u][:, :],
                                      start=True, stop=True)
                        if k % 2:
                            mm.then_inc(t_up.sem, 1)

                def down(i, u):
                    x_ = expert(e, i, u)
                    v_y.wait(e, i, u, back=2)
                    a_up.wait(e, i, u)
                    for r in range(2):
                        for k in range(FC):
                            mm = e.matmul(pY[u][:, r * D:(r + 1) * D], ac[u][:, k, r * P:(r + 1) * P], w2_all[:, bass.ds(x_ * FF + k * D, D)],
                                          start=k == 0, stop=k == FC - 1)
                    mm.then_inc(t_dn.sem, 1)

                up(0, 0)
                with e.Fori(0, NI6) as i:
                    for u in range(2):
                        up(i + u, 1 - u)
                        down(i, u)
                down(NI6, 0)

        with ExitStack() as seven:
            s7 = lambda n, sh, dt=F32: sb(n, sh, dt, seven)
            y1 = s7("y1", [P, B, TPB, D])
            y2 = s7("y2", [P, B, TPB, D])
            fin = s7("fin", [P, B, TPB, D])
            d_ld = [sem(f"d_ld{b}") for b in range(B)]
            a7, v7, p7, d_out = sem("a7"), sem("v7"), sem("p7"), sem("d_out")
            block = seven.enter_context(nc.Block())

            @block.sync
            def _(e):
                for b in range(B):
                    for k, t in enumerate((y1, y2)):
                        e.dma_start(t[:, b, :, :], y_scr[k * T + b * S:k * T + (b + 1) * S, :].rearrange("(n p) d -> p n d", p=P)).then_inc(d_ld[b], 16)
                for b in range(B):
                    e.wait_ge(p7, b + 1)
                    e.dma_start(of[b * S:(b + 1) * S, :].rearrange("(n p) d -> p n d", p=P), fin[:, b, :, :]).then_inc(d_out, 16)
                e.wait_ge(d_out, 16 * B)

            @block.scalar
            def _(e):
                for b in range(B):
                    e.wait_ge(d_ld[b], 32)
                    for n in range(TPB):
                        g = b * TPB + n
                        e.activation(y1[:, b, n, :], y1[:, b, n, :], ACT.Copy, scale=gates[:, 0, g:g + 1]).then_inc(a7, 1)

            @block.vector
            def _(e):
                for b in range(B):
                    e.wait_ge(d_ld[b], 32)
                    for n in range(TPB):
                        g = b * TPB + n
                        e.wait_ge(a7, g + 1)
                        e.scalar_tensor_tensor(out=y2[:, b, n, :], in0=y2[:, b, n, :], scalar=gates[:, 1, g:g + 1], in1=y1[:, b, n, :],
                                               op0=ALU.mult, op1=ALU.add).then_inc(v7, 1)
                    e.wait_ge(v7, (b + 1) * (TPB + 1) - 1)
                    e.tensor_tensor(y2[:, b, :, :], y2[:, b, :, :], strided(gb_bc[:, b, :], 0, [[0, TPB], [1, D]]), ALU.mult).then_inc(v7, 1)

            @block.gpsimd
            def _(e):
                for b in range(B):
                    e.wait_ge(v7, (b + 1) * (TPB + 1))
                    e.tensor_tensor(fin[:, b, :, :], y2[:, b, :, :], x_all[:, 1 + b * TPB:1 + (b + 1) * TPB, :], ALU.add).then_inc(p7, 1)


_INS = ['L0_attn_x', 'L0_attn_alpha', 'L0_attn_Wq', 'L0_attn_bq', 'L0_attn_Wk', 'L0_attn_bk', 'L0_attn_Wv', 'L0_attn_bv',
        'L0_attn_W_o', 'L0_attn_Wfc', 'L0_attn_bfc', 'L0_ffn_rw1', 'L0_ffn_rb1', 'L0_ffn_rw2', 'L0_ffn_rb2', 'L0_ffn_W1',
        'L0_ffn_b1', 'L0_ffn_W2', 'L0_ffn_b2', 'L0_c', 'L0_wmod']


def kernel(**inputs):
    import numpy as _np
    import concourse.bacc as _bacc
    from concourse import mybir as _mybir
    from concourse.bass_utils import run_bass_kernel_spmd as _run

    nc = _bacc.Bacc("TRN2", target_bir_lowering=False, num_devices=1)
    arrays, args = {}, []
    for name in _INS:
        a = _np.ascontiguousarray(inputs[name])
        if a.ndim == 0:
            a = a.reshape(1, 1)
        arrays[f"in_{name}"] = a
        args.append(nc.dram_tensor(f"in_{name}", a.shape, _mybir.dt.from_np(a.dtype), kind="ExternalInput").ap())
    args.append(nc.dram_tensor("out_0", (B, S, D), F32, kind="ExternalOutput").ap())
    build(nc, *args)
    r = _run(nc, [arrays], core_ids=[0])
    return r.results[0]["out_0"]
```

```python
import numpy as np
import concourse.bass as bass
from concourse import mybir
from contextlib import ExitStack

F32 = mybir.dt.float32
F32R = mybir.dt.float32r
BF16 = mybir.dt.bfloat16
I32 = mybir.dt.int32
U32 = mybir.dt.uint32
ALU = mybir.AluOpType
ACT = mybir.ActivationFunctionType
AX = mybir.AxisListType

P = 128
B, S, D = 4, 1024, 128
H, HD = 16, 8
T = B * S
NT = T // P
TPB = S // P
MIN_W, MAX_W = 24, 120
HALO = 64
HG = 4
QB = 32
WIN = QB + 2 * HALO
KW = P + 2 * HALO
KBLK = KW // QB
GRP = 512
NG = T // GRP
BIG = 1e30
EPS = 1e-5
NE, TOPK, FF = 8, 2, 512
FC = FF // P
FT = 256
NF = T * TOPK // FT + NE - 1
SC = NF * FT // P
ISQ = 1.0 / float(np.sqrt(HD))


class Count:

    def __init__(self, sem, n, ring=2):
        self.sem, self.n, self.ring = sem, n, ring

    def open(self, eng):
        eng.sem_inc(self.sem, self.ring * self.n)

    def wait(self, eng, turn, u, k=None, back=0):
        k = self.n if k is None else k
        eng.wait_ge(self.sem, turn * (self.ring * self.n) + (self.n * (self.ring + u - back) + k))


class Flights:

    def __init__(self, sem, n):
        self.sem, self.n = sem, n

    def open(self, eng):
        eng.sem_inc(self.sem, 16)

    def wait(self, eng, turn, k=0):
        eng.wait_ge(self.sem, turn * (16 * self.n) + (16 + 16 * k))


def strided(ap, offset, dims):
    return bass.AP(tensor=ap.tensor, offset=ap.offset + offset, ap=[list(ap.ap[0])] + dims)


def tiles(eng, total, ring, ahead, step):
    turns = (total - ahead) // ring
    with eng.Fori(0, turns) as i:
        for u in range(ring):
            step(i, u, total)
    for j in range(turns * ring, total):
        step(j // ring, j % ring, total - 1 - j)


def later(i, u, n, ring):
    return i + (u + n) // ring, (u + n) % ring


def apart(eng):
    eng.nop(nofuse=True)


def bcast_row(rows, b, n):
    return rows[:, bass.ds(b, 1), :].broadcast_to([P, n, D])


def build(nc, x, alpha, Wq, bq, Wk, bk, Wv, bv, W_o, Wfc, bfc, rw1, rb1, rw2, rb2, W1, b1, W2, b2, c, wmod, out, stop=9):
    top = ExitStack()

    def sem(name):
        return top.enter_context(nc.semaphore(name))

    def sb(name, shape, dt=F32, ctx=top):
        return ctx.enter_context(nc.sbuf_tensor(name, shape, dt))

    def pb(ctx, name, shape, dt=F32):
        return ctx.enter_context(nc.psum_tensor(name, shape, dt))

    xf = x.rearrange("b s d -> (b s) d")
    of = out.rearrange("b s d -> (b s) d")

    with top:
        x_all = sb("x_all", [P, NT + 1, D])
        ident = sb("ident", [P, P])
        ga_bc = sb("ga_bc", [P, B + 1, D])
        gacv_bc = sb("gacv_bc", [P, B + 1, D])
        sb_bc = sb("sb_bc", [P, B, D])
        cb_bc = sb("cb_bc", [P, B, D])
        gb_bc = sb("gb_bc", [P, B, D])
        q_scr = nc.dram_tensor("q_scr", (4, QB, HG, T), F32, kind="Internal").ap()
        k_scr = nc.dram_tensor("k_scr", (4, QB, HG, T), F32, kind="Internal").ap()
        v_scr = nc.dram_tensor("v_scr", (T + 2 * HALO, D), F32, kind="Internal").ap()

        attn = ExitStack()
        kst = sb("kst", [P, HG, T + 2 * HALO], F32R, attn)
        wqs = sb("wqs", [P, D], F32, attn)
        wk_sb = sb("wk_sb", [P, D], F32, attn)
        wv_sb = sb("wv_sb", [P, D], F32, attn)
        wc = sb("wc", [P, D], F32, attn)
        bqs = sb("bqs", [P, 1], F32, attn)
        bk_sb = sb("bk_sb", [P, 1], F32, attn)
        sa_t = sb("sa_t", [P, B], F32, attn)
        ca_t = sb("ca_t", [P, B], F32, attn)
        rstd = sb("rstd", [P, NT], F32, attn)
        nmr = sb("nmr", [P, NT], F32, attn)
        identb = sb("identb", [P, P], BF16, attn)
        eqh = sb("eqh", [P, 4], F32, attn)
        eqg = sb("eqg", [P, 4], F32, attn)
        eqd = sb("eqd", [P, 4], F32, attn)
        eqq = sb("eqq", [P, 4], F32, attn)
        st_den = sb("st_den", [P, D], F32, attn)
        masks = sb("masks", [P, TPB, 4 * WIN], BF16, attn)

        with ExitStack() as one:
            s1 = lambda n, sh, dt=F32: sb(n, sh, dt, one)
            wq_sb = s1("wq_sb", [P, D])
            wfc_sb = s1("wfc_sb", [P, D])
            wo_sb = s1("wo_sb", [P, HD])
            bq_sb = s1("bq_sb", [P, 1])
            bv_sb = s1("bv_sb", [P, 1])
            bfc_bc = s1("bfc_bc", [P, D])
            cT = s1("cT", [P, B])
            silu = s1("silu", [P, B])
            tmp4 = s1("tmp4", [P, B])
            wmod_sb = s1("wmod_sb", [P, 6 * D])
            stats = s1("stats", [P, NT, 6])
            mv = s1("mv", [P, NT, 2])
            varr = s1("varr", [P, NT + 2])
            xl = s1("xl", [B, 2, D])
            statl = s1("statl", [B, 2, 6])
            mvl = s1("mvl", [B, 2, 2])
            nml = s1("nml", [B, 2])
            sac = s1("sac", [B, 2 * D])
            fl = s1("fl", [B, 2, D])
            flsum = s1("flsum", [B, 1])
            rcp = s1("rcp", [P, NT + 2])
            sc = s1("sc", [1, 16])
            sci = s1("sci", [1, 4], I32)
            ones_r = s1("ones_r", [B, P])
            half = s1("half", [P, 1])
            pint = s1("pint", [P, 1], I32)
            pbits = s1("pbits", [P, 6], I32)
            pf = s1("pf", [P, 6])
            ci = s1("ci", [P, WIN], I32)
            cf = s1("cf", [P, WIN])
            dist = s1("dist", [P, WIN])
            adist = s1("adist", [P, WIN])
            mint = s1("mint", [P, WIN], BF16)
            eq16 = s1("eq16", [P, H])
            bdo = s1("bdo", [P, D])
            bdoT = s1("bdoT", [P, D])
            sgn = s1("sgn", [P, B, D])
            zero_kv = s1("zero_kv", [P, HG * HALO])
            ps_row = [pb(one, f"ps_row{b}", [P, 512]) for b in range(B)]
            ps_col = pb(one, "ps_col", [P, 512])
            ps_a = pb(one, "ps_a", [P, 512])
            ps_b = pb(one, "ps_b", [P, 512])
            ps_h = pb(one, "ps_h", [P, 512])

            ld_al = sem("ld_al")
            ld_x, ld_w, ld_c, ld_f = sem("ld_x"), sem("ld_w"), sem("ld_c"), sem("ld_f")
            s_pad = sem("s_pad")
            p_cst = sem("p_cst")
            v1, a1, t1 = sem("v1"), sem("a1"), sem("t1")
            kv = [0]
            nv = {}
            block = one.enter_context(nc.Block())

            @block.vector
            def _(e):
                def step(name, ins):
                    kv[0] += 1
                    nv[name] = kv[0]
                    ins.then_inc(v1, 1)

                def own():
                    e.wait_ge(v1, kv[0])

                step("zero", e.memset(zero_kv[:, :], 0.0))
                e.wait_ge(a1, 1)
                e.wait_ge(ld_c, 32)
                step("silu1", e.tensor_scalar(tmp4[:, :], silu[:, :], 1.0, None, ALU.add))
                own()
                step("silu2", e.reciprocal(tmp4[:, :], tmp4[:, :]))
                own()
                e.wait_ge(p_cst, 4)
                step("silu3", e.tensor_tensor(silu[:, :], cT[:, :], tmp4[:, :], ALU.mult))
                for k, (sh, msk) in enumerate(((5, 3), (2, 7), (0, 3), (3, 15), (0, 31), (3, 3))):
                    step(f"pb{k}", e.tensor_scalar(pbits[:, k:k + 1], pint[:, :], sh, msk, ALU.logical_shift_right, ALU.bitwise_and))
                own()
                step("pf", e.tensor_copy(pf[:, :], pbits[:, :]))
                step("cf", e.tensor_copy(cf[:, :], ci[:, :]))
                own()
                step("eqh", e.tensor_scalar(eqh[:, :], cf[:, 0:4], pf[:, 0:1], None, ALU.is_equal))
                step("eqg", e.tensor_scalar(eqg[:, :], cf[:, 0:4], pf[:, 1:2], None, ALU.is_equal))
                step("eqq", e.tensor_scalar(eqq[:, :], cf[:, 0:4], pf[:, 2:3], None, ALU.is_equal))
                step("eqd", e.tensor_scalar(eqd[:, :], cf[:, 0:4], pf[:, 5:6], None, ALU.is_equal))
                step("eq16", e.tensor_scalar(eq16[:, :], cf[:, 0:H], pf[:, 3:4], None, ALU.is_equal))
                own()
                step("st", e.tensor_tensor(st_den[:, :].rearrange("p (g h d) -> p g h d", g=4, h=4),
                                           strided(eqh[:, :], 0, [[0, 4], [1, 4], [0, 8]]),
                                           strided(eqg[:, :], 0, [[1, 4], [0, 4], [0, 8]]), ALU.mult))
                e.wait_ge(ld_w, 16 * 9)
                step("bdo", e.tensor_tensor(bdo[:, :].rearrange("p (h k) -> p h k", h=H),
                                            strided(wo_sb[:, :], 0, [[0, H], [1, HD]]),
                                            strided(eq16[:, :], 0, [[1, H], [0, HD]]), ALU.mult))
                step("identb", e.tensor_copy(identb[:, :], ident[:, :]))
                step("ones", e.memset(ones_r[:, :], 1.0))
                e.wait_ge(t1, 1)
                step("bdoT", e.tensor_copy(bdoT[:, :], ps_a[:, 0:D]))
                e.wait_ge(t1, 2)
                step("modT1", e.tensor_copy(sa_t[:, :], ps_col[:, 0:B]))
                step("modT2", e.tensor_scalar(ca_t[:, :], ps_col[:, B:2 * B], 1.0, None, ALU.add))
                step("wqs", e.tensor_scalar(wqs[:, :], wq_sb[:, :], -ISQ, None, ALU.mult))
                step("bqs", e.tensor_scalar(bqs[:, :], bq_sb[:, :], -ISQ, None, ALU.mult))
                e.wait_ge(ld_x, 16 * B)
                e.wait_ge(ld_f, 32)
                for n in range(NT):
                    step("_s", e.bn_stats(stats[:, n, :], x_all[:, n + 1, :]))
                for k in range(2):
                    step("_s", e.bn_stats(statl[:, k, :], xl[:, k, :]))
                own()
                for k in range(2):
                    step("_a", e.bn_aggr(mvl[:, k, :], statl[:, k, :]))
                for n in range(NT):
                    step("_a", e.bn_aggr(mv[:, n, :], stats[:, n, :]))
                own()
                step("_v", e.memset(varr[:, NT:], 1.0))
                own()
                step("_v", e.tensor_scalar(varr[0:B, NT:], mvl[:, :, 1], EPS, None, ALU.add))
                step("var", e.tensor_scalar(varr[:, 0:NT], mv[:, :, 1], EPS, None, ALU.add))
                e.wait_ge(a1, 3)
                step("_r", e.reciprocal(rcp[:, :], varr[:, :]))
                own()
                step("_r", e.tensor_copy(rstd[:, :], rcp[:, 0:NT]))
                step("_r", e.scalar_tensor_tensor(out=nmr[:, :], in0=mv[:, :, 0], scalar=-1.0, in1=rcp[:, 0:NT], op0=ALU.mult, op1=ALU.mult))
                step("_r", e.scalar_tensor_tensor(out=nml[:, :], in0=mvl[:, :, 0], scalar=-1.0, in1=rcp[0:B, NT:], op0=ALU.mult, op1=ALU.mult))
                step("_r", e.tensor_copy(sac[:, 0:D], ps_h[0:B, 0:D]))
                step("_r", e.tensor_scalar(sac[:, D:], ps_h[0:B, D:2 * D], 1.0, None, ALU.add))
                own()
                for k in range(2):
                    step("_f", e.tensor_scalar(xl[:, k, :], xl[:, k, :], rcp[0:B, NT + k:NT + k + 1], nml[:, k:k + 1], ALU.mult, ALU.add))
                    own()
                    step("_f", e.tensor_tensor(xl[:, k, :], xl[:, k, :], sac[:, D:], ALU.mult))
                    own()
                    step("_f", e.tensor_tensor(xl[:, k, :], xl[:, k, :], sac[:, 0:D], ALU.add))
                    own()
                step("fd", e.tensor_tensor(fl[:, 0, :], xl[:, 0, :], xl[:, 1, :], ALU.subtract))
                own()
                step("fa", e.scalar_tensor_tensor(out=fl[:, 1, :], in0=fl[:, 0, :], scalar=-1.0, in1=fl[:, 0, :], op0=ALU.mult, op1=ALU.max))
                own()
                step("fs", e.tensor_reduce(flsum[:, :], fl[:, 1, :], AX.X, ALU.add))
                e.wait_ge(t1, 3)
                step("fs2", e.tensor_copy(sc[:, 1:2], ps_b[0:1, 256:257]))
                e.wait_ge(a1, 2)
                step("al1", e.tensor_scalar(sc[:, 3:4], sc[:, 2:3], 1.0, None, ALU.add))
                own()
                step("al2", e.reciprocal(sc[:, 4:5], sc[:, 3:4]))
                own()
                step("al3", e.tensor_scalar(sc[:, 5:6], sc[:, 4:5], -1.0, 1.0, ALU.mult, ALU.add))
                own()
                step("al4", e.tensor_tensor(sc[:, 6:7], sc[:, 5:6], fl[0:1, 1, 0:1], ALU.mult))
                step("al5", e.tensor_scalar(sc[:, 7:8], sc[:, 1:2], 1.0 / (B * D), None, ALU.mult))
                own()
                step("fm", e.tensor_tensor(sc[:, 7:8], sc[:, 7:8], sc[:, 4:5], ALU.mult))
                own()
                step("sg", e.tensor_tensor(sc[:, 8:9], sc[:, 7:8], sc[:, 6:7], ALU.add))
                e.wait_ge(a1, 4)
                step("sg1", e.tensor_scalar(sc[:, 10:11], sc[:, 9:10], 1.0, None, ALU.add))
                own()
                step("sg2", e.reciprocal(sc[:, 11:12], sc[:, 10:11]))
                own()

                def floor(name, val, dst, k):
                    step(name + "1", e.tensor_copy(sci[:, k:k + 1], val))
                    own()
                    step(name + "2", e.tensor_copy(dst, sci[:, k:k + 1]))
                    own()
                    step(name + "3", e.tensor_tensor(sc[:, 15:16], dst, val, ALU.is_gt))
                    own()
                    step(name + "4", e.tensor_tensor(dst, dst, sc[:, 15:16], ALU.subtract))
                    own()

                step("w0", e.tensor_scalar(sc[:, 12:13], sc[:, 11:12], float(MAX_W - MIN_W), float(MIN_W), ALU.mult, ALU.add))
                own()
                floor("w", sc[:, 12:13], sc[:, 13:14], 0)
                step("h1", e.tensor_scalar(sc[:, 14:15], sc[:, 13:14], 0.5, None, ALU.mult))
                own()
                step("h2", e.tensor_copy(sci[:, 1:2], sc[:, 14:15]))
                own()
                step("h3", e.tensor_copy(sc[:, 12:13], sci[:, 1:2]))
                own()
                step("h4", e.tensor_tensor(sc[:, 15:16], sc[:, 12:13], sc[:, 14:15], ALU.is_gt))
                own()
                step("h5", e.tensor_tensor(sc[:, 12:13], sc[:, 12:13], sc[:, 15:16], ALU.subtract))
                e.wait_ge(t1, 4)
                step("half", e.tensor_copy(half[:, :], ps_h[:, 256:257]))
                e.wait_ge(t1, 5)
                step("wc", e.tensor_copy(wc[:, :], ps_b[:, 0:D]))
                own()
                step("dist", e.tensor_scalar(dist[:, :], cf[:, :], pf[:, 4:5], float(HALO), ALU.subtract, ALU.subtract))
                own()
                step("adist", e.scalar_tensor_tensor(out=adist[:, :], in0=dist[:, :], scalar=-1.0, in1=dist[:, :], op0=ALU.mult, op1=ALU.max))
                own()
                step("mint", e.tensor_scalar(mint[:, :], adist[:, :], half[:, 0:1], BIG, ALU.is_gt, ALU.mult))
                own()
                step("_m", e.tensor_copy(masks[:, :, :].rearrange("p t (q w) -> p (t q) w", q=4),
                                         strided(mint[:, :], 0, [[0, TPB * 4], [1, WIN]])))
                own()
                for q in range(HALO // QB):
                    step("_e", e.memset(masks[:, 0, q * WIN:q * WIN + HALO - q * QB], BIG))
                    qq = 3 - q
                    step("_e", e.memset(masks[:, TPB - 1, (qq + 1) * WIN - HALO + q * QB:(qq + 1) * WIN], BIG))
                e.wait_ge(t1, 6)
                for b in range(B):
                    r = ps_row[b]
                    step("_g", e.tensor_scalar(sgn[:, b, :], r[:, 0:D], 0.0, 0.5, ALU.is_ge, ALU.subtract))
                    step("_b", e.tensor_copy(sb_bc[:, b, :], r[:, D:2 * D]))
                    step("_b", e.tensor_scalar(cb_bc[:, b, :], r[:, 2 * D:3 * D], 1.0, None, ALU.add))
                    own()
                    step("_b", e.tensor_tensor(ga_bc[:, b + 1, :], r[:, 0:D], sgn[:, b, :], ALU.mult))
                    own()
                    step("_b", e.tensor_scalar(ga_bc[:, b + 1, :], ga_bc[:, b + 1, :], 0.125, 4.0, ALU.max, ALU.mult))
                    own()
                    step("_b", e.tensor_tensor(ga_bc[:, b + 1, :], ga_bc[:, b + 1, :], sgn[:, b, :], ALU.mult))
                    own()
                    step("_g", e.tensor_scalar(sgn[:, b, :], r[:, 3 * D:4 * D], 0.0, 0.5, ALU.is_ge, ALU.subtract))
                    own()
                    step("_b", e.tensor_tensor(gb_bc[:, b, :], r[:, 3 * D:4 * D], sgn[:, b, :], ALU.mult))
                    own()
                    step("_b", e.tensor_scalar(gb_bc[:, b, :], gb_bc[:, b, :], 0.125, 4.0, ALU.max, ALU.mult))
                    own()
                    step("_b", e.tensor_tensor(gb_bc[:, b, :], gb_bc[:, b, :], sgn[:, b, :], ALU.mult))
                    own()
                step("_c", e.tensor_copy(ga_bc[:, 0, :], ga_bc[:, 1, :]))
                step("_c", e.tensor_tensor(bfc_bc[:, :], bfc_bc[:, :], ps_a[:, 0:D], ALU.add))
                own()
                step("_c", e.tensor_tensor(gacv_bc[:, :, :], ga_bc[:, :, :], strided(bfc_bc[:, :], 0, [[0, B + 1], [1, D]]), ALU.mult))

            @block.sync
            def _(e):
                with nc.allow_non_contiguous_dma(reason="four values a partition"):
                    e.dma_start(cT[:, :], c.rearrange("b d -> d b")).then_inc(ld_c, 16)
                e.dma_start(wmod_sb[:, :], wmod).then_inc(ld_c, 16)
                e.dma_start(xl[:, 0, :], x[:, S - 1, :]).then_inc(ld_f, 16)
                e.dma_start(xl[:, 1, :], x[:, S - 2, :]).then_inc(ld_f, 16)
                e.dma_start(sc[0:1, 0:1], alpha).then_inc(ld_al, 16)
                for b in range(B):
                    e.dma_start(x_all[:, 1 + b * TPB:1 + (b + 1) * TPB, :],
                                xf[b * S:(b + 1) * S, :].rearrange("(n p) d -> p n d", p=P)).then_inc(ld_x, 16)
                for dst, src in ((wq_sb, Wq), (wk_sb, Wk), (wv_sb, Wv), (wfc_sb, Wfc)):
                    e.dma_start(dst[:, :], src).then_inc(ld_w, 16)
                e.dma_start(wo_sb[:, :], W_o.rearrange("h d k -> (h d) k")).then_inc(ld_w, 16)
                for dst, src in ((bq_sb, bq), (bk_sb, bk), (bv_sb, bv)):
                    e.dma_start(dst[:, :], src.rearrange("(d a) -> d a", a=1)).then_inc(ld_w, 16)
                e.dma_start(bfc_bc[:, :], bfc.rearrange("(a d) -> a d", a=1).broadcast_to([P, D])).then_inc(ld_w, 16)
                e.wait_ge(v1, nv["zero"])
                e.dma_start(kst[:, :, 0:HALO].bitcast(F32), zero_kv[:, :].rearrange("p (g t) -> p g t", g=HG)).then_inc(s_pad, 16)
                e.dma_start(kst[:, :, HALO + T:].bitcast(F32), zero_kv[:, :].rearrange("p (g t) -> p g t", g=HG)).then_inc(s_pad, 16)
                e.dma_start(v_scr[0:HALO, :], zero_kv[0:HALO, 0:D]).then_inc(s_pad, 16)
                e.dma_start(v_scr[HALO + T:, :], zero_kv[0:HALO, 0:D]).then_inc(s_pad, 16)
                e.wait_ge(s_pad, 64)

            @block.gpsimd
            def _(e):
                e.memset(x_all[:, 0, :], 0.0)
                e.memset(ident[:, :], 0.0).then_inc(p_cst, 1)
                e.iota(pint[:, :], [[0, 1]], 0, 1).then_inc(p_cst, 1)
                e.iota(ci[:, :], [[1, WIN]], 0, 0).then_inc(p_cst, 1)
                e.wait_ge(p_cst, 1)
                e.affine_select(out=ident[:, :], in_=ident[:, :], compare_op=ALU.not_equal, fill=1.0,
                                base=0, pattern=[[-1, P]], channel_multiplier=1).then_inc(p_cst, 1)

            @block.scalar
            def _(e):
                e.wait_ge(ld_c, 32)
                e.activation(silu[:, :], cT[:, :], ACT.Exp, scale=-1.0).then_inc(a1, 1)
                e.wait_ge(ld_al, 16)
                e.activation(sc[:, 2:3], sc[:, 0:1], ACT.Exp, scale=-1.0).then_inc(a1, 1)
                e.wait_ge(v1, nv["var"])
                e.activation(varr[:, :], varr[:, :], ACT.Sqrt).then_inc(a1, 1)
                e.wait_ge(v1, nv["sg"])
                e.activation(sc[:, 9:10], sc[:, 8:9], ACT.Exp, scale=-1.0).then_inc(a1, 1)

            @block.tensor
            def _(e):
                e.wait_ge(v1, nv["bdo"])
                e.wait_ge(p_cst, 4)
                e.transpose(ps_a[:, 0:D], bdo[:, :], ident[:, :]).then_inc(t1, 1)
                e.wait_ge(v1, nv["silu3"])
                for j in range(2):
                    e.matmul(ps_col[:, j * B:(j + 1) * B], wmod_sb[:, j * D:(j + 1) * D], silu[:, :], start=True, stop=True)
                e.matmul(ps_h[0:B, 0:2 * D], silu[:, :], wmod_sb[:, 0:2 * D], start=True, stop=True).then_inc(t1, 1)
                e.wait_ge(v1, nv["fs"])
                e.matmul(ps_b[0:1, 256:257], flsum[:, :], ones_r[0:B, 0:1], start=True, stop=True).then_inc(t1, 1)
                e.wait_ge(v1, nv["h5"])
                e.matmul(ps_h[:, 256:257], ones_r[0:1, :], sc[0:1, 12:13], start=True, stop=True).then_inc(t1, 1)
                e.wait_ge(v1, nv["bdoT"])
                e.matmul(ps_b[:, 0:D], bdoT[:, :], wfc_sb[:, :], start=True, stop=True).then_inc(t1, 1)
                for b in range(B):
                    e.matmul(ps_row[b][:, :], strided(silu[:, b:b + 1], 0, [[0, P]]), wmod_sb[:, 2 * D:6 * D], start=True, stop=True)
                e.wait_ge(v1, nv["wc"])
                e.matmul(ps_a[:, 0:D], strided(bv_sb[:, 0:1], 0, [[0, P]]), wc[:, :], start=True, stop=True).then_inc(t1, 1)

        with ExitStack() as two:
            hn = [sb(f"hn{u}", [P, 4, D], F32, two) for u in range(2)]
            hT = [sb(f"hT{u}", [P, GRP], F32, two) for u in range(2)]
            khi = [sb(f"khi{u}", [P, GRP], F32R, two) for u in range(2)]
            klo = [sb(f"klo{u}", [P, GRP], F32R, two) for u in range(2)]
            qhi = [sb(f"qhi{u}", [P, GRP], F32R, two) for u in range(2)]
            qlo = [sb(f"qlo{u}", [P, GRP], F32R, two) for u in range(2)]
            vn = [sb(f"vn{u}", [P, 4, D], F32, two) for u in range(2)]
            pT = [pb(two, f"pT{u}", [P, GRP]) for u in range(2)]
            pK = [pb(two, f"pK{u}", [P, GRP]) for u in range(2)]
            pQ = [pb(two, f"pQ{u}", [P, GRP]) for u in range(2)]
            pV = [pb(two, f"pV{u}", [P, GRP]) for u in range(2)]
            v_hn = Count(sem("v_hn"), 4)
            t_tr = Count(sem("t_tr"), 1)
            a_hT = Count(sem("a_hT"), 1)
            t_kqv = Count(sem("t_kqv"), 3)
            a_kqv = Count(sem("a_kqv"), 3)
            v_lo = Count(sem("v_lo"), 2)
            d_st = [Flights(sem(f"d_st{u}"), 4 + 1) for u in range(2)]
            d_k = [Flights(sem(f"d_k{u}"), 4) for u in range(2)]
            d_kst = sem("d_kst")
            block = two.enter_context(nc.Block())

            @block.vector
            def _(e):
                v_hn.open(e)
                v_lo.open(e)
                with e.Fori(0, NG // 2) as i:
                    for u in range(2):
                        t_tr.wait(e, i, u, back=2)
                        for n in range(4):
                            g = i * 8 + (4 * u + n)
                            e.tensor_scalar(hn[u][:, n, :], x_all[:, bass.ds(g + 1, 1), :].rearrange("p a d -> p (a d)"),
                                            rstd[:, bass.ds(g, 1)], nmr[:, bass.ds(g, 1)], ALU.mult, ALU.add).then_inc(v_hn.sem, 1)
                        d_st[u].wait(e, i)
                        d_k[u].wait(e, i)
                        a_kqv.wait(e, i, u, 1)
                        e.scalar_tensor_tensor(out=klo[u][:, :], in0=pK[u][:, :], scalar=bk_sb[:, 0:1],
                                               in1=khi[u][:, :].bitcast(F32), op0=ALU.add, op1=ALU.subtract).then_inc(v_lo.sem, 1)
                        a_kqv.wait(e, i, u, 2)
                        e.scalar_tensor_tensor(out=qlo[u][:, :], in0=pQ[u][:, :], scalar=bqs[:, 0:1],
                                               in1=qhi[u][:, :].bitcast(F32), op0=ALU.add, op1=ALU.subtract).then_inc(v_lo.sem, 1)

            @block.scalar
            def _(e):
                a_hT.open(e)
                a_kqv.open(e)
                with e.Fori(0, NG // 2) as i:
                    for u in range(2):
                        t_tr.wait(e, i, u)
                        t_kqv.wait(e, i, u, back=2)
                        apart(e)
                        e.activation(hT[u][:, :], pT[u][:, :], ACT.Identity, bias=sa_t[:, bass.ds(i, 1)],
                                     scale=ca_t[:, bass.ds(i, 1)]).then_inc(a_hT.sem, 1)
                        d_st[u].wait(e, i)
                        d_k[u].wait(e, i)
                        v_lo.wait(e, i, u, back=2)
                        t_kqv.wait(e, i, u, 1)
                        e.activation(khi[u][:, :], pK[u][:, :], ACT.Identity, bias=bk_sb[:, 0:1]).then_inc(a_kqv.sem, 1)
                        t_kqv.wait(e, i, u, 2)
                        e.activation(qhi[u][:, :], pQ[u][:, :], ACT.Identity, bias=bqs[:, 0:1]).then_inc(a_kqv.sem, 1)
                        t_kqv.wait(e, i, u, 3)
                        e.activation(vn[u][:, :, :], pV[u][:, :].rearrange("p (n d) -> p n d", n=4), ACT.Copy).then_inc(a_kqv.sem, 1)

            @block.tensor
            def _(e):
                t_tr.open(e)
                t_kqv.open(e)
                with e.Fori(0, NG // 2) as i:
                    for u in range(2):
                        a_hT.wait(e, i, u, back=2)
                        for n in range(4):
                            v_hn.wait(e, i, u, n + 1)
                            mm = e.transpose(pT[u][:, n * P:(n + 1) * P], hn[u][:, n, :], ident[:, :])
                        mm.then_inc(t_tr.sem, 1)
                        a_hT.wait(e, i, u)
                        v_lo.wait(e, i, u, back=2)
                        a_kqv.wait(e, i, u, back=2)
                        e.matmul(pK[u][:, :], wk_sb[:, :], hT[u][:, :], start=True, stop=True).then_inc(t_kqv.sem, 1)
                        e.matmul(pQ[u][:, :], wqs[:, :], hT[u][:, :], start=True, stop=True).then_inc(t_kqv.sem, 1)
                        for n in range(4):
                            mm = e.matmul(pV[u][:, n * P:(n + 1) * P], hT[u][:, n * P:(n + 1) * P], wv_sb[:, :], start=True, stop=True)
                        mm.then_inc(t_kqv.sem, 1)

            @block.sync
            def _(e):
                for f in (*d_st, *d_k):
                    f.open(e)
                with e.Fori(0, NG // 2) as i:
                    for u in range(2):
                        tok = i * (2 * GRP) + u * GRP
                        v_lo.wait(e, i, u, 1)
                        for k, part in enumerate((khi, klo, khi, klo)):
                            e.dma_start(k_scr[k, :, :, bass.ds(tok, GRP)].rearrange("r g t -> g r t"), part[u][:, :].bitcast(F32)).then_inc(d_k[u].sem, 16)
                        v_lo.wait(e, i, u, 2)
                        for k, part in enumerate((qhi, qhi, qlo, qlo)):
                            e.dma_start(q_scr[k, :, :, bass.ds(tok, GRP)].rearrange("r g t -> g r t"), part[u][:, :].bitcast(F32)).then_inc(d_st[u].sem, 16)
                        a_kqv.wait(e, i, u, 3)
                        e.dma_start(v_scr[bass.ds(tok + HALO, GRP), :].rearrange("(n p) d -> p n d", p=P), vn[u][:, :, :]).then_inc(d_st[u].sem, 16)
                        d_k[u].wait(e, i + 1)
                        e.dma_start(kst[:, :, bass.ds(tok + HALO, GRP)].bitcast(F32),
                                    k_scr[:, :, :, bass.ds(tok, GRP)].rearrange("k r g t -> (k r) g t")).then_inc(d_kst, 16)
                for u in range(2):
                    d_st[u].wait(e, NG // 2)
                e.wait_ge(d_kst, 16 * NG)

        with ExitStack() as three:
            qbd = [sb(f"qbd{u}", [P, HG, 4, 4 * QB], F32R, three) for u in range(2)]
            qst = [sb(f"qst{u}", [P, HG, P], F32, three) for u in range(2)]
            vrep = [sb(f"vrep{u}", [P, KBLK, D], F32, three) for u in range(2)]
            vbd = [sb(f"vbd{u}", [P, KBLK, D], F32, three) for u in range(2)]
            pr = sb("pr", [P, HG, 4 * WIN], F32, three)
            prT = [sb(f"prT{u}", [P, HG, 4 * WIN], F32, three) for u in range(2)]
            nmax = sb("nmax", [P, 4 * HG], F32, three)
            rs = [sb(f"rs{u}", [P, 32], F32, three) for u in range(2)]
            rsT = sb("rsT", [P, 32], F32, three)
            rden = sb("rden", [P, 32], F32, three)
            mvd = sb("mvd", [P, 4, 32], F32, three)
            rbc = sb("rbc", [P, P], F32, three)
            oT = sb("oT", [P, P], F32, three)
            xg = sb("xg", [P, D], F32, three)
            xa = sb("xa", [P, D], F32, three)
            pS = [pb(three, f"pS{k}", [P, 1024]) for k in range(2)]
            pO = [pb(three, f"pO{u}", [P, 512]) for u in range(2)]
            pR = pb(three, "pR", [P, 512])
            pF = pb(three, "pF", [P, 512])
            t_s = Count(sem("t_s"), 4)
            v_mx = Count(sem("v_mx"), 4)
            a_e = Count(sem("a_e"), 16)
            v_tr = Count(sem("v_tr"), 4)
            v_den = Count(sem("v_den"), 3)
            p_vb = Count(sem("p_vb"), 1)
            p_qb = Count(sem("p_qb"), 1)
            t_o = Count(sem("t_o"), 1)
            t_r = Count(sem("t_r"), 1)
            a_r = Count(sem("a_r"), 1)
            v_o = Count(sem("v_o"), 1)
            t_f = Count(sem("t_f"), 1)
            v_x = Count(sem("v_x"), 1)
            p_x = Count(sem("p_x"), 2)
            s_z = sem("s_z")
            s_zp = sem("s_zp")
            d_q = [sem(f"d_q{u}") for u in range(2)]
            d_v = [sem(f"d_v{u}") for u in range(2)]
            block = three.enter_context(nc.Block())
            NI = NT // 2

            @block.sync
            def _(e):
                with e.Fori(0, NI) as i:
                    for u in range(2):
                        tok = i * (2 * P) + u * P
                        p_qb.wait(e, i, u, back=2)
                        e.dma_start(qst[u][:, :, :], q_scr[:, :, :, bass.ds(tok, P)].rearrange("k r g t -> (k r) g t")).then_inc(d_q[u], 16)
                        p_vb.wait(e, i, u, back=2)
                        for r in range(4):
                            src = v_scr[bass.ds(tok, KW), :].rearrange("(n k) d -> k n d", k=QB)
                            e.dma_start(vrep[u][32 * r:32 * r + 32, :, :], src).then_inc(d_v[u], 16)
                p_qb.wait(e, NI, 0, back=2)
                e.dma_start(qst[0][:, :, :], q_scr[:, :, :, 0:P].rearrange("k r g t -> (k r) g t")).then_inc(d_q[0], 16)

            @block.gpsimd
            def _(e):
                p_vb.open(e)
                p_x.open(e)
                p_qb.open(e)
                e.memset(vbd[1][:, :, :], 0.0).then_inc(s_zp, 1)

                def queries(i, u):
                    e.wait_ge(d_q[u], i * 16 + 16)
                    t_s.wait(e, i, u, back=2)
                    p_qb.wait(e, i, u, back=1)
                    e.tensor_tensor(qbd[u][:, :, :, :].rearrange("p g q (h t) -> p (g q) h t", h=4),
                                    strided(qst[u][:, :, :], 0, [[QB, 4 * HG], [0, 4], [1, QB]]),
                                    strided(eqd[:, :], 0, [[0, 4 * HG], [1, 4], [0, QB]]), ALU.mult).then_inc(p_qb.sem, 1)

                def residual(i, u):
                    g = i * 2 + u
                    sl = x_all[:, bass.ds(g, 1), :].rearrange("p a d -> p (a d)")
                    b = (g + (TPB - 1)) // TPB
                    p_x.wait(e, i, u, back=1)
                    apart(e)
                    e.tensor_tensor(xg[:, :], sl, gacv_bc[:, bass.ds(b, 1), :].rearrange("p a d -> p (a d)"), ALU.add).then_inc(p_x.sem, 1)
                    p_x.wait(e, i, u, 1)
                    v_x.wait(e, i, u)
                    apart(e)
                    e.tensor_tensor(sl, xg[:, :], xa[:, :], ALU.add).then_inc(p_x.sem, 1)

                queries(0, 0)
                with e.Fori(0, NI) as i:
                    for u in range(2):
                        e.wait_ge(d_v[u], i * 64 + 64)
                        t_o.wait(e, i, u, back=1)
                        e.tensor_tensor(vbd[u][:, :, :].rearrange("p n (g h d) -> p (n g) h d", g=HG, h=4),
                                        vrep[u][:, :, :].rearrange("p n (g h d) -> p (n g) h d", g=HG, h=4),
                                        strided(eqh[:, :], 0, [[0, KBLK * HG], [1, 4], [0, HD]]), ALU.mult).then_inc(p_vb.sem, 1)
                        queries(i + u, 1 - u)
                        residual(i, u)
                residual(NI, 0)
                p_x.wait(e, NI, 0)

            @block.scalar
            def _(e):
                a_e.open(e)
                a_r.open(e)
                with e.Fori(0, NI) as i:
                    for u in range(2):
                        for hg in range(HG):
                            v_mx.wait(e, i, u, hg + 1)
                            v_tr.wait(e, i, u, hg + 1, back=1)
                            if hg == 0:
                                v_den.wait(e, i, u, back=1)
                            for q in range(4):
                                k = 4 * hg + q
                                e.activation(pr[:, hg, q * WIN:(q + 1) * WIN], pS[hg % 2][:, q * (KW + QB):q * (KW + QB) + WIN], ACT.Exp,
                                             bias=nmax[:, k:k + 1], scale=-1.0, accum_out=rs[u][:, k:k + 1]).then_inc(a_e.sem, 1)
                            if hg == 1:
                                t_r.wait(e, i, u)
                                v_o.wait(e, i, u, back=1)
                                e.activation(rbc[:, :], pR[:, 0:P], ACT.Copy).then_inc(a_r.sem, 1)
                t_r.wait(e, NI, 0)
                v_o.wait(e, NI, 0, back=1)
                e.activation(rbc[:, :], pR[:, 0:P], ACT.Copy).then_inc(a_r.sem, 1)

            @block.tensor
            def _(e):
                t_s.open(e)
                t_o.open(e)
                t_r.open(e)
                t_f.open(e)
                e.wait_ge(s_z, 1)
                e.wait_ge(s_zp, 1)

                def scores(i, u, hg):
                    if hg >= 2:
                        a_e.wait(e, i, u, 4 * (hg - 1))
                    else:
                        a_e.wait(e, i, u, 4 * (hg + 3), back=1)
                    tok = i * (2 * P) + u * P
                    for q in range(4):
                        e.matmul(pS[hg % 2][:, q * KW:(q + 1) * KW], qbd[u][:, hg, q, :],
                                 kst[:, hg, bass.ds(tok, KW)], start=q % 2 == 0, stop=False, skip_group_check=True)
                        if q % 2:
                            m = (i * 2 + u) % TPB
                            mm = e.matmul(strided(pS[hg % 2][:, 0:1], (q - 1) * (KW + QB), [[KW + QB, 2], [1, WIN]]), identb[:, :],
                                          masks[:, bass.ds(m, 1), (q - 1) * WIN:(q + 1) * WIN].rearrange("p a w -> p (a w)"),
                                          start=False, stop=True, skip_group_check=True)
                    mm.then_inc(t_s.sem, 1)

                def weighted(i, u):
                    w = 1 - u
                    v_tr.wait(e, i, u, back=1)
                    p_vb.wait(e, i, u, back=1)
                    v_o.wait(e, i, u, back=2)
                    for j in range(KBLK):
                        lo, hi = max(0, j - 4), min(3, j)
                        for hg in range(HG):
                            mm = e.matmul(pO[w][32 * hg:32 * hg + 32, lo * QB:(hi + 1) * QB], vbd[w][:, j, 32 * hg:32 * hg + 32],
                                          strided(prT[w][:, hg, 0:1], j * QB + lo * (WIN - QB), [[WIN - QB, hi - lo + 1], [1, QB]]),
                                          start=j == 0, stop=j == KBLK - 1, skip_group_check=True)
                    mm.then_inc(t_o.sem, 1)

                def spread(i, u):
                    v_den.wait(e, i, u)
                    a_r.wait(e, i, u, back=1)
                    e.matmul(pR[:, 0:P], st_den[:, :], mvd[:, :, :].rearrange("p q t -> p (q t)"), start=True, stop=True).then_inc(t_r.sem, 1)

                def project(i, u):
                    v_o.wait(e, i, u)
                    v_x.wait(e, i, u, back=1)
                    e.matmul(pF[:, 0:D], oT[:, :], wc[:, :], start=True, stop=True).then_inc(t_f.sem, 1)

                with e.Fori(0, NI) as i:
                    for u in range(2):
                        p_qb.wait(e, i, u)
                        scores(i, u, 0)
                        scores(i, u, 1)
                        weighted(i, u)
                        scores(i, u, 2)
                        spread(i, u)
                        scores(i, u, 3)
                        project(i, u)
                weighted(NI, 0)
                spread(NI, 0)
                project(NI, 0)

            @block.vector
            def _(e):
                for cnt in (v_mx, v_tr, v_den, v_o, v_x):
                    cnt.open(e)
                for w in range(2):
                    e.memset(rs[w][:, :], 1.0)
                e.memset(prT[1][:, :, :], 0.0).then_inc(s_z, 1)
                e.wait_ge(s_z, 1)

                def maxima(i, u, hg):
                    t_s.wait(e, i, u, hg + 1)
                    a_e.wait(e, i, u, 4 * hg + 4, back=1)
                    e.tensor_reduce(nmax[:, 4 * hg:4 * hg + 4], strided(pS[hg % 2][:, 0:1], 0, [[KW + QB, 4], [1, WIN]]),
                                    AX.X, ALU.min).then_inc(v_mx.sem, 1)

                def turn(i, u, hg):
                    a_e.wait(e, i, u, 4 * hg + 4)
                    if hg == 0:
                        t_o.wait(e, i, u, back=1)
                    e.transpose(prT[u][:, hg, :], pr[:, hg, :]).then_inc(v_tr.sem, 1)

                def denominators(i, u):
                    w = 1 - u
                    a_e.wait(e, i, u, back=1)
                    v_den.wait(e, i, u, 2, back=1)
                    e.transpose(rsT[:, :], rs[w][:, :]).then_inc(v_den.sem, 1)
                    v_den.wait(e, i, u, 1)
                    e.reciprocal(rden[:, :], rsT[:, :]).then_inc(v_den.sem, 1)
                    v_den.wait(e, i, u, 2)
                    t_r.wait(e, i, u, back=1)
                    e.tensor_tensor(mvd[:, :, :], strided(rden[:, :], 0, [[0, 4], [1, 32]]),
                                    strided(eqq[:, :], 0, [[1, 4], [0, 32]]), ALU.mult).then_inc(v_den.sem, 1)

                def normalise(i, u):
                    a_r.wait(e, i, u)
                    t_o.wait(e, i, u)
                    t_f.wait(e, i, u, back=1)
                    e.tensor_tensor(oT[:, :], pO[1 - u][:, 0:P], rbc[:, :], ALU.mult).then_inc(v_o.sem, 1)

                def scaled(i, u):
                    g = i * 2 + u
                    b = (g + (TPB - 1)) // TPB
                    t_f.wait(e, i, u)
                    p_x.wait(e, i, u, back=1)
                    e.tensor_tensor(xa[:, :], pF[:, 0:D], ga_bc[:, bass.ds(b, 1), :].rearrange("p a d -> p (a d)"), ALU.mult).then_inc(v_x.sem, 1)

                with e.Fori(0, NI) as i:
                    for u in range(2):
                        maxima(i, u, 0)
                        denominators(i, u)
                        maxima(i, u, 1)
                        turn(i, u, 0)
                        maxima(i, u, 2)
                        normalise(i, u)
                        turn(i, u, 1)
                        maxima(i, u, 3)
                        scaled(i, u)
                        turn(i, u, 2)
                        turn(i, u, 3)
                denominators(NI, 0)
                normalise(NI, 0)
                scaled(NI, 0)

        attn.close()

        gates = sb("gates", [P, 2, NT])
        gidx = sb("gidx", [P, 2 * (NF)], I32)
        sidx = sb("sidx", [P, 2 * (NF)], I32)
        eid = sb("eid", [1, NF], I32)
        h_scr = nc.dram_tensor("h_scr", (T, D), F32, kind="Internal").ap()
        w1_all = sb("w1_all", [P, NE * FF])
        w2_all = sb("w2_all", [P, NE * FC * D])
        b1_all = sb("b1_all", [P, NE * FC])
        b2_all = sb("b2_all", [P, NE, D])
        d_wt = sem("d_wt")
        N_WT = 6
        y_scr = nc.dram_tensor("y_scr", (2 * T + NF * FT + 3, D), F32, kind="Internal").ap()

        route = ExitStack()
        score = sb("score", [P, NT, NE], F32, route)
        rev = sb("rev", [P, NE], F32, route)
        upper = sb("upper", [P, P], BF16, route)
        onesb = sb("onesb", [P, P], BF16, route)
        io_lo = sb("io_lo", [P, P, 2 * NT], BF16, route)
        io_hi = sb("io_hi", [P, SC, 2 * NT], BF16, route)
        io_c = sb("io_c", [P, 2 * NT], BF16, route)
        io_p = sb("io_p", [P, 1], F32, route)
        io_s = sb("io_s", [P, SC], F32, route)
        io_j = sb("io_j", [1, NF], F32, route)
        p5 = sem("p5")
        with ExitStack() as four:
            s4 = lambda n, sh, dt=F32: sb(n, sh, dt, four)
            rw1_sb = s4("rw1_sb", [P, FF])
            rb1_sb = s4("rb1_sb", [P, FC])
            rw2_sb = s4("rw2_sb", [P, FC, NE])
            rb2_bc = s4("rb2_bc", [P, NE])
            stat2 = s4("stat2", [P, NT, 6])
            mv2 = s4("mv2", [P, NT, 2])
            var2 = s4("var2", [P, NT])
            rstd2 = s4("rstd2", [P, NT])
            nmr2 = s4("nmr2", [P, NT])
            rw2p = s4("rw2p", [P, FC, QB])
            sel = s4("sel", [P, NE])
            hn2 = [s4(f"hn2{u}", [P, 4, D]) for u in range(2)]
            hm2 = [s4(f"hm2{u}", [P, 4, D]) for u in range(2)]
            h2 = [s4(f"h2{u}", [P, 4, D]) for u in range(2)]
            h2T = [s4(f"h2T{u}", [P, GRP]) for u in range(2)]
            act = [s4(f"act{u}", [P, FC, GRP]) for u in range(2)]
            scp = [s4(f"scp{u}", [P, GRP]) for u in range(2)]
            pT2 = [pb(four, f"pT2{u}", [P, GRP]) for u in range(2)]
            pA2 = [pb(four, f"pA2{k}", [P, GRP]) for k in range(FC)]
            pSp = pb(four, "pSp", [P, GRP])
            pSc = pb(four, "pSc", [P, GRP])
            d_rw = sem("d_rw")
            v_st = sem("v_st")
            a_rt = sem("a_rt")
            v_h2 = Count(sem("v_h2"), 4)
            p_h2 = Count(sem("p_h2"), 2)
            t_t2 = Count(sem("t_t2"), 1)
            a_t2 = Count(sem("a_t2"), 1)
            t_a2 = Count(sem("t_a2"), FC)
            a_a2 = Count(sem("a_a2"), FC)
            t_sp = Count(sem("t_sp"), 1)
            v_sp = Count(sem("v_sp"), 1)
            t_sc = Count(sem("t_sc"), 1)
            v_sc = Count(sem("v_sc"), 1)
            d_h = [Flights(sem(f"d_h{u}"), 1) for u in range(2)]
            block = four.enter_context(nc.Block())

            @block.sync
            def _(e):
                for f in d_h:
                    f.open(e)
                e.dma_start(rw1_sb[:, :], rw1).then_inc(d_rw, 16)
                e.dma_start(rw2_sb[:, :, :], rw2.rearrange("(c p) n -> p c n", p=P)).then_inc(d_rw, 16)
                with nc.allow_non_contiguous_dma(reason="four values a partition"):
                    e.dma_start(rb1_sb[:, :], rb1.rearrange("(c p) -> p c", p=P)).then_inc(d_rw, 16)
                e.dma_start(rb2_bc[:, :], rb2.rearrange("(a n) -> a n", a=1).broadcast_to([P, NE])).then_inc(d_rw, 16)
                for k in range(2):
                    half_e = slice(k * NE // 2, (k + 1) * NE // 2)
                    e.dma_start(w1_all[:, k * NE * FF // 2:(k + 1) * NE * FF // 2].rearrange("p (e f) -> p e f", f=FF),
                                W1[half_e, :, :].rearrange("e d f -> d e f")).then_inc(d_wt, 16)
                    e.dma_start(w2_all[:, k * NE * FF // 2:(k + 1) * NE * FF // 2].rearrange("p (c d) -> p c d", d=D),
                                W2[half_e, :, :].rearrange("e (c p) d -> p (e c) d", p=P)).then_inc(d_wt, 16)
                with nc.allow_non_contiguous_dma(reason="32 values a partition, once"):
                    e.dma_start(b1_all[:, :], b1.rearrange("e (c p) -> p (e c)", p=P)).then_inc(d_wt, 16)
                e.dma_start(b2_all[:, :, :], b2.rearrange("(a e) d -> a e d", a=1).broadcast_to([P, NE, D])).then_inc(d_wt, 16)
                with e.Fori(0, NG // 2) as i:
                    for u in range(2):
                        p_h2.wait(e, i, u)
                        e.dma_start(h_scr[bass.ds(i * (2 * GRP) + u * GRP, GRP), :].rearrange("(n p) d -> p n d", p=P),
                                    h2[u][:, :, :]).then_inc(d_h[u].sem, 16)
                for u in range(2):
                    d_h[u].wait(e, NG // 2)

            @block.vector
            def _(e):
                for cnt in (v_h2, v_sp, v_sc):
                    cnt.open(e)
                with e.Fori(0, NT // 4) as i:
                    for n in range(4):
                        g = i * 4 + n
                        e.bn_stats(stat2[:, bass.ds(g, 1), :].rearrange("p a s -> p (a s)"),
                                   x_all[:, bass.ds(g + 1, 1), :].rearrange("p a d -> p (a d)")).then_inc(v_st, 1)
                e.wait_ge(v_st, NT)
                for n in range(NT):
                    e.bn_aggr(mv2[:, n, :], stat2[:, n, :]).then_inc(v_st, 1)
                e.wait_ge(v_st, 2 * NT)
                e.tensor_scalar(var2[:, :], mv2[:, :, 1], EPS, None, ALU.add).then_inc(v_st, 1)
                e.wait_ge(a_rt, 1)
                e.reciprocal(rstd2[:, :], var2[:, :]).then_inc(v_st, 1)
                e.wait_ge(v_st, 2 * NT + 2)
                e.scalar_tensor_tensor(out=nmr2[:, :], in0=mv2[:, :, 0], scalar=-1.0, in1=rstd2[:, :], op0=ALU.mult, op1=ALU.mult).then_inc(v_st, 1)
                e.wait_ge(v_st, 2 * NT + 3)

                e.memset(rw2p[:, :, :], 0.0).then_inc(v_st, 1)
                e.wait_ge(d_rw, 64)
                e.wait_ge(v_st, 2 * NT + 4)
                e.tensor_copy(rw2p[:, :, 0:NE], rw2_sb[:, :, :]).then_inc(v_st, 1)
                e.tensor_reduce(sel[:, :], strided(ident[:, :], 0, [[1, NE], [QB, 4]]), AX.X, ALU.add).then_inc(v_st, 1)

                def normalised(i, u):
                    p_h2.wait(e, i, u, 1, back=2)
                    for n in range(4):
                        g = i * 8 + (4 * u + n)
                        e.tensor_scalar(hn2[u][:, n, :], x_all[:, bass.ds(g + 1, 1), :].rearrange("p a d -> p (a d)"),
                                        rstd2[:, bass.ds(g, 1)], nmr2[:, bass.ds(g, 1)], ALU.mult, ALU.add).then_inc(v_h2.sem, 1)

                def step(i, u, left):
                    t_sp.wait(e, i, u)
                    t_sc.wait(e, i, u, back=2)
                    e.tensor_copy(scp[u][:, :], pSp[:, :]).then_inc(v_sp.sem, 1)
                    if left >= 2:
                        normalised(i + 1, u)
                    t_sc.wait(e, i, u)
                    e.tensor_tensor(score[:, bass.ds(i * 8 + 4 * u, 4), :], pSc[:, 0:4 * NE].rearrange("p (n k) -> p n k", n=4),
                                    strided(rb2_bc[:, :], 0, [[0, 4], [1, NE]]), ALU.add).then_inc(v_sc.sem, 1)

                normalised(0, 0)
                normalised(0, 1)
                tiles(e, NG, 2, 2, step)

            @block.gpsimd
            def _(e):
                p_h2.open(e)
                small = dict(allow_small_or_imprecise_dtypes=True)
                e.iota(rev[:, :], [[-1, NE]], NE, 0, **small).then_inc(p5, 1)
                e.memset(onesb[:, :], 1.0).then_inc(p5, 1)
                e.wait_ge(p5, 2)
                e.affine_select(out=upper[:, :], in_=onesb[:, :], compare_op=ALU.is_gt, fill=0.0, base=0,
                                pattern=[[1, P]], channel_multiplier=-1).then_inc(p5, 1)
                e.iota(io_j[:, :], [[1, NF]], 0, 0, **small).then_inc(p5, 1)
                e.iota(io_c[:, :], [[1, 2 * NT]], 1, 0, **small).then_inc(p5, 1)
                e.iota(io_p[:, :], [[0, 1]], 0, 1, **small).then_inc(p5, 1)
                e.iota(io_s[:, :], [[P, SC]], 0, 1, **small).then_inc(p5, 1)
                e.iota(io_lo[:, :, :], [[1, P], [0, 2 * NT]], 0, 0, **small).then_inc(p5, 1)
                with e.Fori(0, NG // 2) as i:
                    for u in range(2):
                        v_h2.wait(e, i, u)
                        t_t2.wait(e, i, u, back=2)
                        d_h[u].wait(e, i)
                        apart(e)
                        e.tensor_tensor(hm2[u][:, :, :], hn2[u][:, :, :], bcast_row(cb_bc, i, 4), ALU.mult).then_inc(p_h2.sem, 1)
                        p_h2.wait(e, i, u, 1)
                        apart(e)
                        e.tensor_tensor(h2[u][:, :, :], hm2[u][:, :, :], bcast_row(sb_bc, i, 4), ALU.add).then_inc(p_h2.sem, 1)

                e.iota(io_hi[:, :, :], [[1, SC], [0, 2 * NT]], 0, 0, **small).then_inc(p5, 1)

            @block.scalar
            def _(e):
                a_t2.open(e)
                a_a2.open(e)
                e.wait_ge(v_st, 2 * NT + 1)
                e.activation(var2[:, :], var2[:, :], ACT.Sqrt).then_inc(a_rt, 1)
                e.wait_ge(d_rw, 64)
                with e.Fori(0, NG // 2) as i:
                    for u in range(2):
                        t_t2.wait(e, i, u)
                        t_a2.wait(e, i, u, back=2)
                        e.activation(h2T[u][:, :], pT2[u][:, :], ACT.Copy).then_inc(a_t2.sem, 1)
                        for k in range(FC):
                            t_a2.wait(e, i, u, k + 1)
                            t_sp.wait(e, i, u, back=2)
                            e.activation(act[u][:, k, :], pA2[k][:, :], ACT.Relu, bias=rb1_sb[:, k:k + 1]).then_inc(a_a2.sem, 1)

            @block.tensor
            def _(e):
                for cnt in (t_t2, t_a2, t_sp, t_sc):
                    cnt.open(e)

                def transposed(i, u):
                    p_h2.wait(e, i, u)
                    a_t2.wait(e, i, u, back=2)
                    for n in range(4):
                        mm = e.transpose(pT2[u][:, n * P:(n + 1) * P], h2[u][:, n, :], ident[:, :])
                    mm.then_inc(t_t2.sem, 1)

                def step(i, u, left):
                    a_t2.wait(e, i, u)
                    for k in range(FC):
                        a_a2.wait(e, i, u, k + 1, back=1)
                        e.matmul(pA2[k][:, :], rw1_sb[:, k * P:(k + 1) * P], h2T[u][:, :], start=True, stop=True).then_inc(t_a2.sem, 1)
                    v_sp.wait(e, i, u, back=1)
                    for k in range(FC):
                        a_a2.wait(e, i, u, k + 1)
                        mm = e.matmul(pSp[QB * k:QB * k + QB, :], rw2p[:, k, :], act[u][:, k, :], start=True, stop=True, skip_group_check=True)
                    mm.then_inc(t_sp.sem, 1)
                    if left >= 1:
                        transposed(*later(i, u, 1, 2))
                    v_sc.wait(e, i, u, back=1)
                    v_sp.wait(e, i, u)
                    for n in range(4):
                        mm = e.matmul(pSc[:, n * NE:(n + 1) * NE], scp[u][:, n * P:(n + 1) * P], sel[:, :], start=True, stop=True)
                    mm.then_inc(t_sc.sem, 1)

                transposed(0, 0)
                e.wait_ge(d_rw, 64)
                e.wait_ge(v_st, 2 * NT + 6)
                tiles(e, NG, 2, 2, step)

        with ExitStack() as five:
            s5 = lambda n, sh, dt=F32: sb(n, sh, dt, five)
            m12 = s5("m12", [P, 2, NT])
            eqm = s5("eqm", [P, NT, NE])
            rank = s5("rank", [P, NT])
            oh = [s5(f"oh{k}", [P, NT, NE]) for k in range(2)]
            sc2 = s5("sc2", [P, NT, NE])
            ohb = s5("ohb", [P, NT * NE], BF16)
            tot = s5("tot", [P, NT + 16, NE])
            cum = [s5(f"cum{k}", [P, NT + 16, NE]) for k in range(2)]
            off = s5("off", [P, NT, NE])
            cnt_i = s5("cnt_i", [P, NE], I32)
            til = s5("til", [P, NE])
            tcu = [s5(f"tcu{k}", [P, 8 + NE]) for k in range(2)]
            base = s5("base", [P, NE])
            posg = s5("posg", [P, NT, NE])
            posm = s5("posm", [P, NT, NE])
            pos = s5("pos", [P, 2, NT])
            pos_i = s5("pos_i", [P, 2 * NT], I32)
            lo_i = s5("lo_i", [P, 2 * NT], I32)
            hi_i = s5("hi_i", [P, 2 * NT], I32)
            lo_b = s5("lo_b", [P, 2 * NT], BF16)
            hi_b = s5("hi_b", [P, 2 * NT], BF16)
            one_lo = s5("one_lo", [P, P, 2 * NT], BF16)
            one_hi = s5("one_hi", [P, SC, 2 * NT], BF16)
            mapv = s5("mapv", [P, 2, SC, 2 * NT], BF16)
            ge = s5("ge", [1, NF, NE])
            eidf = s5("eidf", [1, NF])
            cc = s5("cc", [P, SC])
            pp = s5("pp", [P, SC])
            fa = s5("fa", [P, SC])
            fb = s5("fb", [P, SC])
            fc = s5("fc", [P, SC])
            fd = s5("fd", [P, SC])
            pPre = pb(five, "pPre", [P, 512])
            pTot = pb(five, "pTot", [P, 512])
            pMap = pb(five, "pMap", [P, 512])
            v5, a5, t5 = sem("v5"), sem("a5"), sem("t5")
            n5 = {}
            k5 = [0]
            block = five.enter_context(nc.Block())

            @block.vector
            def _(e):
                def step(ins, name=None):
                    k5[0] += 1
                    if name:
                        n5[name] = k5[0]
                    ins.then_inc(v5, 1)

                def own():
                    e.wait_ge(v5, k5[0])

                def per_tile(t):
                    return strided(t, 0, [[1, NT], [0, NE]])

                def per_expert(t, n=NT):
                    return strided(t, 0, [[0, n], [1, NE]])

                e.wait_ge(p5, 2)
                cur = score
                for k in range(2):
                    step(e.tensor_reduce(m12[:, k, :], cur[:, :, :], AX.X, ALU.max), f"m{k}")
                    own()
                    step(e.tensor_tensor(eqm[:, :, :], cur[:, :, :], per_tile(m12[:, k, :]), ALU.is_equal))
                    own()
                    step(e.tensor_tensor(eqm[:, :, :], eqm[:, :, :], per_expert(rev[:, :]), ALU.mult))
                    own()
                    step(e.tensor_reduce(rank[:, :], eqm[:, :, :], AX.X, ALU.max))
                    own()
                    step(e.tensor_tensor(oh[k][:, :, :], per_expert(rev[:, :]), per_tile(rank[:, :]), ALU.is_equal))
                    own()
                    if k == 0:
                        step(e.scalar_tensor_tensor(out=sc2[:, :, :], in0=oh[0][:, :, :], scalar=-3e38, in1=score[:, :, :],
                                                    op0=ALU.mult, op1=ALU.add))
                        own()
                        cur = sc2
                step(e.tensor_tensor(ohb[:, :].rearrange("p (t k) -> p t k", k=NE), oh[0][:, :, :], oh[1][:, :, :], ALU.add), "ohb")
                step(e.tensor_tensor(gates[:, 1, :], m12[:, 1, :], m12[:, 0, :], ALU.subtract), "gd")
                for t in (tot, cum[0], cum[1]):
                    step(e.memset(t[:, 0:16, :], 0.0))
                for t in tcu:
                    step(e.memset(t[:, 0:8], 0.0))
                own()
                e.wait_ge(t5, 1)
                step(e.tensor_copy(tot[:, 16:, :], pTot[:, 0:NT * NE].rearrange("p (t k) -> p t k", k=NE)))
                own()
                src = tot
                for r, s in enumerate((1, 2, 4, 8, 16)):
                    dst = cum[r % 2]
                    step(e.tensor_tensor(dst[:, 16:, :], src[:, 16:, :], src[:, 16 - s:16 + NT - s, :], ALU.add))
                    own()
                    src = dst
                step(e.tensor_scalar(til[:, :], src[:, 16 + NT - 1, :], float(FT - 1), None, ALU.add))
                own()
                step(e.tensor_copy(cnt_i[:, :], til[:, :]))
                own()
                step(e.tensor_scalar(cnt_i[:, :], cnt_i[:, :], FT.bit_length() - 1, None, ALU.logical_shift_right))
                own()
                step(e.tensor_copy(tcu[0][:, 8:], cnt_i[:, :]))
                own()
                for r, s in enumerate((1, 2, 4)):
                    step(e.tensor_tensor(tcu[(r + 1) % 2][:, 8:], tcu[r % 2][:, 8:], tcu[r % 2][:, 8 - s:8 + NE - s], ALU.add))
                    own()
                step(e.tensor_copy(til[:, :], cnt_i[:, :]))
                own()
                step(e.tensor_tensor(base[:, :], tcu[1][:, 8:], til[:, :], ALU.subtract))
                own()
                step(e.tensor_scalar(base[:, :], base[:, :], float(FT), None, ALU.mult))
                e.wait_ge(p5, 9)
                step(e.tensor_tensor(ge[:, :, :], strided(io_j[:, :], 0, [[1, NF], [0, NE]]),
                                     strided(tcu[1][0:1, 8:9], 0, [[0, NF], [1, NE]]), ALU.is_ge))
                own()
                step(e.tensor_reduce(eidf[:, :], ge[:, :, :], AX.X, ALU.add))
                own()
                step(e.tensor_scalar(eid[:, :], eidf[:, :], float(NE - 1), None, ALU.min))
                step(e.tensor_tensor(off[:, :, :], src[:, 16:, :], tot[:, 16:, :], ALU.subtract))
                own()
                step(e.tensor_tensor(off[:, :, :], off[:, :, :], per_expert(base[:, :]), ALU.add))
                own()
                step(e.tensor_tensor(posg[:, :, :], pPre[:, 0:NT * NE].rearrange("p (t k) -> p t k", k=NE), off[:, :, :], ALU.add))
                own()
                for k in range(2):
                    step(e.tensor_tensor(posm[:, :, :], posg[:, :, :], oh[k][:, :, :], ALU.mult))
                    own()
                    step(e.tensor_reduce(pos[:, k, :], posm[:, :, :], AX.X, ALU.add))
                    own()
                step(e.tensor_copy(pos_i[:, :], pos[:, :, :].rearrange("p k t -> p (k t)")))
                own()
                step(e.tensor_scalar(lo_i[:, :], pos_i[:, :], P - 1, None, ALU.bitwise_and))
                step(e.tensor_scalar(hi_i[:, :], pos_i[:, :], P.bit_length() - 1, None, ALU.logical_shift_right))
                own()
                step(e.tensor_copy(lo_b[:, :], lo_i[:, :]))
                step(e.tensor_copy(hi_b[:, :], hi_i[:, :]))
                own()
                step(e.tensor_tensor(one_hi[:, :, :], io_hi[:, :, :], strided(hi_b[:, :], 0, [[0, SC], [1, 2 * NT]]), ALU.is_equal))
                step(e.tensor_tensor(one_lo[:, :, :], io_lo[:, :, :], strided(lo_b[:, :], 0, [[0, P], [1, 2 * NT]]), ALU.is_equal))
                own()
                step(e.tensor_tensor(mapv[:, 0, :, :], one_hi[:, :, :], strided(io_c[:, :], 0, [[0, SC], [1, 2 * NT]]), ALU.mult))
                step(e.tensor_scalar(mapv[:, 1, :, :], one_hi[:, :, :], io_p[:, 0:1], None, ALU.mult), "map")
                e.wait_ge(a5, 1)
                step(e.tensor_scalar(m12[:, 0, :], m12[:, 1, :], 1.0, None, ALU.add))
                own()
                step(e.reciprocal(gates[:, 0, :], m12[:, 0, :]))
                own()
                step(e.tensor_tensor(gates[:, 1, :], m12[:, 1, :], gates[:, 0, :], ALU.mult))
                e.wait_ge(t5, 2)
                step(e.tensor_copy(cc[:, :], pMap[:, 0:SC]))
                step(e.tensor_copy(pp[:, :], pMap[:, SC:2 * SC]))
                own()
                step(e.tensor_scalar(fa[:, :], cc[:, :], float(NT + 1), -float(NT), ALU.is_ge, ALU.mult))
                own()
                step(e.tensor_tensor(fb[:, :], fa[:, :], cc[:, :], ALU.add))
                own()
                step(e.tensor_scalar(fb[:, :], fb[:, :], float(P), -float(P), ALU.mult, ALU.add))
                own()
                step(e.tensor_tensor(fb[:, :], fb[:, :], pp[:, :], ALU.add))
                own()
                step(e.tensor_scalar(gidx[:, 0:SC], fb[:, :], 0.0, None, ALU.max))
                step(e.tensor_scalar(fc[:, :], cc[:, :], float(P), -float(P), ALU.mult, ALU.add))
                own()
                step(e.tensor_tensor(fc[:, :], fc[:, :], pp[:, :], ALU.add))
                step(e.tensor_scalar(fd[:, :], io_s[:, :], float(2 * T + P), None, ALU.add))
                step(e.tensor_scalar(fa[:, :], cc[:, :], 0.0, None, ALU.is_equal))
                own()
                step(e.tensor_tensor(fd[:, :], fd[:, :], fa[:, :], ALU.mult))
                own()
                step(e.tensor_tensor(sidx[:, 0:SC], fd[:, :], fc[:, :], ALU.add))
                own()

            @block.scalar
            def _(e):
                e.wait_ge(v5, n5["gd"])
                e.activation(m12[:, 1, :], gates[:, 1, :], ACT.Exp).then_inc(a5, 1)

            @block.tensor
            def _(e):
                e.wait_ge(p5, 3)
                e.wait_ge(v5, n5["ohb"])
                e.matmul(pPre[:, 0:NT * NE], upper[:, :], ohb[:, :], start=True, stop=True)
                e.matmul(pTot[:, 0:NT * NE], onesb[:, :], ohb[:, :], start=True, stop=True).then_inc(t5, 1)
                e.wait_ge(v5, n5["map"])
                for k in range(2 * NT):
                    mm = e.matmul(pMap[:, 0:2 * SC], one_lo[:, :, k], mapv[:, :, :, k].rearrange("p a s -> p (a s)"),
                                  start=k == 0, stop=k == 2 * NT - 1)
                mm.then_inc(t5, 1)

        route.close()

        with ExitStack() as six:
            s6 = lambda n, sh, dt=F32: sb(n, sh, dt, six)
            R = 3
            AHEAD = 5
            gi = [s6(f"gi{u}", [P, 2], I32) for u in range(R)]
            si = [s6(f"si{u}", [P, 2], I32) for u in range(R)]
            w1t = [s6(f"w1t{u}", [P, FF]) for u in range(R)]
            hg = [s6(f"hg{u}", [P, 2, P]) for u in range(R)]
            hgT = [s6(f"hgT{u}", [P, FT]) for u in range(R)]
            ac = [s6(f"ac{u}", [P, FC, FT]) for u in range(R)]
            ys = [s6(f"ys{u}", [P, 2, D]) for u in range(R)]
            pTg = pb(six, "pTg", [P, 512])
            pU = [[pb(six, f"pU{u}{k}", [P, 512]) for k in range(2)] for u in range(R)]
            pY = pb(six, "pY", [P, 512])
            d_g = [sem(f"d_g{u}") for u in range(R)]
            d_y = [Flights(sem(f"d_y{u}"), 2) for u in range(R)]
            v_gi = Count(sem("v_gi"), 1, R)
            v_si = Count(sem("v_si"), 1, R)
            v_w = Count(sem("v_w"), 1, R)
            t_tg = Count(sem("t_tg"), 1, R)
            v_tg = Count(sem("v_tg"), 1, R)
            t_up = Count(sem("t_up"), 2, R)
            a_up = Count(sem("a_up"), FC, R)
            t_dn = Count(sem("t_dn"), 1, R)
            v_y = Count(sem("v_y"), 1, R)
            block = six.enter_context(nc.Block())

            def expert(e, i, u):
                return e.value_load(eid[0:1, bass.ds(i * R + u, 1)], min_val=0, max_val=NE - 1)

            def at(i, u, n):
                return later(i, u, n, R)

            @block.gpsimd
            def _(e):
                def gather(i, u):
                    v_gi.wait(e, i, u)
                    t_tg.wait(e, i, u, back=R)
                    apart(e)
                    for k in range(2):
                        e.indirect_dma_start(out=hg[u][:, k, :], out_offset=None, in_=h_scr,
                                             in_offset=bass.IndirectOffsetOnAxis(ap=gi[u][:, k:k + 1].bitcast(U32), axis=0)).then_inc(d_g[u], 16)

                def scatter(i, u):
                    v_si.wait(e, i, u)
                    v_y.wait(e, i, u)
                    apart(e)
                    for k in range(2):
                        e.indirect_dma_start(out=y_scr, out_offset=bass.IndirectOffsetOnAxis(ap=si[u][:, k:k + 1].bitcast(U32), axis=0),
                                             in_=ys[u][:, k, :], in_offset=None).then_inc(d_y[u].sem, 16)

                for j in range(R):
                    gather(0, j)
                for u in range(R):
                    spare = 2 * T + NF * FT + u
                    e.dma_start(y_scr[spare:spare + 1, :], ident[0:1, :]).then_inc(d_y[u].sem, 16)
                for j in range(R, AHEAD):
                    gather(*at(0, j, 0))

                def step(i, u, left):
                    scatter(i, u)
                    if left >= AHEAD:
                        gather(*at(i, u, AHEAD))

                tiles(e, NF, R, AHEAD, step)
                for u in range(R):
                    e.wait_ge(d_g[u], 32 * (NF // R))
                    d_y[u].wait(e, NF // R)

            @block.scalar
            def _(e):
                a_up.open(e)
                e.wait_ge(d_wt, 16 * N_WT)

                def relu(i, u, left):
                    x_ = expert(e, i, u)
                    t_dn.wait(e, i, u, back=R)
                    for k in range(FC):
                        if k % 2 == 0:
                            t_up.wait(e, i, u, k // 2 + 1)
                            apart(e)
                        e.activation(ac[u][:, k, :], pU[u][k // 2][:, (k % 2) * FT:(k % 2 + 1) * FT], ACT.Relu,
                                     bias=b1_all[:, bass.ds(x_ * FC + k, 1)]).then_inc(a_up.sem, 1)

                tiles(e, NF, R, 0, relu)

            @block.vector
            def _(e):
                for cnt in (v_gi, v_si, v_w, v_tg, v_y):
                    cnt.open(e)

                def gather_index(i, u):
                    t_tg.wait(e, i, u, back=R)
                    apart(e)
                    e.tensor_copy(gi[u][:, :], gidx[:, bass.ds(i * (2 * R) + 2 * u, 2)]).then_inc(v_gi.sem, 1)

                def first_matrix(i, u):
                    x_ = expert(e, i, u)
                    t_up.wait(e, i, u, back=R)
                    apart(e)
                    e.tensor_copy(w1t[u][:, :], w1_all[:, bass.ds(x_ * FF, FF)]).then_inc(v_w.sem, 1)

                def scatter_index(i, u):
                    d_y[u].wait(e, i)
                    apart(e)
                    e.tensor_copy(si[u][:, :], sidx[:, bass.ds(i * (2 * R) + 2 * u, 2)]).then_inc(v_si.sem, 1)

                def gathered(i, u):
                    t_tg.wait(e, i, u)
                    t_up.wait(e, i, u, back=R)
                    e.tensor_copy(hgT[u][:, :], pTg[:, 0:FT]).then_inc(v_tg.sem, 1)

                def result(i, u):
                    x_ = expert(e, i, u)
                    t_dn.wait(e, i, u)
                    e.tensor_tensor(ys[u][:, :, :], pY[:, 0:2 * D].rearrange("p (k d) -> p k d", k=2),
                                    b2_all[:, bass.ds(x_, 1), :].broadcast_to([P, 2, D]), ALU.add).then_inc(v_y.sem, 1)

                for j in range(R):
                    gather_index(0, j)
                e.wait_ge(d_wt, 16 * N_WT)
                for j in range(2):
                    first_matrix(0, j)
                    gathered(0, j)
                    gather_index(*at(0, j, R))

                def step(i, u, left):
                    if left >= 2:
                        first_matrix(*at(i, u, 2))
                    scatter_index(i, u)
                    if left >= 2:
                        gathered(*at(i, u, 2))
                    if left >= AHEAD:
                        gather_index(*at(i, u, AHEAD))
                    result(i, u)

                tiles(e, NF, R, AHEAD, step)

            @block.tensor
            def _(e):
                for cnt in (t_tg, t_up, t_dn):
                    cnt.open(e)
                e.wait_ge(d_wt, 16 * N_WT)

                def rows(i, u):
                    e.wait_ge(d_g[u], i * 32 + 32)
                    v_tg.wait(e, i, u, back=1)
                    for k in range(2):
                        mm = e.transpose(pTg[:, k * P:(k + 1) * P], hg[u][:, k, :], ident[:, :])
                    mm.then_inc(t_tg.sem, 1)

                def up(i, u):
                    v_w.wait(e, i, u)
                    v_tg.wait(e, i, u)
                    a_up.wait(e, i, u, back=R)
                    for k in range(FC):
                        mm = e.matmul(pU[u][k // 2][:, (k % 2) * FT:(k % 2 + 1) * FT], w1t[u][:, k * P:(k + 1) * P], hgT[u][:, :],
                                      start=True, stop=True)
                        if k % 2:
                            mm.then_inc(t_up.sem, 1)

                def down(i, u):
                    x_ = expert(e, i, u)
                    v_y.wait(e, i, u, back=1)
                    a_up.wait(e, i, u)
                    for r in range(2):
                        for k in range(FC):
                            mm = e.matmul(pY[:, r * D:(r + 1) * D], ac[u][:, k, r * P:(r + 1) * P], w2_all[:, bass.ds(x_ * FF + k * D, D)],
                                          start=k == 0, stop=k == FC - 1)
                    mm.then_inc(t_dn.sem, 1)

                rows(0, 0)
                rows(0, 1)
                up(0, 0)

                def step(i, u, left):
                    if left >= 2:
                        rows(*at(i, u, 2))
                    if left >= 1:
                        up(*at(i, u, 1))
                    down(i, u)

                tiles(e, NF, R, 2, step)

        with ExitStack() as seven:
            s7 = lambda n, sh, dt=F32: sb(n, sh, dt, seven)
            y1 = s7("y1", [P, B, TPB, D])
            y2 = s7("y2", [P, B, TPB, D])
            fin = s7("fin", [P, B, TPB, D])
            d_ld = [sem(f"d_ld{b}") for b in range(B)]
            a7, v7, p7, d_out = sem("a7"), sem("v7"), sem("p7"), sem("d_out")
            block = seven.enter_context(nc.Block())

            @block.sync
            def _(e):
                for b in range(B):
                    for k, t in enumerate((y1, y2)):
                        e.dma_start(t[:, b, :, :], y_scr[k * T + b * S:k * T + (b + 1) * S, :].rearrange("(n p) d -> p n d", p=P)).then_inc(d_ld[b], 16)
                for b in range(B):
                    e.wait_ge(p7, b + 1)
                    e.dma_start(of[b * S:(b + 1) * S, :].rearrange("(n p) d -> p n d", p=P), fin[:, b, :, :]).then_inc(d_out, 16)
                e.wait_ge(d_out, 16 * B)

            @block.scalar
            def _(e):
                for b in range(B):
                    e.wait_ge(d_ld[b], 32)
                    for n in range(TPB):
                        g = b * TPB + n
                        e.activation(y1[:, b, n, :], y1[:, b, n, :], ACT.Copy, scale=gates[:, 0, g:g + 1]).then_inc(a7, 1)

            @block.vector
            def _(e):
                for b in range(B):
                    e.wait_ge(d_ld[b], 32)
                    for n in range(TPB):
                        g = b * TPB + n
                        e.wait_ge(a7, g + 1)
                        e.scalar_tensor_tensor(out=y2[:, b, n, :], in0=y2[:, b, n, :], scalar=gates[:, 1, g:g + 1], in1=y1[:, b, n, :],
                                               op0=ALU.mult, op1=ALU.add).then_inc(v7, 1)
                    e.wait_ge(v7, (b + 1) * (TPB + 1) - 1)
                    e.tensor_tensor(y2[:, b, :, :], y2[:, b, :, :], strided(gb_bc[:, b, :], 0, [[0, TPB], [1, D]]), ALU.mult).then_inc(v7, 1)

            @block.gpsimd
            def _(e):
                for b in range(B):
                    e.wait_ge(v7, (b + 1) * (TPB + 1))
                    e.tensor_tensor(fin[:, b, :, :], y2[:, b, :, :], x_all[:, 1 + b * TPB:1 + (b + 1) * TPB, :], ALU.add).then_inc(p7, 1)


_INS = ['L0_attn_x', 'L0_attn_alpha', 'L0_attn_Wq', 'L0_attn_bq', 'L0_attn_Wk', 'L0_attn_bk', 'L0_attn_Wv', 'L0_attn_bv',
        'L0_attn_W_o', 'L0_attn_Wfc', 'L0_attn_bfc', 'L0_ffn_rw1', 'L0_ffn_rb1', 'L0_ffn_rw2', 'L0_ffn_rb2', 'L0_ffn_W1',
        'L0_ffn_b1', 'L0_ffn_W2', 'L0_ffn_b2', 'L0_c', 'L0_wmod']


def kernel(**inputs):
    import numpy as _np
    import concourse.bacc as _bacc
    from concourse import mybir as _mybir
    from concourse.bass_utils import run_bass_kernel_spmd as _run

    nc = _bacc.Bacc("TRN2", target_bir_lowering=False, num_devices=1)
    arrays, args = {}, []
    for name in _INS:
        a = _np.ascontiguousarray(inputs[name])
        if a.ndim == 0:
            a = a.reshape(1, 1)
        arrays[f"in_{name}"] = a
        args.append(nc.dram_tensor(f"in_{name}", a.shape, _mybir.dt.from_np(a.dtype), kind="ExternalInput").ap())
    args.append(nc.dram_tensor("out_0", (B, S, D), F32, kind="ExternalOutput").ap())
    build(nc, *args)
    r = _run(nc, [arrays], core_ids=[0])
    return r.results[0]["out_0"]
```

```python
import numpy as np
import concourse.bass as bass
from concourse import mybir
from contextlib import ExitStack

F32 = mybir.dt.float32
F32R = mybir.dt.float32r
BF16 = mybir.dt.bfloat16
I32 = mybir.dt.int32
U32 = mybir.dt.uint32
ALU = mybir.AluOpType
ACT = mybir.ActivationFunctionType
AX = mybir.AxisListType

P = 128
B, S, D = 4, 1024, 128
H, HD = 16, 8
T = B * S
NT = T // P
TPB = S // P
MIN_W, MAX_W = 24, 120
HALO = 64
HG = 4
QB = 32
WIN = QB + 2 * HALO
KW = P + 2 * HALO
KBLK = KW // QB
GRP = 512
NG = T // GRP
BIG = 1e30
EPS = 1e-5
NE, TOPK, FF = 8, 2, 512
FC = FF // P
FT = 128
NF = T * TOPK // FT + NE - 1
FR = FT // P
SC = NF * FR
ISQ = 1.0 / float(np.sqrt(HD))


class Count:

    def __init__(self, sem, n, ring=2):
        self.sem, self.n, self.ring = sem, n, ring

    def open(self, eng):
        eng.sem_inc(self.sem, self.ring * self.n)

    def wait(self, eng, turn, u, k=None, back=0):
        k = self.n if k is None else k
        eng.wait_ge(self.sem, turn * (self.ring * self.n) + (self.n * (self.ring + u - back) + k))


class Flights:

    def __init__(self, sem, n):
        self.sem, self.n = sem, n

    def open(self, eng):
        eng.sem_inc(self.sem, 16)

    def wait(self, eng, turn, k=0):
        eng.wait_ge(self.sem, turn * (16 * self.n) + (16 + 16 * k))


def strided(ap, offset, dims):
    return bass.AP(tensor=ap.tensor, offset=ap.offset + offset, ap=[list(ap.ap[0])] + dims)


def tiles(eng, total, ring, ahead, step, head=0):
    turns = (total - ahead) // ring
    for j in range(head * ring):
        step(j // ring, j % ring, total)
    with eng.Fori(head, turns) as i:
        for u in range(ring):
            step(i, u, total)
    for j in range(turns * ring, total):
        step(j // ring, j % ring, total - 1 - j)


def later(i, u, n, ring):
    return i + (u + n) // ring, (u + n) % ring


def is_first(i, u):
    return isinstance(i, int) and i == 0 and u == 0


def apart(eng):
    eng.nop(nofuse=True)


def bcast_row(rows, b, n):
    return rows[:, bass.ds(b, 1), :].broadcast_to([P, n, D])


def build(nc, x, alpha, Wq, bq, Wk, bk, Wv, bv, W_o, Wfc, bfc, rw1, rb1, rw2, rb2, W1, b1, W2, b2, c, wmod, out):
    top = ExitStack()

    def sem(name):
        return top.enter_context(nc.semaphore(name))

    def sb(name, shape, dt=F32, ctx=top):
        return ctx.enter_context(nc.sbuf_tensor(name, shape, dt))

    def pb(ctx, name, shape, dt=F32):
        return ctx.enter_context(nc.psum_tensor(name, shape, dt))

    xf = x.rearrange("b s d -> (b s) d")
    of = out.rearrange("b s d -> (b s) d")

    with top:
        x_all = sb("x_all", [P, NT + 1, D])
        ident = sb("ident", [P, P])
        ga_bc = sb("ga_bc", [P, B + 1, D])
        gacv_bc = sb("gacv_bc", [P, B + 1, D])
        sb_bc = sb("sb_bc", [P, B, D])
        cb_bc = sb("cb_bc", [P, B, D])
        gb_bc = sb("gb_bc", [P, B, D])
        q_scr = nc.dram_tensor("q_scr", (4, QB, HG, T), F32, kind="Internal").ap()
        v_scr = nc.dram_tensor("v_scr", (T + 2 * HALO, D), F32, kind="Internal").ap()

        stat2 = sb("stat2", [P, NT + 1, 6])
        mv2 = sb("mv2", [P, NT, 2])

        attn = ExitStack()
        kst = sb("kst", [P, HG, T + 2 * HALO], F32R, attn)
        wqs = sb("wqs", [P, D], F32, attn)
        wk_sb = sb("wk_sb", [P, D], F32, attn)
        wv_sb = sb("wv_sb", [P, D], F32, attn)
        wc = sb("wc", [P, D], F32, attn)
        wcg = sb("wcg", [P, B + 1, D], F32, attn)
        bqs = sb("bqs", [P, 1], F32, attn)
        bk_sb = sb("bk_sb", [P, 1], F32, attn)
        sa_t = sb("sa_t", [P, B], F32, attn)
        ca_t = sb("ca_t", [P, B], F32, attn)
        rstd = sb("rstd", [P, NT], F32, attn)
        nmr = sb("nmr", [P, NT], F32, attn)
        identb = sb("identb", [P, P], BF16, attn)
        eqh = sb("eqh", [P, 4], F32, attn)
        eqg = sb("eqg", [P, 4], F32, attn)
        eqd = sb("eqd", [P, 4], F32, attn)
        eqq = sb("eqq", [P, 4], F32, attn)
        st_den = sb("st_den", [P, D], F32, attn)
        pick = sb("pick", [P, 4, HG, 4, QB], F32R, attn)
        masks = sb("masks", [P, TPB, 4 * WIN], BF16, attn)

        prep = ExitStack()
        modrow = sb("modrow", [P, B, 4 * D], F32, prep)
        cvr = sb("cvr", [P, D], F32, prep)
        bfc_bc = sb("bfc_bc", [P, D], F32, prep)
        mint = sb("mint", [P, WIN], BF16, prep)
        pickf = sb("pickf", [P, 4, HG, 4, QB], F32, prep)
        with ExitStack() as one:
            s1 = lambda n, sh, dt=F32: sb(n, sh, dt, one)
            wq_sb = s1("wq_sb", [P, D])
            wfc_sb = s1("wfc_sb", [P, D])
            wo_sb = s1("wo_sb", [P, HD])
            bq_sb = s1("bq_sb", [P, 1])
            bv_sb = s1("bv_sb", [P, 1])
            cT = s1("cT", [P, B])
            silu = s1("silu", [P, B])
            tmp4 = s1("tmp4", [P, B])
            wmod_sb = s1("wmod_sb", [P, 6 * D])
            stats = s1("stats", [P, NT, 6])
            mv = s1("mv", [P, NT, 2])
            varr = s1("varr", [P, NT])
            rcp = s1("rcp", [P, NT])
            xl = s1("xl", [B, 2, D])
            statl = s1("statl", [B, 2, 6])
            mvl = s1("mvl", [B, 2, 2])
            varl = s1("varl", [B, 2])
            rcpl = s1("rcpl", [B, 2])
            nml = s1("nml", [B, 2])
            sac = s1("sac", [B, 2 * D])
            fl = s1("fl", [B, 2, D])
            flsum = s1("flsum", [B, 1])
            sc = s1("sc", [1, 16])
            sci = s1("sci", [1, 4], I32)
            ones_r = s1("ones_r", [B, P])
            half = s1("half", [P, 1])
            pint = s1("pint", [P, 1], I32)
            pbits = s1("pbits", [P, 6], I32)
            pf = s1("pf", [P, 6])
            ci = s1("ci", [P, WIN], I32)
            cf = s1("cf", [P, WIN])
            dist = s1("dist", [P, WIN])
            adist = s1("adist", [P, WIN])
            eq16 = s1("eq16", [P, H])
            bdo = s1("bdo", [P, D])
            bdoT = s1("bdoT", [P, D])
            zero_kv = s1("zero_kv", [P, HG * HALO])
            ps_row = [pb(one, f"ps_row{b}", [P, 512]) for b in range(B)]
            ps_col = pb(one, "ps_col", [P, 512])
            ps_a = pb(one, "ps_a", [P, 512])
            ps_b = pb(one, "ps_b", [P, 512])
            ps_h = pb(one, "ps_h", [P, 512])

            ld_c, ld_f, ld_o, ld_w, ld_al = sem("ld_c"), sem("ld_f"), sem("ld_o"), sem("ld_w"), sem("ld_al")
            ld_x = [sem(f"ld_x{b}") for b in range(B)]
            s_pad = sem("s_pad")
            p_cst = sem("p_cst")
            v1, a1, t1 = sem("v1"), sem("a1"), sem("t1")
            kv = [0]
            nv = {}
            block = one.enter_context(nc.Block())

            @block.vector
            def _(e):
                def step(name, ins):
                    kv[0] += 1
                    nv[name] = kv[0]
                    ins.then_inc(v1, 1)

                def own():
                    e.wait_ge(v1, kv[0])

                def x_stats(b):
                    e.wait_ge(ld_x[b], 16)
                    for n in range(b * TPB, (b + 1) * TPB):
                        step("_s", e.bn_stats(stats[:, n, :], x_all[:, n + 1, :]))

                step("zero", e.memset(zero_kv[:, :], 0.0))
                step("ones", e.memset(ones_r[:, :], 1.0))
                e.wait_ge(p_cst, 4)
                for k, (sh, msk) in enumerate(((5, 3), (2, 7), (0, 3), (3, 15), (0, 31), (3, 3))):
                    step(f"pb{k}", e.tensor_scalar(pbits[:, k:k + 1], pint[:, :], sh, msk, ALU.logical_shift_right, ALU.bitwise_and))
                own()
                step("pf", e.tensor_copy(pf[:, :], pbits[:, :]))
                step("cf", e.tensor_copy(cf[:, :], ci[:, :]))
                own()
                step("eqh", e.tensor_scalar(eqh[:, :], cf[:, 0:4], pf[:, 0:1], None, ALU.is_equal))
                step("eqg", e.tensor_scalar(eqg[:, :], cf[:, 0:4], pf[:, 1:2], None, ALU.is_equal))
                step("eqq", e.tensor_scalar(eqq[:, :], cf[:, 0:4], pf[:, 2:3], None, ALU.is_equal))
                step("eqd", e.tensor_scalar(eqd[:, :], cf[:, 0:4], pf[:, 5:6], None, ALU.is_equal))
                step("eq16", e.tensor_scalar(eq16[:, :], cf[:, 0:H], pf[:, 3:4], None, ALU.is_equal))
                step("identb", e.tensor_copy(identb[:, :], ident[:, :]))
                step("dist", e.tensor_scalar(dist[:, :], cf[:, :], pf[:, 4:5], float(HALO), ALU.subtract, ALU.subtract))
                own()
                step("adist", e.scalar_tensor_tensor(out=adist[:, :], in0=dist[:, :], scalar=-1.0, in1=dist[:, :], op0=ALU.mult, op1=ALU.max))
                step("st", e.tensor_tensor(st_den[:, :].rearrange("p (g h d) -> p g h d", g=4, h=4),
                                           strided(eqh[:, :], 0, [[0, 4], [1, 4], [0, 8]]),
                                           strided(eqg[:, :], 0, [[1, 4], [0, 4], [0, 8]]), ALU.mult))
                e.wait_ge(a1, 1)
                step("silu1", e.tensor_scalar(tmp4[:, :], silu[:, :], 1.0, None, ALU.add))
                own()
                step("silu2", e.reciprocal(tmp4[:, :], tmp4[:, :]))
                own()
                step("silu3", e.tensor_tensor(silu[:, :], cT[:, :], tmp4[:, :], ALU.mult))
                e.wait_ge(ld_o, 16)
                step("bdo", e.tensor_tensor(bdo[:, :].rearrange("p (h k) -> p h k", h=H),
                                            strided(wo_sb[:, :], 0, [[0, H], [1, HD]]),
                                            strided(eq16[:, :], 0, [[1, H], [0, HD]]), ALU.mult))
                e.wait_ge(ld_f, 32)
                for k in range(2):
                    step("_s", e.bn_stats(statl[:, k, :], xl[:, k, :]))
                own()
                for k in range(2):
                    step("_a", e.bn_aggr(mvl[:, k, :], statl[:, k, :]))
                own()
                step("varl", e.tensor_scalar(varl[:, :], mvl[:, :, 1], EPS, None, ALU.add))
                x_stats(0)
                e.wait_ge(a1, 2)
                step("_r", e.reciprocal(rcpl[:, :], varl[:, :]))
                e.wait_ge(t1, 1)
                step("modT1", e.tensor_copy(sa_t[:, :], ps_col[:, 0:B]))
                step("modT2", e.tensor_scalar(ca_t[:, :], ps_col[:, B:2 * B], 1.0, None, ALU.add))
                step("_r", e.tensor_copy(sac[:, 0:D], ps_h[0:B, 0:D]))
                step("_r", e.tensor_scalar(sac[:, D:], ps_h[0:B, D:2 * D], 1.0, None, ALU.add))
                own()
                step("_r", e.scalar_tensor_tensor(out=nml[:, :], in0=mvl[:, :, 0], scalar=-1.0, in1=rcpl[:, :], op0=ALU.mult, op1=ALU.mult))
                e.wait_ge(t1, 2)
                step("bdoT", e.tensor_copy(bdoT[:, :], ps_a[:, 0:D]))
                own()
                for k in range(2):
                    step("_f", e.tensor_scalar(xl[:, k, :], xl[:, k, :], rcpl[:, k:k + 1], nml[:, k:k + 1], ALU.mult, ALU.add))
                own()
                step("_f", e.tensor_tensor(xl[:, :, :], xl[:, :, :], strided(sac[:, :], D, [[0, 2], [1, D]]), ALU.mult))
                own()
                step("_f", e.tensor_tensor(xl[:, :, :], xl[:, :, :], strided(sac[:, :], 0, [[0, 2], [1, D]]), ALU.add))
                own()
                step("fd", e.tensor_tensor(fl[:, 0, :], xl[:, 0, :], xl[:, 1, :], ALU.subtract))
                own()
                step("fa", e.scalar_tensor_tensor(out=fl[:, 1, :], in0=fl[:, 0, :], scalar=-1.0, in1=fl[:, 0, :], op0=ALU.mult, op1=ALU.max))
                own()
                step("fs", e.tensor_reduce(flsum[:, :], fl[:, 1, :], AX.X, ALU.add))
                x_stats(1)
                e.wait_ge(a1, 3)
                step("al1", e.tensor_scalar(sc[:, 3:4], sc[:, 2:3], 1.0, None, ALU.add))
                own()
                step("al2", e.reciprocal(sc[:, 4:5], sc[:, 3:4]))
                own()
                step("al3", e.tensor_scalar(sc[:, 5:6], sc[:, 4:5], -1.0, 1.0, ALU.mult, ALU.add))
                own()
                step("al4", e.tensor_tensor(sc[:, 6:7], sc[:, 5:6], fl[0:1, 1, 0:1], ALU.mult))
                e.wait_ge(t1, 3)
                step("al5", e.tensor_scalar(sc[:, 7:8], ps_col[0:1, 256:257], 1.0 / (B * D), None, ALU.mult))
                own()
                step("fm", e.tensor_tensor(sc[:, 7:8], sc[:, 7:8], sc[:, 4:5], ALU.mult))
                own()
                step("sg", e.tensor_tensor(sc[:, 8:9], sc[:, 7:8], sc[:, 6:7], ALU.add))
                x_stats(2)
                e.wait_ge(a1, 4)
                step("sg1", e.tensor_scalar(sc[:, 10:11], sc[:, 9:10], 1.0, None, ALU.add))
                x_stats(3)
                own()
                for n in range(NT):
                    step("_a", e.bn_aggr(mv[:, n, :], stats[:, n, :]))
                own()
                step("var", e.tensor_scalar(varr[:, :], mv[:, :, 1], EPS, None, ALU.add))
                step("sg2", e.reciprocal(sc[:, 11:12], sc[:, 10:11]))
                own()

                def floor(val, dst, k):
                    step("_i", e.tensor_copy(sci[:, k:k + 1], val))
                    own()
                    step("_i", e.tensor_copy(dst, sci[:, k:k + 1]))
                    own()
                    step("_i", e.tensor_tensor(sc[:, 15:16], dst, val, ALU.is_gt))
                    own()
                    step("_i", e.tensor_tensor(dst, dst, sc[:, 15:16], ALU.subtract))
                    own()

                step("w0", e.tensor_scalar(sc[:, 12:13], sc[:, 11:12], float(MAX_W - MIN_W), float(MIN_W), ALU.mult, ALU.add))
                own()
                floor(sc[:, 12:13], sc[:, 13:14], 0)
                step("h1", e.tensor_scalar(sc[:, 14:15], sc[:, 13:14], 0.5, None, ALU.mult))
                own()
                floor(sc[:, 14:15], sc[:, 12:13], 1)
                nv["half"] = kv[0]
                e.wait_ge(ld_w, 16 * 8)
                step("wqs", e.tensor_scalar(wqs[:, :], wq_sb[:, :], -ISQ, None, ALU.mult))
                step("bqs", e.tensor_scalar(bqs[:, :], bq_sb[:, :], -ISQ, None, ALU.mult))
                e.wait_ge(a1, 5 + B)
                step("_r", e.reciprocal(rcp[:, :], varr[:, :]))
                own()
                step("_r", e.tensor_copy(rstd[:, :], rcp[:, :]))
                step("_r", e.scalar_tensor_tensor(out=nmr[:, :], in0=mv[:, :, 0], scalar=-1.0, in1=rcp[:, :], op0=ALU.mult, op1=ALU.mult))
                e.wait_ge(t1, 4)
                step("wc", e.tensor_copy(wc[:, :], ps_b[:, 0:D]))
                e.wait_ge(t1, 5 + B)
                step("half2", e.tensor_copy(half[:, :], ps_h[:, 256:257]))
                own()
                step("mint", e.tensor_scalar(mint[:, :], adist[:, :], half[:, 0:1], BIG, ALU.is_gt, ALU.mult))

            @block.sync
            def _(e):
                with nc.allow_non_contiguous_dma(reason="four values a partition"):
                    e.dma_start(cT[:, :], c.rearrange("b d -> d b")).then_inc(ld_c, 16)
                e.dma_start(wmod_sb[:, :], wmod).then_inc(ld_c, 16)
                e.dma_start(xl[:, 0, :], x[:, S - 1, :]).then_inc(ld_f, 16)
                e.dma_start(xl[:, 1, :], x[:, S - 2, :]).then_inc(ld_f, 16)
                e.dma_start(wo_sb[:, :], W_o.rearrange("h d k -> (h d) k")).then_inc(ld_o, 16)
                for b in range(B):
                    e.dma_start(x_all[:, 1 + b * TPB:1 + (b + 1) * TPB, :],
                                xf[b * S:(b + 1) * S, :].rearrange("(n p) d -> p n d", p=P)).then_inc(ld_x[b], 16)
                    if b == 0:
                        e.dma_start(sc[0:1, 0:1], alpha).then_inc(ld_al, 16)
                for dst, src in ((wfc_sb, Wfc), (wq_sb, Wq), (wk_sb, Wk), (wv_sb, Wv)):
                    e.dma_start(dst[:, :], src).then_inc(ld_w, 16)
                for dst, src in ((bv_sb, bv), (bq_sb, bq), (bk_sb, bk)):
                    e.dma_start(dst[:, :], src.rearrange("(d a) -> d a", a=1)).then_inc(ld_w, 16)
                e.dma_start(bfc_bc[:, :], bfc.rearrange("(a d) -> a d", a=1).broadcast_to([P, D])).then_inc(ld_w, 16)
                e.wait_ge(v1, nv["zero"])
                e.dma_start(kst[:, :, 0:HALO].bitcast(F32), zero_kv[:, :].rearrange("p (g t) -> p g t", g=HG)).then_inc(s_pad, 16)
                e.dma_start(kst[:, :, HALO + T:].bitcast(F32), zero_kv[:, :].rearrange("p (g t) -> p g t", g=HG)).then_inc(s_pad, 16)
                e.dma_start(v_scr[0:HALO, :], zero_kv[0:HALO, 0:D]).then_inc(s_pad, 16)
                e.dma_start(v_scr[HALO + T:, :], zero_kv[0:HALO, 0:D]).then_inc(s_pad, 16)
                e.wait_ge(s_pad, 64)

            @block.gpsimd
            def _(e):
                e.memset(ident[:, :], 0.0).then_inc(p_cst, 1)
                e.iota(pint[:, :], [[0, 1]], 0, 1).then_inc(p_cst, 1)
                e.iota(ci[:, :], [[1, WIN]], 0, 0).then_inc(p_cst, 1)
                e.wait_ge(p_cst, 1)
                e.affine_select(out=ident[:, :], in_=ident[:, :], compare_op=ALU.not_equal, fill=1.0,
                                base=0, pattern=[[-1, P]], channel_multiplier=1).then_inc(p_cst, 1)
                e.memset(x_all[:, 0, :], 0.0)
                e.memset(pickf[:, :, :, :, :], 0.0).then_inc(p_cst, 1)
                e.wait_ge(p_cst, 5)
                for m, places in enumerate(((0, 2), (1, 3), (0, 1), (2, 3))):
                    for a in places:
                        e.tensor_copy(pickf[:, m, :, a, :], ident[:, :].rearrange("p (g r) -> p g r", g=HG)).then_inc(p_cst, 1)

            @block.scalar
            def _(e):
                e.wait_ge(ld_c, 32)
                e.activation(silu[:, :], cT[:, :], ACT.Exp, scale=-1.0).then_inc(a1, 1)
                e.wait_ge(v1, nv["varl"])
                e.activation(varl[:, :], varl[:, :], ACT.Sqrt).then_inc(a1, 1)
                e.wait_ge(ld_al, 16)
                e.activation(sc[:, 2:3], sc[:, 0:1], ACT.Exp, scale=-1.0).then_inc(a1, 1)
                e.wait_ge(v1, nv["sg"])
                e.activation(sc[:, 9:10], sc[:, 8:9], ACT.Exp, scale=-1.0).then_inc(a1, 1)
                for b in range(B):
                    e.wait_ge(t1, 5 + b)
                    e.activation(modrow[:, b, :], ps_row[b][:, :], ACT.Copy).then_inc(a1, 1)
                e.wait_ge(v1, nv["var"])
                e.activation(varr[:, :], varr[:, :], ACT.Sqrt).then_inc(a1, 1)
                e.wait_ge(t1, 6 + B)
                e.activation(cvr[:, :], ps_a[:, 0:D], ACT.Copy).then_inc(a1, 1)

            @block.tensor
            def _(e):
                e.wait_ge(v1, nv["silu3"])
                for j in range(2):
                    e.matmul(ps_col[:, j * B:(j + 1) * B], wmod_sb[:, j * D:(j + 1) * D], silu[:, :], start=True, stop=True)
                e.matmul(ps_h[0:B, 0:2 * D], silu[:, :], wmod_sb[:, 0:2 * D], start=True, stop=True).then_inc(t1, 1)
                e.wait_ge(p_cst, 4)
                e.wait_ge(v1, nv["bdo"])
                e.transpose(ps_a[:, 0:D], bdo[:, :], ident[:, :]).then_inc(t1, 1)
                e.wait_ge(v1, nv["fs"])
                e.matmul(ps_col[0:1, 256:257], flsum[:, :], ones_r[0:B, 0:1], start=True, stop=True).then_inc(t1, 1)
                e.wait_ge(ld_w, 16 * 8)
                e.matmul(ps_b[:, 0:D], bdoT[:, :], wfc_sb[:, :], start=True, stop=True).then_inc(t1, 1)
                for b in range(B):
                    e.matmul(ps_row[b][:, :], strided(silu[:, b:b + 1], 0, [[0, P]]), wmod_sb[:, 2 * D:6 * D], start=True, stop=True).then_inc(t1, 1)
                e.wait_ge(v1, nv["half"])
                e.matmul(ps_h[:, 256:257], ones_r[0:1, :], sc[0:1, 12:13], start=True, stop=True).then_inc(t1, 1)
                e.wait_ge(v1, nv["wc"])
                e.matmul(ps_a[:, 0:D], strided(bv_sb[:, 0:1], 0, [[0, P]]), wc[:, :], start=True, stop=True).then_inc(t1, 1)

        with ExitStack() as two:
            hn = [sb(f"hn{u}", [P, 4, D], F32, two) for u in range(2)]
            hT = [sb(f"hT{u}", [P, GRP], F32, two) for u in range(2)]
            khi = [sb(f"khi{u}", [P, GRP], F32R, two) for u in range(2)]
            klo = [sb(f"klo{u}", [P, GRP], F32R, two) for u in range(2)]
            qhi = [sb(f"qhi{u}", [P, GRP], F32R, two) for u in range(2)]
            qlo = [sb(f"qlo{u}", [P, GRP], F32R, two) for u in range(2)]
            vn = [sb(f"vn{u}", [P, 4, D], F32, two) for u in range(2)]
            qsk = [sb(f"qsk{u}", [P, HG, GRP], F32R, two) for u in range(2)]
            pT = pb(two, "pT", [P, GRP])
            pK = pb(two, "pK", [P, GRP])
            pQ = pb(two, "pQ", [P, GRP])
            pV = pb(two, "pV", [P, GRP])
            pSt = [pb(two, f"pSt{k}", [P, GRP]) for k in range(4)]
            v_hn = Count(sem("v_hn"), 4)
            t_tr = Count(sem("t_tr"), 1)
            a_hT = Count(sem("a_hT"), 1)
            t_kqv = Count(sem("t_kqv"), 3)
            a_kqv = Count(sem("a_kqv"), 3)
            v_lo = Count(sem("v_lo"), 2)
            t_stk = Count(sem("t_stk"), 2 * HG)
            a_stk = Count(sem("a_stk"), HG)
            v_stk = Count(sem("v_stk"), HG)
            p_mod, v_cst = sem("p_mod"), sem("v_cst")
            sgn = sb("sgn", [P, B, D], F32, two)
            d_qs = [Flights(sem(f"d_qs{u}"), HG) for u in range(2)]
            d_vs = [Flights(sem(f"d_vs{u}"), 1) for u in range(2)]
            block = two.enter_context(nc.Block())

            def stacked(e, i, u, k, copy):
                t_stk.wait(e, i, u, k + 1)
                if k < HG:
                    apart(e)
                    copy(kst[:, k, bass.ds(i * (2 * GRP) + (u * GRP + HALO), GRP)], pSt[k % 4][:, :])
                else:
                    d_qs[u].wait(e, i)
                    copy(qsk[u][:, k - HG, :], pSt[k % 4][:, :])

            @block.vector
            def _(e):
                for cnt in (v_hn, v_lo, v_stk):
                    cnt.open(e)

                def normalised(i, u):
                    t_tr.wait(e, i, u, back=2)
                    for n in range(4):
                        g = i * 8 + (4 * u + n)
                        e.tensor_scalar(hn[u][:, n, :], x_all[:, bass.ds(g + 1, 1), :].rearrange("p a d -> p (a d)"),
                                        rstd[:, bass.ds(g, 1)], nmr[:, bass.ds(g, 1)], ALU.mult, ALU.add).then_inc(v_hn.sem, 1)

                def step(i, u, left):
                    t_stk.wait(e, i, u, back=2)
                    a_kqv.wait(e, i, u, 1)
                    e.scalar_tensor_tensor(out=klo[u][:, :], in0=pK[:, :], scalar=bk_sb[:, 0:1],
                                           in1=khi[u][:, :].bitcast(F32), op0=ALU.add, op1=ALU.subtract).then_inc(v_lo.sem, 1)
                    a_kqv.wait(e, i, u, 2)
                    e.scalar_tensor_tensor(out=qlo[u][:, :], in0=pQ[:, :], scalar=bqs[:, 0:1],
                                           in1=qhi[u][:, :].bitcast(F32), op0=ALU.add, op1=ALU.subtract).then_inc(v_lo.sem, 1)
                    if left >= 2:
                        normalised(i + 1, u)
                    for k in range(1, 2 * HG, 2):
                        stacked(e, i, u, k, lambda dst, src: e.tensor_copy(dst, src).then_inc(v_stk.sem, 1))

                normalised(0, 0)
                e.tensor_copy(pick[:, :, :, :, :], pickf[:, :, :, :, :]).then_inc(v_cst, 1)
                normalised(0, 1)
                e.tensor_copy(masks[:, :, :].rearrange("p t (q w) -> p (t q) w", q=4),
                              strided(mint[:, :], 0, [[0, TPB * 4], [1, WIN]])).then_inc(v_cst, 1)
                tiles(e, NG, 2, 2, step)

            @block.scalar
            def _(e):
                for cnt in (a_hT, a_kqv, a_stk):
                    cnt.open(e)

                def modulated(i, u):
                    t_tr.wait(e, i, u)
                    t_kqv.wait(e, i, u, back=2)
                    apart(e)
                    e.activation(hT[u][:, :], pT[:, :], ACT.Identity, bias=sa_t[:, bass.ds(i, 1)],
                                 scale=ca_t[:, bass.ds(i, 1)]).then_inc(a_hT.sem, 1)

                def step(i, u, left):
                    t_stk.wait(e, i, u, back=2)
                    t_kqv.wait(e, i, u, 1)
                    e.activation(khi[u][:, :], pK[:, :], ACT.Identity, bias=bk_sb[:, 0:1]).then_inc(a_kqv.sem, 1)
                    t_kqv.wait(e, i, u, 2)
                    e.activation(qhi[u][:, :], pQ[:, :], ACT.Identity, bias=bqs[:, 0:1]).then_inc(a_kqv.sem, 1)
                    t_kqv.wait(e, i, u, 3)
                    d_vs[u].wait(e, i)
                    e.activation(vn[u][:, :, :], pV[:, :].rearrange("p (n d) -> p n d", n=4), ACT.Copy).then_inc(a_kqv.sem, 1)
                    if left >= 1:
                        modulated(*later(i, u, 1, 2))
                    for k in range(0, 2 * HG, 2):
                        stacked(e, i, u, k, lambda dst, src: e.activation(dst, src, ACT.Copy).then_inc(a_stk.sem, 1))

                modulated(0, 0)
                tiles(e, NG, 2, 2, step)

            @block.tensor
            def _(e):
                for cnt in (t_tr, t_kqv, t_stk):
                    cnt.open(e)

                def transposed(i, u):
                    a_hT.wait(e, i, u, back=1)
                    for n in range(4):
                        v_hn.wait(e, i, u, n + 1)
                        mm = e.transpose(pT[:, n * P:(n + 1) * P], hn[u][:, n, :], ident[:, :])
                    mm.then_inc(t_tr.sem, 1)

                def step(i, u, left):
                    a_hT.wait(e, i, u)
                    v_lo.wait(e, i, u, back=1)
                    a_kqv.wait(e, i, u, back=1)
                    e.matmul(pK[:, :], wk_sb[:, :], hT[u][:, :], start=True, stop=True).then_inc(t_kqv.sem, 1)
                    e.matmul(pQ[:, :], wqs[:, :], hT[u][:, :], start=True, stop=True).then_inc(t_kqv.sem, 1)
                    for n in range(4):
                        mm = e.matmul(pV[:, n * P:(n + 1) * P], hT[u][:, n * P:(n + 1) * P], wv_sb[:, :], start=True, stop=True)
                    mm.then_inc(t_kqv.sem, 1)
                    if left >= 1:
                        transposed(*later(i, u, 1, 2))
                    for k in range(2 * HG):
                        g = k % HG
                        if g == 0:
                            a_kqv.wait(e, i, u, k // HG + 1)
                            v_lo.wait(e, i, u, k // HG + 1)
                        read = v_stk if k % 2 else a_stk
                        if k < 4:
                            read.wait(e, i, u, (k + 4) // 2 + 1, back=1)
                        else:
                            read.wait(e, i, u, (k - 4) // 2 + 1)
                        hi, lo = (khi, klo) if k < HG else (qhi, qlo)
                        e.matmul(pSt[k % 4][:, :], pick[:, 2 * (k // HG), g, :, :].rearrange("p a r -> p (a r)"), hi[u][:, :], start=True, stop=False)
                        e.matmul(pSt[k % 4][:, :], pick[:, 2 * (k // HG) + 1, g, :, :].rearrange("p a r -> p (a r)"), lo[u][:, :],
                                 start=False, stop=True).then_inc(t_stk.sem, 1)

                transposed(0, 0)
                e.wait_ge(v_cst, 1)
                tiles(e, NG, 2, 2, step)

            @block.gpsimd
            def _(e):
                n = [0]

                def step(ins):
                    n[0] += 1
                    ins.then_inc(p_mod, 1)

                def own():
                    e.wait_ge(p_mod, n[0])

                def row(k):
                    return modrow[:, :, k * D:(k + 1) * D]

                for k, dst in ((0, ga_bc[:, 1:, :]), (3, gb_bc[:, :, :])):
                    step(e.tensor_scalar(sgn[:, :, :], row(k), 0.0, 0.5, ALU.is_ge, ALU.subtract))
                    own()
                    step(e.tensor_tensor(dst, row(k), sgn[:, :, :], ALU.mult))
                    own()
                    step(e.tensor_scalar(dst, dst, 0.125, 4.0, ALU.max, ALU.mult))
                    own()
                    step(e.tensor_tensor(dst, dst, sgn[:, :, :], ALU.mult))
                    own()
                step(e.tensor_copy(sb_bc[:, :, :], row(1)))
                step(e.tensor_scalar(cb_bc[:, :, :], row(2), 1.0, None, ALU.add))
                step(e.tensor_copy(ga_bc[:, 0, :], ga_bc[:, 1, :]))
                e.wait_ge(v_cst, 2)
                for q in range(HALO // QB):
                    step(e.memset(masks[:, 0, q * WIN:q * WIN + HALO - q * QB], BIG))
                    qq = 3 - q
                    step(e.memset(masks[:, TPB - 1, (qq + 1) * WIN - HALO + q * QB:(qq + 1) * WIN], BIG))
                step(e.tensor_tensor(cvr[:, :], cvr[:, :], bfc_bc[:, :], ALU.add))
                own()
                step(e.tensor_tensor(wcg[:, :, :], ga_bc[:, :, :], strided(wc[:, :], 0, [[0, B + 1], [1, D]]), ALU.mult))
                step(e.tensor_tensor(gacv_bc[:, :, :], ga_bc[:, :, :], strided(cvr[:, :], 0, [[0, B + 1], [1, D]]), ALU.mult))

            @block.sync
            def _(e):
                for f in (*d_qs, *d_vs):
                    f.open(e)
                with e.Fori(0, NG // 2) as i:
                    for u in range(2):
                        tok = i * (2 * GRP) + u * GRP
                        a_kqv.wait(e, i, u, 3)
                        apart(e)
                        e.dma_start(v_scr[bass.ds(tok + HALO, GRP), :].rearrange("(n p) d -> p n d", p=P), vn[u][:, :, :]).then_inc(d_vs[u].sem, 16)
                        for g in range(HG):
                            (v_stk if g % 2 else a_stk).wait(e, i, u, (HG + g) // 2 + 1)
                            apart(e)
                            e.dma_start(q_scr[:, :, g, bass.ds(tok, GRP)].rearrange("k r t -> (k r) t"), qsk[u][:, g, :].bitcast(F32)).then_inc(d_qs[u].sem, 16)
                for u in range(2):
                    d_vs[u].wait(e, NG // 2)
                    d_qs[u].wait(e, NG // 2)

        prep.close()

        with ExitStack() as three:
            qbd = [sb(f"qbd{u}", [P, HG, 4, 4 * QB], F32R, three) for u in range(2)]
            qst = [sb(f"qst{u}", [P, HG, P], F32, three) for u in range(2)]
            vrep = [sb(f"vrep{u}", [P, KBLK, D], F32, three) for u in range(2)]
            vbd = [sb(f"vbd{u}", [P, KBLK, D], F32, three) for u in range(2)]
            pr = sb("pr", [P, HG, 4 * WIN], F32, three)
            prT = [sb(f"prT{u}", [P, HG, 4 * WIN], F32, three) for u in range(2)]
            nmax = sb("nmax", [P, 4 * HG], F32, three)
            rs = [sb(f"rs{u}", [P, 32], F32, three) for u in range(2)]
            rsT = sb("rsT", [P, 32], F32, three)
            rden = sb("rden", [P, 32], F32, three)
            mvd = sb("mvd", [P, 4, 32], F32, three)
            rbc = sb("rbc", [P, P], F32, three)
            oT = sb("oT", [P, P], F32, three)
            xg = sb("xg", [P, D], F32, three)
            tload = sb("tload", [1, 1], F32, three)
            xa = sb("xa", [P, D], F32, three)
            pS = [pb(three, f"pS{k}", [P, 1024]) for k in range(2)]
            pO = [pb(three, f"pO{u}", [P, 512]) for u in range(2)]
            pR = pb(three, "pR", [P, 512])
            pF = pb(three, "pF", [P, 512])
            t_s = Count(sem("t_s"), 4)
            v_mx = Count(sem("v_mx"), 4)
            a_e = Count(sem("a_e"), 16)
            v_tr = Count(sem("v_tr"), 4)
            v_den = Count(sem("v_den"), 3)
            p_vb = Count(sem("p_vb"), 1)
            p_qb = Count(sem("p_qb"), 1)
            t_o = Count(sem("t_o"), 1)
            t_r = Count(sem("t_r"), 1)
            a_r = Count(sem("a_r"), 1)
            v_o = Count(sem("v_o"), 1)
            t_f = Count(sem("t_f"), 1)
            a_x = Count(sem("a_x"), 1)
            p_x = Count(sem("p_x"), 2)
            v_s2 = sem("v_s2")
            s_z = sem("s_z")
            s_zp = sem("s_zp")
            d_q = [sem(f"d_q{u}") for u in range(2)]
            d_v = [sem(f"d_v{u}") for u in range(2)]
            block = three.enter_context(nc.Block())
            NI = NT // 2

            def spread_queries(e, u):
                return e.tensor_tensor(qbd[u][:, :, :, :].rearrange("p g q (h t) -> p (g q) h t", h=4),
                                       strided(qst[u][:, :, :], 0, [[QB, 4 * HG], [0, 4], [1, QB]]),
                                       strided(eqd[:, :], 0, [[0, 4 * HG], [1, 4], [0, QB]]), ALU.mult)

            @block.sync
            def _(e):
                def step(i, u):
                    tok = i * (2 * P) + u * P
                    p_qb.wait(e, i, u, back=2)
                    e.dma_start(qst[u][:, :, :], q_scr[:, :, :, bass.ds(tok, P)].rearrange("k r g t -> (k r) g t")).then_inc(d_q[u], 16)
                    p_vb.wait(e, i, u, back=2)
                    for r in range(4):
                        src = v_scr[bass.ds(tok, KW), :].rearrange("(n k) d -> k n d", k=QB)
                        e.dma_start(vrep[u][32 * r:32 * r + 32, :, :], src).then_inc(d_v[u], 16)

                step(0, 0)
                step(0, 1)
                e.wait_ge(s_z, 3)
                with e.Fori(1, NI) as i:
                    for u in range(2):
                        step(i, u)

            @block.gpsimd
            def _(e):
                p_vb.open(e)
                p_x.open(e)
                e.sem_inc(p_qb.sem, 2 * p_qb.n + 1)
                e.memset(vbd[1][:, :, :], 0.0).then_inc(s_zp, 1)
                e.memset(prT[1][:, :, :], 0.0).then_inc(s_zp, 1)

                def queries(i, u):
                    e.wait_ge(d_q[u], i * 16 + 16)
                    t_s.wait(e, i, u, back=2)
                    p_qb.wait(e, i, u, back=1)
                    spread_queries(e, u).then_inc(p_qb.sem, 1)

                def residual(i, u):
                    g = i * 2 + u
                    sl = x_all[:, bass.ds(g, 1), :].rearrange("p a d -> p (a d)")
                    b = (g + (TPB - 1)) // TPB
                    p_x.wait(e, i, u, back=1)
                    apart(e)
                    e.tensor_tensor(xg[:, :], sl, gacv_bc[:, bass.ds(b, 1), :].rearrange("p a d -> p (a d)"), ALU.add).then_inc(p_x.sem, 1)
                    p_x.wait(e, i, u, 1)
                    a_x.wait(e, i, u)
                    apart(e)
                    e.tensor_tensor(sl, xg[:, :], xa[:, :], ALU.add).then_inc(p_x.sem, 1)

                def values(i, u):
                    e.wait_ge(d_v[u], i * 64 + 64)
                    t_o.wait(e, i, u, back=1)
                    e.tensor_tensor(vbd[u][:, :, :].rearrange("p n (g h d) -> p (n g) h d", g=HG, h=4),
                                    vrep[u][:, :, :].rearrange("p n (g h d) -> p (n g) h d", g=HG, h=4),
                                    strided(eqh[:, :], 0, [[0, KBLK * HG], [1, 4], [0, HD]]), ALU.mult).then_inc(p_vb.sem, 1)

                def step(i, u, left):
                    if left >= 2:
                        queries(i + 1, u)
                    residual(i, u)
                    if left >= 1:
                        values(*later(i, u, 1, 2))

                queries(0, 1)
                values(0, 0)
                tiles(e, NT, 2, 2, step)
                residual(NI, 0)
                p_x.wait(e, NI, 0)

            @block.scalar
            def _(e):
                e.activation(tload[:, :], ident[0:1, 0:1], ACT.Exp)
                a_e.open(e)
                a_r.open(e)
                e.sem_inc(a_x.sem, 2 * a_x.n - 1)

                def projected(i, u):
                    t_f.wait(e, i, u, back=1)
                    p_x.wait(e, i, u, back=2)
                    e.activation(xa[:, :], pF[:, 0:D], ACT.Copy).then_inc(a_x.sem, 1)

                with e.Fori(0, NI) as i:
                    for u in range(2):
                        for hg in range(HG):
                            v_mx.wait(e, i, u, hg + 1)
                            v_tr.wait(e, i, u, hg + 1, back=1)
                            if hg == 0:
                                v_den.wait(e, i, u, back=1)
                            for q in range(4):
                                k = 4 * hg + q
                                e.activation(pr[:, hg, q * WIN:(q + 1) * WIN], pS[hg % 2][:, q * (KW + QB):q * (KW + QB) + WIN], ACT.Exp,
                                             bias=nmax[:, k:k + 1], scale=-1.0, accum_out=rs[u][:, k:k + 1]).then_inc(a_e.sem, 1)
                            if hg == 0:
                                projected(i, u)
                            if hg == 2:
                                t_r.wait(e, i, u)
                                v_o.wait(e, i, u, back=1)
                                e.activation(rbc[:, :], pR[:, 0:P], ACT.Copy).then_inc(a_r.sem, 1)
                projected(NI, 0)
                t_r.wait(e, NI, 0)
                v_o.wait(e, NI, 0, back=1)
                e.activation(rbc[:, :], pR[:, 0:P], ACT.Copy).then_inc(a_r.sem, 1)
                e.activation(tload[:, :], ident[0:1, 0:1], ACT.Sqrt)
                projected(NI, 1)

            @block.tensor
            def _(e):
                t_s.open(e)
                t_o.open(e)
                t_r.open(e)
                e.sem_inc(t_f.sem, 2 * t_f.n - 1)
                e.wait_ge(s_z, 3)
                e.wait_ge(s_zp, 2)

                def scores(i, u, hg):
                    if hg >= 2:
                        a_e.wait(e, i, u, 4 * (hg - 1))
                    else:
                        a_e.wait(e, i, u, 4 * (hg + 3), back=1)
                    tok = i * (2 * P) + u * P
                    for q in range(4):
                        e.matmul(pS[hg % 2][:, q * KW:(q + 1) * KW], qbd[u][:, hg, q, :],
                                 kst[:, hg, bass.ds(tok, KW)], start=q % 2 == 0, stop=False, skip_group_check=True)
                        if q % 2:
                            m = (i * 2 + u) % TPB
                            mm = e.matmul(strided(pS[hg % 2][:, 0:1], (q - 1) * (KW + QB), [[KW + QB, 2], [1, WIN]]), identb[:, :],
                                          masks[:, bass.ds(m, 1), (q - 1) * WIN:(q + 1) * WIN].rearrange("p a w -> p (a w)"),
                                          start=False, stop=True, skip_group_check=True)
                    mm.then_inc(t_s.sem, 1)

                def weighted(i, u, blocks):
                    w = 1 - u
                    if 0 in blocks:
                        v_tr.wait(e, i, u, back=1)
                        p_vb.wait(e, i, u, back=1)
                        v_o.wait(e, i, u, back=2)
                    for j in blocks:
                        lo, hi = max(0, j - 4), min(3, j)
                        for hg in range(HG):
                            mm = e.matmul(pO[w][32 * hg:32 * hg + 32, lo * QB:(hi + 1) * QB], vbd[w][:, j, 32 * hg:32 * hg + 32],
                                          strided(prT[w][:, hg, 0:1], j * QB + lo * (WIN - QB), [[WIN - QB, hi - lo + 1], [1, QB]]),
                                          start=j == 0, stop=j == KBLK - 1, skip_group_check=True)
                    if KBLK - 1 in blocks:
                        mm.then_inc(t_o.sem, 1)

                def spread(i, u):
                    v_den.wait(e, i, u)
                    a_r.wait(e, i, u, back=1)
                    e.matmul(pR[:, 0:P], st_den[:, :], mvd[:, :, :].rearrange("p q t -> p (q t)"), start=True, stop=True).then_inc(t_r.sem, 1)

                def project(i, u):
                    v_o.wait(e, i, u, back=1)
                    a_x.wait(e, i, u, back=2)
                    b = (i * 2 + u + (TPB - 2)) // TPB
                    e.matmul(pF[:, 0:D], oT[:, :], wcg[:, bass.ds(b, 1), :].rearrange("p a d -> p (a d)"), start=True, stop=True).then_inc(t_f.sem, 1)

                with e.Fori(0, NI) as i:
                    for u in range(2):
                        p_qb.wait(e, i, u)
                        scores(i, u, 0)
                        project(i, u)
                        scores(i, u, 1)
                        weighted(i, u, range(0, 3))
                        scores(i, u, 2)
                        weighted(i, u, range(3, 6))
                        scores(i, u, 3)
                        spread(i, u)
                        weighted(i, u, range(6, KBLK))
                project(NI, 0)
                spread(NI, 0)
                weighted(NI, 0, range(KBLK))
                project(NI, 1)

            @block.vector
            def _(e):
                for cnt in (v_mx, v_den, v_o):
                    cnt.open(e)
                e.sem_inc(v_tr.sem, 2 * v_tr.n - 1)
                for w in range(2):
                    e.memset(rs[w][:, :], 1.0)
                e.memset(pr[:, HG - 1, :], 0.0).then_inc(s_z, 1)
                e.memset(oT[:, :], 0.0).then_inc(s_z, 1)
                e.wait_ge(s_z, 2)
                e.wait_ge(s_zp, 2)
                e.wait_ge(d_q[0], 16)
                spread_queries(e, 0).then_inc(s_z, 1)

                def maxima(i, u, hg):
                    t_s.wait(e, i, u, hg + 1)
                    a_e.wait(e, i, u, 4 * hg + 4, back=1)
                    e.tensor_reduce(nmax[:, 4 * hg:4 * hg + 4], strided(pS[hg % 2][:, 0:1], 0, [[KW + QB, 4], [1, WIN]]),
                                    AX.X, ALU.min).then_inc(v_mx.sem, 1)

                def turn(i, u, hg):
                    a_e.wait(e, i, u, 4 * hg + 4)
                    if hg == 0:
                        t_o.wait(e, i, u, back=1)
                    e.transpose(prT[u][:, hg, :], pr[:, hg, :]).then_inc(v_tr.sem, 1)

                def turn_last(i, u):
                    a_e.wait(e, i, u, back=1)
                    e.transpose(prT[1 - u][:, HG - 1, :], pr[:, HG - 1, :]).then_inc(v_tr.sem, 1)

                def denominators(i, u):
                    w = 1 - u
                    a_e.wait(e, i, u, back=1)
                    v_den.wait(e, i, u, back=1)
                    e.transpose(rsT[:, :], rs[w][:, :]).then_inc(v_den.sem, 1)

                def inverted(i, u):
                    v_den.wait(e, i, u, 1)
                    e.reciprocal(rden[:, :], rsT[:, :]).then_inc(v_den.sem, 1)

                def laid_out(i, u):
                    v_den.wait(e, i, u, 2)
                    t_r.wait(e, i, u, back=1)
                    e.tensor_tensor(mvd[:, :, :], strided(rden[:, :], 0, [[0, 4], [1, 32]]),
                                    strided(eqq[:, :], 0, [[1, 4], [0, 32]]), ALU.mult).then_inc(v_den.sem, 1)

                def statistics(i, u):
                    p_x.wait(e, i, u, back=1)
                    apart(e)
                    done = bass.ds((i * 2 + (u + NT)) % (NT + 1), 1)
                    e.bn_stats(stat2[:, done, :].rearrange("p a s -> p (a s)"), x_all[:, done, :].rearrange("p a d -> p (a d)")).then_inc(v_s2, 1)

                def normalise(i, u):
                    a_r.wait(e, i, u)
                    t_o.wait(e, i, u)
                    t_f.wait(e, i, u, back=1)
                    e.tensor_tensor(oT[:, :], pO[1 - u][:, 0:P], rbc[:, :], ALU.mult).then_inc(v_o.sem, 1)

                with e.Fori(0, NI) as i:
                    for u in range(2):
                        maxima(i, u, 0)
                        turn_last(i, u)
                        denominators(i, u)
                        inverted(i, u)
                        maxima(i, u, 1)
                        turn(i, u, 0)
                        maxima(i, u, 2)
                        laid_out(i, u)
                        turn(i, u, 1)
                        statistics(i, u)
                        maxima(i, u, 3)
                        turn(i, u, 2)
                        normalise(i, u)
                turn_last(NI, 0)
                denominators(NI, 0)
                inverted(NI, 0)
                laid_out(NI, 0)
                statistics(NI, 0)
                normalise(NI, 0)
                e.wait_ge(v_s2, NT + 1)
                for g in range(NT - 1):
                    e.bn_aggr(mv2[:, g, :], stat2[:, g + 1, :]).then_inc(v_s2, 1)
                statistics(NI, 1)
                e.wait_ge(v_s2, 2 * NT + 1)
                e.bn_aggr(mv2[:, NT - 1, :], stat2[:, NT, :]).then_inc(v_s2, 1)

        attn.close()

        gates = sb("gates", [P, 2, NT])
        gidx = sb("gidx", [P, SC], I32)
        sidx = sb("sidx", [P, SC], I32)
        eid = sb("eid", [1, NF], I32)
        h_scr = nc.dram_tensor("h_scr", (T, D), F32, kind="Internal").ap()
        w1_all = sb("w1_all", [P, NE, FF + D + FC])
        w2_all = sb("w2_all", [P, NE * FC * D])
        d_wt = sem("d_wt")
        N_WT = 4 + NE + 1
        y_scr = nc.dram_tensor("y_scr", (2 * T + NF * FT, D), F32, kind="Internal").ap()

        route = ExitStack()
        score = sb("score", [P, NT, NE], F32, route)
        rev = sb("rev", [P, NE], F32, route)
        upper = sb("upper", [P, P], BF16, route)
        onesb = sb("onesb", [P, P], BF16, route)
        io_lo = sb("io_lo", [P, P, 2 * NT], BF16, route)
        io_row = sb("io_row", [P, P], BF16, route)
        io_c = sb("io_c", [P, 2 * NT], BF16, route)
        io_p = sb("io_p", [P, 1], F32, route)
        io_s = sb("io_s", [P, SC], F32, route)
        io_j = sb("io_j", [1, NF], F32, route)
        p5 = sem("p5")
        with ExitStack() as four:
            s4 = lambda n, sh, dt=F32: sb(n, sh, dt, four)
            rw1_sb = s4("rw1_sb", [P, FF])
            rb1_sb = s4("rb1_sb", [P, FC])
            rw2_sb = s4("rw2_sb", [P, FC, NE])
            rb2_bc = s4("rb2_bc", [P, NE])
            var2 = s4("var2", [P, NT])
            rstd2 = s4("rstd2", [P, NT])
            nmr2 = s4("nmr2", [P, NT])
            rw2p = s4("rw2p", [P, FC, QB])
            sel = s4("sel", [P, NE])
            hn2 = [s4(f"hn2{u}", [P, 4, D]) for u in range(2)]
            hm2 = [s4(f"hm2{u}", [P, 4, D]) for u in range(2)]
            h2 = [s4(f"h2{u}", [P, 4, D]) for u in range(2)]
            h2T = [s4(f"h2T{u}", [P, GRP]) for u in range(2)]
            act = [s4(f"act{u}", [P, FC, GRP]) for u in range(2)]
            scp = [s4(f"scp{u}", [P, GRP]) for u in range(2)]
            pT2 = [pb(four, f"pT2{u}", [P, GRP]) for u in range(2)]
            pA2 = [pb(four, f"pA2{k}", [P, GRP]) for k in range(FC)]
            pSp = pb(four, "pSp", [P, GRP])
            pSc = pb(four, "pSc", [P, GRP])
            d_rw = sem("d_rw")
            v_st = sem("v_st")
            a_rt, v_io = sem("a_rt"), sem("v_io")
            v_h2 = Count(sem("v_h2"), 4)
            p_h2 = Count(sem("p_h2"), 2)
            t_t2 = Count(sem("t_t2"), 1)
            a_t2 = Count(sem("a_t2"), 1)
            t_a2 = Count(sem("t_a2"), FC)
            a_a2 = Count(sem("a_a2"), FC)
            t_sp = Count(sem("t_sp"), 1)
            v_sp = Count(sem("v_sp"), 1)
            t_sc = Count(sem("t_sc"), 1)
            v_sc = Count(sem("v_sc"), 1)
            d_h = [Flights(sem(f"d_h{u}"), 1) for u in range(2)]
            block = four.enter_context(nc.Block())

            @block.sync
            def _(e):
                for f in d_h:
                    f.open(e)
                e.dma_start(rw1_sb[:, :], rw1).then_inc(d_rw, 16)
                e.dma_start(rw2_sb[:, :, :], rw2.rearrange("(c p) n -> p c n", p=P)).then_inc(d_rw, 16)
                with nc.allow_non_contiguous_dma(reason="four values a partition"):
                    e.dma_start(rb1_sb[:, :], rb1.rearrange("(c p) -> p c", p=P)).then_inc(d_rw, 16)
                e.dma_start(rb2_bc[:, :], rb2.rearrange("(a n) -> a n", a=1).broadcast_to([P, NE])).then_inc(d_rw, 16)
                big = []
                for k in range(2):
                    half_e = slice(k * NE // 2, (k + 1) * NE // 2)
                    big.append((w1_all[:, half_e, 0:FF], W1[half_e, :, :].rearrange("e d f -> d e f")))
                    big.append((w2_all[:, k * NE * FF // 2:(k + 1) * NE * FF // 2].rearrange("p (c d) -> p c d", d=D),
                                W2[half_e, :, :].rearrange("e (c p) d -> p (e c) d", p=P)))
                for j in range(NG):
                    p_h2.wait(e, j // 2, j % 2)
                    e.dma_start(h_scr[j * GRP:(j + 1) * GRP, :].rearrange("(n p) d -> p n d", p=P), h2[j % 2][:, :, :]).then_inc(d_h[j % 2].sem, 16)
                    if 1 <= j <= len(big):
                        e.dma_start(*big[j - 1]).then_inc(d_wt, 16)
                with nc.allow_non_contiguous_dma(reason="4 values a partition and expert, once"):
                    for x_ in range(NE):
                        e.dma_start(w1_all[:, x_, FF + D:], b1[x_:x_ + 1, :].rearrange("e (c p) -> p (e c)", p=P)).then_inc(d_wt, 16)
                e.dma_start(w1_all[:, :, FF:FF + D], b2.rearrange("(a e) d -> a e d", a=1).broadcast_to([P, NE, D])).then_inc(d_wt, 16)
                for u in range(2):
                    d_h[u].wait(e, NG // 2)

            @block.vector
            def _(e):
                for cnt in (v_h2, v_sp, v_sc):
                    cnt.open(e)
                e.tensor_scalar(var2[:, :], mv2[:, :, 1], EPS, None, ALU.add).then_inc(v_st, 1)
                e.wait_ge(a_rt, 1)
                e.reciprocal(rstd2[:, :], var2[:, :]).then_inc(v_st, 1)
                e.wait_ge(v_st, 2)
                e.scalar_tensor_tensor(out=nmr2[:, :], in0=mv2[:, :, 0], scalar=-1.0, in1=rstd2[:, :], op0=ALU.mult, op1=ALU.mult).then_inc(v_st, 1)
                e.wait_ge(v_st, 3)

                def normalised(i, u):
                    p_h2.wait(e, i, u, 1, back=2)
                    for n in range(4):
                        g = i * 8 + (4 * u + n)
                        e.tensor_scalar(hn2[u][:, n, :], x_all[:, bass.ds(g + 1, 1), :].rearrange("p a d -> p (a d)"),
                                        rstd2[:, bass.ds(g, 1)], nmr2[:, bass.ds(g, 1)], ALU.mult, ALU.add).then_inc(v_h2.sem, 1)

                def step(i, u, left):
                    if left >= 2:
                        normalised(i + 1, u)
                    share = bass.ds((i * 2 + u) * (P // NG), P // NG)
                    e.tensor_copy(io_lo[:, share, :], io_row[:, share].rearrange("p (s a) -> p s a", a=1).broadcast_to([P, P // NG, 2 * NT])).then_inc(v_io, 1)
                    t_sp.wait(e, i, u)
                    t_sc.wait(e, i, u, back=2)
                    e.tensor_copy(scp[u][:, :], pSp[:, :]).then_inc(v_sp.sem, 1)
                    if not is_first(i, u):
                        biased(*later(i, u, -1, 2))

                def biased(i, u):
                    t_sc.wait(e, i, u)
                    e.tensor_tensor(score[:, bass.ds(i * 8 + 4 * u, 4), :], pSc[:, 0:4 * NE].rearrange("p (n k) -> p n k", n=4),
                                    strided(rb2_bc[:, :], 0, [[0, 4], [1, NE]]), ALU.add).then_inc(v_sc.sem, 1)

                normalised(0, 0)
                e.memset(rw2p[:, :, :], 0.0).then_inc(v_st, 1)
                e.wait_ge(d_rw, 64)
                e.wait_ge(v_st, 4)
                e.tensor_copy(rw2p[:, :, 0:NE], rw2_sb[:, :, :]).then_inc(v_st, 1)
                e.tensor_reduce(sel[:, :], strided(ident[:, :], 0, [[1, NE], [QB, 4]]), AX.X, ALU.add).then_inc(v_st, 1)
                normalised(0, 1)
                e.wait_ge(p5, 8)
                tiles(e, NG, 2, 2, step, head=1)
                biased(NG // 2 - 1, 1)

            @block.gpsimd
            def _(e):
                p_h2.open(e)
                small = dict(allow_small_or_imprecise_dtypes=True)
                e.iota(rev[:, :], [[-1, NE]], NE, 0, **small).then_inc(p5, 1)
                e.memset(onesb[:, :], 1.0).then_inc(p5, 1)
                e.wait_ge(p5, 2)
                e.affine_select(out=upper[:, :], in_=onesb[:, :], compare_op=ALU.is_gt, fill=0.0, base=0,
                                pattern=[[1, P]], channel_multiplier=-1).then_inc(p5, 1)
                e.iota(io_j[:, :], [[1, NF]], 0, 0, **small).then_inc(p5, 1)
                e.iota(io_c[:, :], [[1, 2 * NT]], 1, 0, **small).then_inc(p5, 1)
                e.iota(io_p[:, :], [[0, 1]], 0, 1, **small).then_inc(p5, 1)
                e.iota(io_s[:, :], [[P, SC]], 0, 1, **small).then_inc(p5, 1)
                e.iota(io_row[:, :], [[1, P]], 0, 0, **small).then_inc(p5, 1)
                with e.Fori(0, NG // 2) as i:
                    for u in range(2):
                        v_h2.wait(e, i, u)
                        t_t2.wait(e, i, u, back=2)
                        d_h[u].wait(e, i)
                        apart(e)
                        e.tensor_tensor(hm2[u][:, :, :], hn2[u][:, :, :], bcast_row(cb_bc, i, 4), ALU.mult).then_inc(p_h2.sem, 1)
                        p_h2.wait(e, i, u, 1)
                        apart(e)
                        e.tensor_tensor(h2[u][:, :, :], hm2[u][:, :, :], bcast_row(sb_bc, i, 4), ALU.add).then_inc(p_h2.sem, 1)

            @block.scalar
            def _(e):
                a_t2.open(e)
                a_a2.open(e)
                e.wait_ge(v_st, 1)
                e.activation(var2[:, :], var2[:, :], ACT.Sqrt).then_inc(a_rt, 1)
                e.wait_ge(d_rw, 64)
                with e.Fori(0, NG // 2) as i:
                    for u in range(2):
                        t_t2.wait(e, i, u)
                        t_a2.wait(e, i, u, back=2)
                        e.activation(h2T[u][:, :], pT2[u][:, :], ACT.Copy).then_inc(a_t2.sem, 1)
                        for k in range(FC):
                            t_a2.wait(e, i, u, k + 1)
                            t_sp.wait(e, i, u, back=2)
                            e.activation(act[u][:, k, :], pA2[k][:, :], ACT.Relu, bias=rb1_sb[:, k:k + 1]).then_inc(a_a2.sem, 1)

            @block.tensor
            def _(e):
                for cnt in (t_t2, t_a2, t_sp, t_sc):
                    cnt.open(e)

                def transposed(i, u):
                    p_h2.wait(e, i, u)
                    a_t2.wait(e, i, u, back=2)
                    for n in range(4):
                        mm = e.transpose(pT2[u][:, n * P:(n + 1) * P], h2[u][:, n, :], ident[:, :])
                    mm.then_inc(t_t2.sem, 1)

                def summed(i, u):
                    v_sc.wait(e, i, u, back=1)
                    v_sp.wait(e, i, u)
                    for n in range(4):
                        mm = e.matmul(pSc[:, n * NE:(n + 1) * NE], scp[u][:, n * P:(n + 1) * P], sel[:, :], start=True, stop=True)
                    mm.then_inc(t_sc.sem, 1)

                def step(i, u, left):
                    a_t2.wait(e, i, u)
                    for k in range(FC):
                        a_a2.wait(e, i, u, k + 1, back=1)
                        e.matmul(pA2[k][:, :], rw1_sb[:, k * P:(k + 1) * P], h2T[u][:, :], start=True, stop=True).then_inc(t_a2.sem, 1)
                    if left >= 1:
                        transposed(*later(i, u, 1, 2))
                    v_sp.wait(e, i, u, back=1)
                    for k in range(FC):
                        a_a2.wait(e, i, u, k + 1)
                        mm = e.matmul(pSp[QB * k:QB * k + QB, :], rw2p[:, k, :], act[u][:, k, :], start=True, stop=True, skip_group_check=True)
                    mm.then_inc(t_sp.sem, 1)
                    if not is_first(i, u):
                        summed(*later(i, u, -1, 2))

                transposed(0, 0)
                e.wait_ge(d_rw, 64)
                e.wait_ge(v_st, 6)
                tiles(e, NG, 2, 2, step, head=1)
                summed(NG // 2 - 1, 1)

        with ExitStack() as five:
            s5 = lambda n, sh, dt=F32: sb(n, sh, dt, five)
            m12 = s5("m12", [P, 2, NT])
            eqm = s5("eqm", [P, NT, NE])
            rank = s5("rank", [P, NT])
            oh = [s5(f"oh{k}", [P, NT, NE]) for k in range(2)]
            sc2 = s5("sc2", [P, NT, NE])
            ohb = s5("ohb", [P, NT * NE], BF16)
            tot = s5("tot", [P, NT + 16, NE])
            cum = [s5(f"cum{k}", [P, NT + 16, NE]) for k in range(2)]
            off = s5("off", [P, NT, NE])
            cnt_i = s5("cnt_i", [P, NE], I32)
            til = s5("til", [P, NE])
            tcu = [s5(f"tcu{k}", [P, 8 + NE]) for k in range(2)]
            base = s5("base", [P, NE])
            posg = s5("posg", [P, NT, NE])
            posm = s5("posm", [P, NT, NE])
            pos = s5("pos", [P, 2, NT])
            pos_i = s5("pos_i", [P, 2 * NT], I32)
            lo_i = s5("lo_i", [P, 2 * NT], I32)
            hi_i = s5("hi_i", [P, 2 * NT], I32)
            lo_b = s5("lo_b", [P, 2 * NT], BF16)
            hi_b = s5("hi_b", [P, 2 * NT], BF16)
            one_lo = s5("one_lo", [P, P, 2 * NT], BF16)
            one_hi = s5("one_hi", [P, SC, 2 * NT], BF16)
            mapv = s5("mapv", [P, 2, SC, 2 * NT], BF16)
            ge = s5("ge", [1, NF, NE])
            eidf = s5("eidf", [1, NF])
            cc = s5("cc", [P, SC])
            pp = s5("pp", [P, SC])
            fa = s5("fa", [P, SC])
            fb = s5("fb", [P, SC])
            fc = s5("fc", [P, SC])
            fd = s5("fd", [P, SC])
            pPre = pb(five, "pPre", [P, 512])
            pTot = pb(five, "pTot", [P, 512])
            pMap = pb(five, "pMap", [P, 512])
            v5, a5, t5 = sem("v5"), sem("a5"), sem("t5")
            n5 = {}
            k5 = [0]
            z5 = sem("z5")
            UP = 16
            block = five.enter_context(nc.Block())

            @block.gpsimd
            def _(e):
                for t in (tot, cum[0], cum[1]):
                    e.memset(t[:, 0:16, :], 0.0).then_inc(z5, 1)
                for t in tcu:
                    e.memset(t[:, 0:8], 0.0).then_inc(z5, 1)

            @block.vector
            def _(e):
                def step(ins, name=None):
                    k5[0] += 1
                    if name:
                        n5[name] = k5[0]
                    ins.then_inc(v5, 1)

                def own():
                    e.wait_ge(v5, k5[0])

                def per_tile(t):
                    return strided(t, 0, [[1, NT], [0, NE]])

                def per_expert(t, n=NT):
                    return strided(t, 0, [[0, n], [1, NE]])

                e.wait_ge(p5, 8)
                cur = score
                for k in range(2):
                    step(e.tensor_reduce(m12[:, k, :], cur[:, :, :], AX.X, ALU.max), f"m{k}")
                    own()
                    step(e.tensor_tensor(eqm[:, :, :], cur[:, :, :], per_tile(m12[:, k, :]), ALU.is_equal))
                    own()
                    step(e.tensor_tensor(eqm[:, :, :], eqm[:, :, :], per_expert(rev[:, :]), ALU.mult))
                    own()
                    step(e.tensor_reduce(rank[:, :], eqm[:, :, :], AX.X, ALU.max))
                    own()
                    step(e.tensor_tensor(oh[k][:, :, :], per_expert(rev[:, :]), per_tile(rank[:, :]), ALU.is_equal))
                    own()
                    if k == 0:
                        step(e.scalar_tensor_tensor(out=sc2[:, :, :], in0=oh[0][:, :, :], scalar=-3e38, in1=score[:, :, :],
                                                    op0=ALU.mult, op1=ALU.add))
                        own()
                        cur = sc2
                step(e.tensor_tensor(ohb[:, :].rearrange("p (t k) -> p t k", k=NE), oh[0][:, :, :], oh[1][:, :, :], ALU.add), "ohb")
                step(e.tensor_tensor(gates[:, 1, :], m12[:, 1, :], m12[:, 0, :], ALU.subtract), "gd")
                e.wait_ge(z5, 5)
                e.wait_ge(t5, 1)
                step(e.tensor_copy(tot[:, 16:, :], pTot[:, 0:NT * NE].rearrange("p (t k) -> p t k", k=NE)))
                own()
                src = tot
                for r, s in enumerate((1, 2, 4, 8, 16)):
                    dst = cum[r % 2]
                    step(e.tensor_tensor(dst[:, 16:, :], src[:, 16:, :], src[:, 16 - s:16 + NT - s, :], ALU.add))
                    own()
                    src = dst
                step(e.tensor_scalar(til[:, :], src[:, 16 + NT - 1, :], float(FT - 1), None, ALU.add))
                own()
                step(e.tensor_copy(cnt_i[:, :], til[:, :]))
                own()
                step(e.tensor_scalar(cnt_i[:, :], cnt_i[:, :], FT.bit_length() - 1, None, ALU.logical_shift_right))
                own()
                step(e.tensor_copy(tcu[0][:, 8:], cnt_i[:, :]))
                step(e.tensor_copy(til[:, :], cnt_i[:, :]))
                step(e.tensor_tensor(off[:, :, :], src[:, 16:, :], tot[:, 16:, :], ALU.subtract))
                own()
                for r, s in enumerate((1, 2, 4)):
                    step(e.tensor_tensor(tcu[(r + 1) % 2][:, 8:], tcu[r % 2][:, 8:], tcu[r % 2][:, 8 - s:8 + NE - s], ALU.add))
                    own()
                step(e.tensor_tensor(base[:, :], tcu[1][:, 8:], til[:, :], ALU.subtract))
                own()
                step(e.tensor_scalar(base[:, :], base[:, :], float(FT), None, ALU.mult))
                own()
                step(e.tensor_tensor(off[:, :, :], off[:, :, :], per_expert(base[:, :]), ALU.add))
                own()
                step(e.tensor_tensor(posg[:, :, :], pPre[:, 0:NT * NE].rearrange("p (t k) -> p t k", k=NE), off[:, :, :], ALU.add))
                own()
                for k in range(2):
                    step(e.tensor_tensor(posm[:, :, :], posg[:, :, :], oh[k][:, :, :], ALU.mult))
                    own()
                    step(e.tensor_reduce(pos[:, k, :], posm[:, :, :], AX.X, ALU.add))
                    own()
                step(e.tensor_copy(pos_i[:, :], pos[:, :, :].rearrange("p k t -> p (k t)")))
                own()
                step(e.tensor_scalar(lo_i[:, :], pos_i[:, :], P - 1, None, ALU.bitwise_and))
                step(e.tensor_scalar(hi_i[:, :], pos_i[:, :], P.bit_length() - 1, None, ALU.logical_shift_right))
                own()
                step(e.tensor_copy(lo_b[:, :], lo_i[:, :]))
                step(e.tensor_copy(hi_b[:, :], hi_i[:, :]))
                own()
                for k in range(2 * NT // UP):
                    uses = slice(k * UP, (k + 1) * UP)
                    step(e.tensor_tensor(one_hi[:, :, uses], io_lo[:, 0:SC, uses], strided(hi_b[:, :], k * UP, [[0, SC], [1, UP]]), ALU.is_equal))
                    own()
                    step(e.tensor_scalar(mapv[:, 1, :, uses], one_hi[:, :, uses], io_p[:, 0:1], None, ALU.mult))
                    step(e.tensor_tensor(mapv[:, 0, :, uses], one_hi[:, :, uses], strided(io_c[:, :], k * UP, [[0, SC], [1, UP]]), ALU.mult))
                    step(e.tensor_tensor(one_lo[:, :, uses], io_lo[:, :, uses], strided(lo_b[:, :], k * UP, [[0, P], [1, UP]]), ALU.is_equal), f"map{k}")
                e.wait_ge(a5, 1)
                step(e.tensor_scalar(m12[:, 0, :], m12[:, 1, :], 1.0, None, ALU.add))
                own()
                step(e.reciprocal(gates[:, 0, :], m12[:, 0, :]))
                own()
                step(e.tensor_tensor(gates[:, 1, :], m12[:, 1, :], gates[:, 0, :], ALU.mult))
                step(e.tensor_tensor(ge[:, :, :], strided(io_j[:, :], 0, [[1, NF], [0, NE]]),
                                     strided(tcu[1][0:1, 8:9], 0, [[0, NF], [1, NE]]), ALU.is_ge))
                own()
                step(e.tensor_reduce(eidf[:, :], ge[:, :, :], AX.X, ALU.add))
                own()
                step(e.tensor_scalar(eid[:, :], eidf[:, :], float(NE - 1), None, ALU.min))
                step(e.tensor_scalar(fd[:, :], io_s[:, :], float(2 * T + P), None, ALU.add))
                e.wait_ge(t5, 2)
                step(e.tensor_copy(cc[:, :], pMap[:, 0:SC]))
                step(e.tensor_copy(pp[:, :], pMap[:, SC:2 * SC]))
                own()
                step(e.tensor_scalar(fa[:, :], cc[:, :], float(NT + 1), -float(NT), ALU.is_ge, ALU.mult))
                own()
                step(e.tensor_tensor(fb[:, :], fa[:, :], cc[:, :], ALU.add))
                own()
                step(e.tensor_scalar(fb[:, :], fb[:, :], float(P), -float(P), ALU.mult, ALU.add))
                own()
                step(e.tensor_tensor(fb[:, :], fb[:, :], pp[:, :], ALU.add))
                own()
                step(e.tensor_scalar(gidx[:, 0:SC], fb[:, :], 0.0, None, ALU.max))
                step(e.tensor_scalar(fc[:, :], cc[:, :], float(P), -float(P), ALU.mult, ALU.add))
                own()
                step(e.tensor_tensor(fc[:, :], fc[:, :], pp[:, :], ALU.add))
                step(e.tensor_scalar(fa[:, :], cc[:, :], 0.0, None, ALU.is_equal))
                own()
                step(e.tensor_tensor(fd[:, :], fd[:, :], fa[:, :], ALU.mult))
                own()
                step(e.tensor_tensor(sidx[:, 0:SC], fd[:, :], fc[:, :], ALU.add))
                own()

            @block.scalar
            def _(e):
                e.wait_ge(v5, n5["gd"])
                e.activation(m12[:, 1, :], gates[:, 1, :], ACT.Exp).then_inc(a5, 1)

            @block.tensor
            def _(e):
                e.wait_ge(p5, 3)
                e.wait_ge(v5, n5["ohb"])
                e.matmul(pPre[:, 0:NT * NE], upper[:, :], ohb[:, :], start=True, stop=True)
                e.matmul(pTot[:, 0:NT * NE], onesb[:, :], ohb[:, :], start=True, stop=True).then_inc(t5, 1)
                for k in range(2 * NT):
                    if k % UP == 0:
                        e.wait_ge(v5, n5[f"map{k // UP}"])
                    mm = e.matmul(pMap[:, 0:2 * SC], one_lo[:, :, k], mapv[:, :, :, k].rearrange("p a s -> p (a s)"),
                                  start=k == 0, stop=k == 2 * NT - 1)
                mm.then_inc(t5, 1)

        route.close()

        with ExitStack() as six:
            s6 = lambda n, sh, dt=F32: sb(n, sh, dt, six)
            R = 6
            AHEAD = R + 2
            gi = [s6(f"gi{u}", [P, FR], I32) for u in range(R)]
            si = [s6(f"si{u}", [P, FR], I32) for u in range(R)]
            w1t = [s6(f"w1t{u}", [P, FF + D + FC]) for u in range(R)]
            hg = [s6(f"hg{u}", [P, FR, P]) for u in range(R)]
            hgT = [s6(f"hgT{u}", [P, FT]) for u in range(R)]
            ac = [s6(f"ac{u}", [P, FC, FT]) for u in range(R)]
            ys = [s6(f"ys{u}", [P, FR, D]) for u in range(R)]
            pTg = [pb(six, f"pTg{w}", [P, 512]) for w in range(2)]
            pU = [[pb(six, f"pU{w}{k}", [P, 512]) for k in range(2)] for w in range(2)]
            pY = [pb(six, f"pY{w}", [P, 512]) for w in range(2)]
            d_g = [sem(f"d_g{u}") for u in range(R)]
            d_y = [sem(f"d_y{u}") for u in range(R)]
            v_gi = Count(sem("v_gi"), 1, R)
            v_si = Count(sem("v_si"), 1, R)
            v_w = Count(sem("v_w"), 1, R)
            t_tg = Count(sem("t_tg"), 1, R)
            v_tg = Count(sem("v_tg"), 1, R)
            t_up = Count(sem("t_up"), 2, R)
            a_up = Count(sem("a_up"), FC, R)
            t_dn = Count(sem("t_dn"), 1, R)
            v_y = Count(sem("v_y"), 1, R)
            block = six.enter_context(nc.Block())

            def expert(e, i, u):
                return e.value_load(eid[0:1, bass.ds(i * R + u, 1)], min_val=0, max_val=NE - 1)

            def at(i, u, n):
                return later(i, u, n, R)

            @block.gpsimd
            def _(e):
                def gather(i, u):
                    v_gi.wait(e, i, u)
                    t_tg.wait(e, i, u, back=R)
                    apart(e)
                    for k in range(FR):
                        e.indirect_dma_start(out=hg[u][:, k, :], out_offset=None, in_=h_scr,
                                             in_offset=bass.IndirectOffsetOnAxis(ap=gi[u][:, k:k + 1].bitcast(U32), axis=0)).then_inc(d_g[u], 16)

                def scatter(i, u):
                    v_si.wait(e, i, u)
                    v_y.wait(e, i, u)
                    apart(e)
                    for k in range(FR):
                        e.indirect_dma_start(out=y_scr, out_offset=bass.IndirectOffsetOnAxis(ap=si[u][:, k:k + 1].bitcast(U32), axis=0),
                                             in_=ys[u][:, k, :], in_offset=None).then_inc(d_y[u], 16)

                for j in range(R):
                    gather(0, j)
                for j in range(R, AHEAD):
                    gather(*at(0, j, 0))

                def step(i, u, left):
                    scatter(i, u)
                    if left >= AHEAD:
                        gather(*at(i, u, AHEAD))

                tiles(e, NF, R, AHEAD, step)
                for u in range(R):
                    n = (NF - u + R - 1) // R
                    e.wait_ge(d_g[u], 16 * FR * n)
                    e.wait_ge(d_y[u], 16 * FR * n)

            @block.scalar
            def _(e):
                a_up.open(e)
                e.wait_ge(d_wt, 16 * N_WT)

                def relu(i, u, left):
                    v_w.wait(e, i, u)
                    t_dn.wait(e, i, u, back=R)
                    for k in range(FC):
                        if k % 2 == 0:
                            t_up.wait(e, i, u, k // 2 + 1)
                        e.activation(ac[u][:, k, :], pU[u % 2][k // 2][:, (k % 2) * FT:(k % 2 + 1) * FT], ACT.Relu,
                                     bias=w1t[u][:, FF + D + k:FF + D + k + 1]).then_inc(a_up.sem, 1)

                tiles(e, NF, R, 0, relu)

            @block.vector
            def _(e):
                for cnt in (v_gi, v_si, v_w, v_tg, v_y):
                    cnt.open(e)

                def gather_index(i, u):
                    t_tg.wait(e, i, u, back=R)
                    apart(e)
                    e.tensor_copy(gi[u][:, :], gidx[:, bass.ds(i * (FR * R) + FR * u, FR)]).then_inc(v_gi.sem, 1)

                def first_matrix(i, u):
                    x_ = expert(e, i, u)
                    v_y.wait(e, i, u, back=R)
                    apart(e)
                    e.tensor_copy(w1t[u][:, :], w1_all[:, bass.ds(x_, 1), :].rearrange("p a f -> p (a f)")).then_inc(v_w.sem, 1)

                def scatter_index(i, u):
                    if not (isinstance(i, int) and i == 0):
                        e.wait_ge(d_y[u], i * (16 * FR))
                        apart(e)
                    e.tensor_copy(si[u][:, :], sidx[:, bass.ds(i * (FR * R) + FR * u, FR)]).then_inc(v_si.sem, 1)

                def gathered(i, u):
                    t_tg.wait(e, i, u)
                    t_up.wait(e, i, u, back=R)
                    e.tensor_copy(hgT[u][:, :], pTg[u % 2][:, 0:FT]).then_inc(v_tg.sem, 1)

                def result(i, u):
                    t_dn.wait(e, i, u)
                    e.tensor_tensor(ys[u][:, :, :], pY[u % 2][:, 0:FR * D].rearrange("p (k d) -> p k d", k=FR),
                                    strided(w1t[u][:, :], FF, [[0, FR], [1, D]]), ALU.add).then_inc(v_y.sem, 1)

                for j in range(R):
                    gather_index(0, j)
                e.wait_ge(d_wt, 16 * N_WT)
                for j in range(2):
                    first_matrix(0, j)
                    gathered(0, j)
                    gather_index(*at(0, j, R))

                def step(i, u, left):
                    if left >= 2:
                        first_matrix(*at(i, u, 2))
                    scatter_index(i, u)
                    if left >= 2:
                        gathered(*at(i, u, 2))
                    if left >= AHEAD:
                        gather_index(*at(i, u, AHEAD))
                    result(i, u)

                tiles(e, NF, R, AHEAD, step, head=1)

            @block.tensor
            def _(e):
                for cnt in (t_tg, t_up, t_dn):
                    cnt.open(e)
                e.wait_ge(d_wt, 16 * N_WT)

                def rows(i, u):
                    e.wait_ge(d_g[u], i * (16 * FR) + 16 * FR)
                    v_tg.wait(e, i, u, back=2)
                    for k in range(FR):
                        mm = e.transpose(pTg[u % 2][:, k * P:(k + 1) * P], hg[u][:, k, :], ident[:, :])
                    mm.then_inc(t_tg.sem, 1)

                def up(i, u):
                    v_w.wait(e, i, u)
                    v_tg.wait(e, i, u)
                    a_up.wait(e, i, u, back=2)
                    for k in range(FC):
                        mm = e.matmul(pU[u % 2][k // 2][:, (k % 2) * FT:(k % 2 + 1) * FT], w1t[u][:, k * P:(k + 1) * P], hgT[u][:, :],
                                      start=True, stop=True)
                        if k % 2:
                            mm.then_inc(t_up.sem, 1)

                def down(i, u, x_):
                    v_y.wait(e, i, u, back=2)
                    a_up.wait(e, i, u)
                    for r in range(FR):
                        for k in range(FC):
                            mm = e.matmul(pY[u % 2][:, r * D:(r + 1) * D], ac[u][:, k, r * P:(r + 1) * P], w2_all[:, bass.ds(x_ * FF + k * D, D)],
                                          start=k == 0, stop=k == FC - 1)
                    mm.then_inc(t_dn.sem, 1)

                rows(0, 0)
                rows(0, 1)
                up(0, 0)

                def step(i, u, left):
                    x_ = expert(e, i, u)
                    if left >= 2:
                        rows(*at(i, u, 2))
                    if left >= 1:
                        up(*at(i, u, 1))
                    down(i, u, x_)

                tiles(e, NF, R, 2, step)

        with ExitStack() as seven:
            s7 = lambda n, sh, dt=F32: sb(n, sh, dt, seven)
            NCH = 2 * B
            TC = NT // NCH
            y1 = s7("y1", [P, NT, D])
            y2 = s7("y2", [P, NT, D])
            fin = s7("fin", [P, NT, D])
            d_ld = [sem(f"d_ld{h}") for h in range(NCH)]
            a7, v7, p7, d_out = sem("a7"), sem("v7"), sem("p7"), sem("d_out")
            block = seven.enter_context(nc.Block())

            POOLS = (1, 4)
            n7 = [(h + 1) * TC + sum(c_ not in POOLS for c_ in range(h)) for h in range(NCH)]
            m7 = [h + 1 + sum(c_ in POOLS for c_ in range(h + 1)) for h in range(NCH)]

            def times_gb(e, h):
                return e.tensor_tensor(y2[:, part(h), :], y2[:, part(h), :], strided(gb_bc[:, h // 2, :], 0, [[0, TC], [1, D]]), ALU.mult)

            def part(h):
                return slice(h * TC, (h + 1) * TC)

            @block.sync
            def _(e):
                for h in range(NCH):
                    for k, t in enumerate((y1, y2)):
                        e.dma_start(t[:, part(h), :], y_scr[k * T + h * TC * P:k * T + (h + 1) * TC * P, :].rearrange("(n p) d -> p n d", p=P)).then_inc(d_ld[h], 16)
                for h in range(NCH):
                    e.wait_ge(p7, m7[h])
                    e.dma_start(of[h * TC * P:(h + 1) * TC * P, :].rearrange("(n p) d -> p n d", p=P), fin[:, part(h), :]).then_inc(d_out, 16)
                e.wait_ge(d_out, 16 * NCH)

            @block.scalar
            def _(e):
                for g in range(NT):
                    if g % TC == 0:
                        e.wait_ge(d_ld[g // TC], 32)
                    e.activation(y1[:, g, :], y1[:, g, :], ACT.Copy, scale=gates[:, 0, g:g + 1]).then_inc(a7, 1)

            @block.vector
            def _(e):
                for h in range(NCH):
                    e.wait_ge(d_ld[h], 32)
                    for g in range(h * TC, (h + 1) * TC):
                        e.wait_ge(a7, g + 1)
                        e.scalar_tensor_tensor(out=y2[:, g, :], in0=y2[:, g, :], scalar=gates[:, 1, g:g + 1], in1=y1[:, g, :],
                                               op0=ALU.mult, op1=ALU.add).then_inc(v7, 1)
                    if h not in POOLS:
                        e.wait_ge(v7, n7[h])
                        times_gb(e, h).then_inc(v7, 1)

            @block.gpsimd
            def _(e):
                for h in range(NCH):
                    if h in POOLS:
                        e.wait_ge(v7, n7[h])
                        times_gb(e, h).then_inc(p7, 1)
                        e.wait_ge(p7, m7[h] - 1)
                    else:
                        e.wait_ge(v7, n7[h] + 1)
                    e.tensor_tensor(fin[:, part(h), :], y2[:, part(h), :], x_all[:, 1 + h * TC:1 + (h + 1) * TC, :], ALU.add).then_inc(p7, 1)


_INS = ['L0_attn_x', 'L0_attn_alpha', 'L0_attn_Wq', 'L0_attn_bq', 'L0_attn_Wk', 'L0_attn_bk', 'L0_attn_Wv', 'L0_attn_bv',
        'L0_attn_W_o', 'L0_attn_Wfc', 'L0_attn_bfc', 'L0_ffn_rw1', 'L0_ffn_rb1', 'L0_ffn_rw2', 'L0_ffn_rb2', 'L0_ffn_W1',
        'L0_ffn_b1', 'L0_ffn_W2', 'L0_ffn_b2', 'L0_c', 'L0_wmod']


def kernel(**inputs):
    import numpy as _np
    import concourse.bacc as _bacc
    from concourse import mybir as _mybir
    from concourse.bass_utils import run_bass_kernel_spmd as _run

    nc = _bacc.Bacc("TRN2", target_bir_lowering=False, num_devices=1)
    arrays, args = {}, []
    for name in _INS:
        a = _np.ascontiguousarray(inputs[name])
        if a.ndim == 0:
            a = a.reshape(1, 1)
        arrays[f"in_{name}"] = a
        args.append(nc.dram_tensor(f"in_{name}", a.shape, _mybir.dt.from_np(a.dtype), kind="ExternalInput").ap())
    args.append(nc.dram_tensor("out_0", (B, S, D), F32, kind="ExternalOutput").ap())
    build(nc, *args)
    r = _run(nc, [arrays], core_ids=[0])
    return r.results[0]["out_0"]
```
